# Optimizing a Trainium2 kernel written in Bass

```python
import numpy as np
import jax
import jax.numpy as jnp

def _softmax(x, axis=-1):
    return jax.nn.softmax(x, axis=axis)

def _gelu(x):
    return jax.nn.gelu(x, approximate=True)

def _silu(x):
    return jax.nn.silu(x)

def _sigmoid(x):
    return jax.nn.sigmoid(x)

def _layernorm(x, axis=-1, eps=1e-05):
    m = jnp.mean(x, axis=axis, keepdims=True)
    v = jnp.var(x, axis=axis, keepdims=True)
    return (x - m) / jnp.sqrt(v + eps)

def _scatter_add(tgt, idx, src, axis=0):
    return tgt.at[idx].add(src)

def _segment_sum(src, seg, n):
    return jax.ops.segment_sum(src, seg, n)
kernel_name = 'mk_decoder_postln_d1_seqx_r8_c0f6b1'

def setup_inputs(seed: int=0):
    np.random.seed(seed)
    _w = jnp.asarray

    def _rec_inputs():
        import jax
        import jax.numpy as jnp
        _rk = jax.random.key(seed)
        x = 7.22e-05 + 1 * jax.random.normal(jax.random.fold_in(_rk, 1), (8, 128, 512), jnp.float32)
        _lenS = 128 - jax.random.randint(jax.random.fold_in(_rk, 7), (8,), 0, max(1, 128 // 4) + 1, jnp.int32)
        _lenS2 = 128 - jax.random.randint(jax.random.fold_in(_rk, 8), (8,), 0, max(1, 128 // 4) + 1, jnp.int32)
        _ctx_4096P = jax.random.normal(jax.random.fold_in(_rk, 11), (8, 16, 512), jnp.float32)
        _ctx_4096c = jax.random.dirichlet(jax.random.fold_in(_rk, 511), 0.3 * jnp.ones((16,), jnp.float32), (8, 128))
        _ctx_4096t = jnp.einsum('bsk,bkd->bsd', _ctx_4096c, _ctx_4096P)
        _ctx_4096t = _ctx_4096t * jax.lax.rsqrt(jnp.mean(jnp.square(_ctx_4096t)) + 1e-12) * 0.953939
        ctx_4096 = 4.13588e-05 + 0.999923 * (_ctx_4096t + 0.3 * jax.random.normal(jax.random.fold_in(_rk, 611), (8, 128, 512), jnp.float32))
        return (x, ctx_4096)
    x, ctx_4096 = _rec_inputs()

    def _L0_attn_setup():
        import jax, jax.numpy as jnp
        import numpy as np
        N_HEADS = 32
        N_KV_HEADS = 8
        DIM = 512
        HEAD_DIM = DIM // N_HEADS
        N_REP = N_HEADS // N_KV_HEADS
        ROPE_THETA = 10000.0

        def _apply_rope(x):
            seq = x.shape[2]
            hd = x.shape[-1]
            inv_freq = 1.0 / ROPE_THETA ** (jnp.arange(0, hd, 2, dtype=jnp.float32) / hd)
            angles = jnp.arange(seq, dtype=jnp.float32)[:, None] * inv_freq[None, :]
            cos = jnp.cos(angles)[None, None]
            sin = jnp.sin(angles)[None, None]
            x1 = x[..., 0::2]
            x2 = x[..., 1::2]
            r1 = x1 * cos - x2 * sin
            r2 = x1 * sin + x2 * cos
            return jnp.stack([r1, r2], axis=-1).reshape(x.shape)
        key = jax.random.key(seed)
        k1, k2, k3 = jax.random.split(key, 3)
        bs, seq = (1, 256)
        x = jax.random.normal(k1, (bs, seq, DIM), dtype=jnp.float32)
        w_qkv = jax.random.normal(k2, (DIM, HEAD_DIM * (N_HEADS + 2 * N_KV_HEADS)), dtype=jnp.float32) * 0.02
        w_o = jax.random.normal(k3, (N_HEADS * HEAD_DIM, DIM), dtype=jnp.float32) * 0.02
        return {'x': x, 'w_qkv': w_qkv, 'w_o': w_o}
    _L0_attn_all = _L0_attn_setup()
    _L0_attn_in = {k: v for k, v in _L0_attn_all.items() if k in ('w_qkv', 'w_o')}
    del _L0_attn_all

    def _L0_xattn_setup():
        import jax, jax.numpy as jnp
        import numpy as np
        B, S, D = (1, 256, 512)
        H, HKV, DK, DV = (32, 8, 128, 128)
        key = jax.random.key(seed)
        ks = jax.random.split(key, 7)
        std = 0.02
        return {'q': jax.random.normal(ks[0], (B, S, D), jnp.float32), 'k': jax.random.normal(ks[1], (B, S, D), jnp.float32), 'v': jax.random.normal(ks[2], (B, S, D), jnp.float32), 'Wq': jax.random.normal(ks[3], (H * DK, D), jnp.float32) * std, 'Wk': jax.random.normal(ks[4], (HKV * DK, D), jnp.float32) * std, 'Wv': jax.random.normal(ks[5], (HKV * DV, D), jnp.float32) * std, 'Wd': jax.random.normal(ks[6], (D, H * DV), jnp.float32) * std}
    _L0_xattn_all = _L0_xattn_setup()
    _L0_xattn_in = {k: v for k, v in _L0_xattn_all.items() if k in ('Wq', 'Wk', 'Wv', 'Wd')}
    del _L0_xattn_all

    def _L0_ffn_setup():
        import jax, jax.numpy as jnp
        import numpy as np
        HID, INTER = (512, 1792)
        B, S = (2, 256)

        def _binary_diff_weight(w, base):
            d = w - base
            coeff = jnp.mean(jnp.abs(d))
            return base + coeff * jnp.sign(d)
        key = jax.random.key(seed)
        ks = jax.random.split(key, 7)
        return {'hidden_states': jax.random.normal(ks[0], (B, S, HID), dtype=jnp.float32), 'w1': jax.random.normal(ks[1], (INTER, HID), dtype=jnp.float32) * 0.02, 'mean_w1': jax.random.normal(ks[2], (INTER, HID), dtype=jnp.float32) * 0.02, 'w2': jax.random.normal(ks[3], (HID, INTER), dtype=jnp.float32) * 0.02, 'mean_w2': jax.random.normal(ks[4], (HID, INTER), dtype=jnp.float32) * 0.02, 'w3': jax.random.normal(ks[5], (INTER, HID), dtype=jnp.float32) * 0.02, 'mean_w3': jax.random.normal(ks[6], (INTER, HID), dtype=jnp.float32) * 0.02}
    _L0_ffn_all = _L0_ffn_setup()
    _L0_ffn_in = {k: v for k, v in _L0_ffn_all.items() if k in ('w1', 'mean_w1', 'w2', 'mean_w2', 'w3', 'mean_w3')}
    del _L0_ffn_all
    return {'x': x, 'ctx_4096': ctx_4096, 'L0_attn_w_qkv': _L0_attn_in['w_qkv'], 'L0_attn_w_o': _L0_attn_in['w_o'], 'L0_xattn_Wq': _L0_xattn_in['Wq'], 'L0_xattn_Wk': _L0_xattn_in['Wk'], 'L0_xattn_Wv': _L0_xattn_in['Wv'], 'L0_xattn_Wd': _L0_xattn_in['Wd'], 'L0_ffn_w1': _L0_ffn_in['w1'], 'L0_ffn_mean_w1': _L0_ffn_in['mean_w1'], 'L0_ffn_w2': _L0_ffn_in['w2'], 'L0_ffn_mean_w2': _L0_ffn_in['mean_w2'], 'L0_ffn_w3': _L0_ffn_in['w3'], 'L0_ffn_mean_w3': _L0_ffn_in['mean_w3']}

def reference(x, ctx_4096, L0_attn_w_qkv, L0_attn_w_o, L0_xattn_Wq, L0_xattn_Wk, L0_xattn_Wv, L0_xattn_Wd, L0_ffn_w1, L0_ffn_mean_w1, L0_ffn_w2, L0_ffn_mean_w2, L0_ffn_w3, L0_ffn_mean_w3):
    import jax
    import jax.numpy as jnp

    def _L0_attn_ref(x, w_qkv, w_o):
        import jax, jax.numpy as jnp
        import numpy as np
        N_HEADS = 32
        N_KV_HEADS = 8
        DIM = 512
        HEAD_DIM = DIM // N_HEADS
        N_REP = N_HEADS // N_KV_HEADS
        ROPE_THETA = 10000.0

        def _apply_rope(x):
            seq = x.shape[2]
            hd = x.shape[-1]
            inv_freq = 1.0 / ROPE_THETA ** (jnp.arange(0, hd, 2, dtype=jnp.float32) / hd)
            angles = jnp.arange(seq, dtype=jnp.float32)[:, None] * inv_freq[None, :]
            cos = jnp.cos(angles)[None, None]
            sin = jnp.sin(angles)[None, None]
            x1 = x[..., 0::2]
            x2 = x[..., 1::2]
            r1 = x1 * cos - x2 * sin
            r2 = x1 * sin + x2 * cos
            return jnp.stack([r1, r2], axis=-1).reshape(x.shape)
        bs, seq, _ = x.shape
        qkv = x @ w_qkv
        q_sz = N_HEADS * HEAD_DIM
        kv_sz = N_KV_HEADS * HEAD_DIM
        xq = qkv[..., :q_sz].reshape(bs, seq, N_HEADS, HEAD_DIM).transpose(0, 2, 1, 3)
        xk = qkv[..., q_sz:q_sz + kv_sz].reshape(bs, seq, N_KV_HEADS, HEAD_DIM).transpose(0, 2, 1, 3)
        xv = qkv[..., q_sz + kv_sz:].reshape(bs, seq, N_KV_HEADS, HEAD_DIM).transpose(0, 2, 1, 3)
        xq = _apply_rope(xq)
        xk = _apply_rope(xk)
        keys = jnp.repeat(xk, N_REP, axis=1)
        values = jnp.repeat(xv, N_REP, axis=1)
        scale = 1.0 / jnp.sqrt(jnp.float32(HEAD_DIM))
        scores = jnp.einsum('bhsd,bhtd->bhst', xq, keys) * scale
        causal = jnp.tril(jnp.ones((seq, seq), dtype=bool))[None, None]
        scores = jnp.where(causal, scores, -jnp.inf)
        probs = jax.nn.softmax(scores, axis=-1)
        out = jnp.einsum('bhst,bhtd->bhsd', probs, values)
        out = out.transpose(0, 2, 1, 3).reshape(bs, seq, N_HEADS * HEAD_DIM)
        return out @ w_o

    def _L0_xattn_ref(q, k, v, Wq, Wk, Wv, Wd):
        import jax, jax.numpy as jnp
        import numpy as np
        B, S, D = (1, 256, 512)
        H, HKV, DK, DV = (32, 8, 128, 128)
        b, s, _ = q.shape
        exp = H // HKV
        Q = (q @ Wq.T).reshape(b, s, HKV, exp, DK)
        K = (k @ Wk.T).reshape(b, s, HKV, DK)
        V = (v @ Wv.T).reshape(b, s, HKV, DV)
        scale = DK ** (-0.5)
        scores = jnp.einsum('bqhed,bkhd->bheqk', Q, K) * scale
        causal = jnp.tril(jnp.ones((s, s), dtype=bool))
        scores = jnp.where(causal, scores, jnp.finfo(scores.dtype).min)
        probs = jax.nn.softmax(scores, axis=-1)
        attn = jnp.einsum('bheqk,bkhd->bqhed', probs, V)
        attn = attn.reshape(b, s, H * DV)
        return attn @ Wd.T

    def _L0_ffn_ref(hidden_states, w1, mean_w1, w2, mean_w2, w3, mean_w3):
        import jax, jax.numpy as jnp
        import numpy as np
        HID, INTER = (512, 1792)
        B, S = (2, 256)

        def _binary_diff_weight(w, base):
            d = w - base
            coeff = jnp.mean(jnp.abs(d))
            return base + coeff * jnp.sign(d)
        W1 = _binary_diff_weight(w1, mean_w1)
        W2 = _binary_diff_weight(w2, mean_w2)
        W3 = _binary_diff_weight(w3, mean_w3)
        gate = jnp.einsum('bsh,ih->bsi', hidden_states, W1)
        up = jnp.einsum('bsh,ih->bsi', hidden_states, W3)
        h = jax.nn.silu(gate) * up
        return jnp.einsum('bsi,hi->bsh', h, W2)
    x = _layernorm(x + _L0_attn_ref(x, L0_attn_w_qkv, L0_attn_w_o), axis=-1)
    x = _layernorm(x + _L0_xattn_ref(x, ctx_4096, ctx_4096, L0_xattn_Wq, L0_xattn_Wk, L0_xattn_Wv, L0_xattn_Wd), axis=-1)
    x = _layernorm(x + _L0_ffn_ref(x, L0_ffn_w1, L0_ffn_mean_w1, L0_ffn_w2, L0_ffn_mean_w2, L0_ffn_w3, L0_ffn_mean_w3), axis=-1)
    return x

_drawn_inputs = setup_inputs


def setup_inputs(seed=0):
    import zlib

    import numpy as np

    out = dict(_drawn_inputs(seed))
    spreads = {}
    factors = {}
    for name, (base, spread) in spreads.items():
        noise = np.random.default_rng([zlib.crc32(name.encode()), seed]).standard_normal(out[name].shape)
        drawn = base * np.exp(spread * noise) if base else spread * noise
        out[name] = jnp.asarray(drawn.astype(out[name].dtype))
    for name, factor in factors.items():
        out[name] = (out[name] * factor).astype(out[name].dtype)
    return out
```

```python
from contextlib import ExitStack

import numpy as np

import concourse.bass as bass
from concourse import mybir

F32 = mybir.dt.float32
F32R = mybir.dt.float32r
ALU = mybir.AluOpType
ACT = mybir.ActivationFunctionType
AXX = mybir.AxisListType.X

P = 128
NB = 8
DM = 512
KT = DM // P
NG = 8
NE = 4
HD = 16
QKV = 768
INTER = 1792
PIECE = 256
NP = INTER // PIECE
NCO = 28
COW = NP * 1024 // NCO
SELF_SCALE = 0.25
CROSS_SCALE = float(P) ** -0.5
NEG = -3.0e38
EPS = 1e-5

C_ID, C_MASK, C_BM, C_COS, C_SIN, C_HALF, C_EPS, C_POW, C_ONE = 0, 128, 256, 264, 280, 296, 298, 299, 300
C_ALL = 428


def counted(value):
    return not (isinstance(value, int) and value <= 0)


def bcast(ap, n, inner):
    if inner:
        a = ap.rearrange("p (a b) -> p a b", b=1)
        return a.to_broadcast([a.shape[0], a.shape[1], n])
    a = ap.rearrange("p (b a) -> p b a", b=1)
    return a.to_broadcast([a.shape[0], n, a.shape[2]])


def decoder_layer(nc, consts_d, x_d, xT_d, ctxT_d, wkv_d, wqkv_d, wo_d, wq_d, wd_d, fw_d, fm_d, out_d):
    with ExitStack() as ctx:
        def sb(name, shape, dt=F32, stack=ctx):
            return stack.enter_context(nc.sbuf_tensor(name, shape, dt))

        consts = sb("consts", [P, C_ALL])
        ident = consts[:, C_ID:C_ID + P]
        cmask = consts[:, C_MASK:C_MASK + P]
        bmask = consts[:, C_BM:C_BM + 8]
        rcos = consts[:, C_COS:C_COS + HD]
        rsin = consts[:, C_SIN:C_SIN + HD]
        half = consts[:, C_HALF:C_HALF + 2]
        ceps = consts[:, C_EPS:C_EPS + 1]
        cpow = consts[:, C_POW:C_POW + 1]
        ones = consts[:, C_ONE:C_ONE + P]
        xs = sb("xs", [P, NB, DM])
        csum = sb("csum", [P, NCO, 3])
        csum3 = sb("csum3", [P, 4])
        coeff = sb("coeff", [P, 3])
        stats = sb("stats", [P, NB, 6])
        moments = sb("moments", [P, NB, 2])
        varep = sb("varep", [P, NB])
        rstd = sb("rstd", [P, NB])
        rmax = sb("rmax", [P, 4, NE])
        nbias = sb("nbias", [P, 4, NE])
        rsum = sb("rsum", [P, 4, NE])
        rinv = sb("rinv", [P, 4, NE])
        gate_mark = sb("gate_mark", [P, 1])
        prob = sb("prob", [P, 4, NE, P])

        with ExitStack() as r_kv:
            kT = sb("kT", [P, NG, NB * P], F32, r_kv)
            vv = sb("vv", [P, NB, NG * P], F32, r_kv)
            with ExitStack() as r1:
                wk_h = sb("wk_h", [P, KT, 1024], F32R, r1)
                wk_l = sb("wk_l", [P, KT, 1024], F32R, r1)
            with ExitStack() as r1:
                wqkv_h = sb("wqkv_h", [P, KT, QKV], F32R, r1)
                wqkv_l = sb("wqkv_l", [P, KT, QKV], F32R, r1)
                wqkv_r = sb("wqkv_r", [P, 2, QKV], F32, r1)
            with ExitStack() as r1:
                wq_h = sb("wq_h", [P, NE, KT, P], F32R, r1)
                wq_l = sb("wq_l", [P, NE, KT, P], F32R, r1)
                wq_r = sb("wq_r", [P, 2, KT * P], F32, r1)
                wd_r = sb("wd_r", [P, NE, DM], F32, r1)
                vg_h = sb("vg_h", [P, NB, P], F32R, r1)
                vg_l = sb("vg_l", [P, NB, P], F32R, r1)
            sb("region1", [P, 9216], F32, r_kv)
            with ExitStack() as r2:
                wv_h = sb("wv_h", [P, KT, 1024], F32R, r2)
                wv_l = sb("wv_l", [P, KT, 1024], F32R, r2)
                wkv_r = sb("wkv_r", [P, 2, 1024], F32, r2)
                cT_r = sb("cT_r", [P, KT, DM], F32, r2)
                cT_h = sb("cT_h", [P, KT, DM], F32R, r2)
                cT_l = sb("cT_l", [P, KT, DM], F32R, r2)
                cw = sb("cw", [P, 2, 3, COW], F32, r2)
                cm = sb("cm", [P, 2, 3, COW], F32, r2)
            with ExitStack() as r2:
                wo_s = sb("wo_s", [P, 2 * NE, DM], F32R, r2)
                bd = sb("bd", [P, NE, 8, P], F32, r2)
                qT = sb("qT", [P, NE, P], F32, r2)
                pT = sb("pT", [P, NE, DM], F32, r2)
                xT_r = sb("xT_r", [P, KT, P], F32, r2)
                xT_h = sb("xT_h", [P, KT, P], F32R, r2)
                xT_l = sb("xT_l", [P, KT, P], F32R, r2)
                rope1 = sb("rope1", [P, 640], F32, r2)
                rope2 = sb("rope2", [P, 640], F32, r2)
                q_tok = sb("q_tok", [P, DM], F32, r2)
                k_rep = sb("k_rep", [P, DM], F32, r2)
                v_tok = sb("v_tok", [P, P], F32, r2)
                v_two = sb("v_two", [P, NG, 2, HD], F32, r2)
                oT_h = sb("oT_h", [P, NE, P], F32R, r2)
                oT_l = sb("oT_l", [P, NE, P], F32R, r2)
                wo_r = sb("wo_r", [P, 2, DM], F32, r2)
                wo_h = sb("wo_h", [P, DM], F32R, r2)
                wo_t = sb("wo_t", [P, DM], F32, r2)
                res = sb("res", [P, DM], F32, r2)
            with ExitStack() as r2:
                xnT_h = sb("xnT_h", [P, KT, NB * P], F32R, r2)
                xnT_l = sb("xnT_l", [P, KT, NB * P], F32R, r2)
                qc = sb("qc", [P, NE, NB * P], F32, r2)
                wd_h = sb("wd_h", [P, NE, DM], F32R, r2)
                wd_l = sb("wd_l", [P, NE, DM], F32R, r2)
                pT_h = sb("pT_h", [P, DM], F32R, r2)
                pT_l = sb("pT_l", [P, DM], F32R, r2)
                aT_h = sb("aT_h", [P, 2, DM], F32R, r2)
                aT_l = sb("aT_l", [P, 2, DM], F32R, r2)
        with ExitStack() as r_ffn:
            x2T_h = sb("x2T_h", [P, KT, NB * P], F32R, r_ffn)
            x2T_l = sb("x2T_l", [P, KT, NB * P], F32R, r_ffn)
            fw = sb("fw", [P, 3, 1024], F32, r_ffn)
            fm = sb("fm", [P, 3, 1024], F32, r_ffn)
            fd = sb("fd", [P, 2, 1024], F32, r_ffn)
            wf = sb("wf", [P, 3, 1024], F32, r_ffn)
            w13_h = sb("w13_h", [P, 2, KT, PIECE], F32R, r_ffn)
            w13_l = sb("w13_l", [P, 2, KT, PIECE], F32R, r_ffn)
            w2_h = sb("w2_h", [P, 2, DM], F32R, r_ffn)
            w2_l = sb("w2_l", [P, 2, DM], F32R, r_ffn)
            silu = sb("silu", [P, 2, DM], F32, r_ffn)
            hf = sb("hf", [P, 2, DM], F32, r_ffn)
            hT_h = sb("hT_h", [P, 2, 2, DM], F32R, r_ffn)
            hT_l = sb("hT_l", [P, 2, 2, DM], F32R, r_ffn)
        bank = [ctx.enter_context(nc.psum_tensor(f"bank{i}", [P, 512], F32)) for i in range(8)]

        def sem(name):
            return ctx.enter_context(nc.semaphore(name))

        consts_in = sem("consts_in")
        wkv_in = [sem(f"wkv_in{i}") for i in range(2)]
        ctx_in = sem("ctx_in")
        wkv_h_ready, wkv_l_ready = sem("wkv_h_ready"), sem("wkv_l_ready")
        ctx_h_ready, ctx_l_ready = sem("ctx_h_ready"), sem("ctx_l_ready")
        kv_ready, k_copied, v_copied = sem("kv_ready"), sem("k_copied"), sem("v_copied")
        wqkv_in = [sem(f"wqkv_in{i}") for i in range(2)]
        wqkv_h_ready, wqkv_l_ready = sem("wqkv_h_ready"), sem("wqkv_l_ready")
        wo_in = [sem(f"wo_in{i}") for i in range(2)]
        wo_h_ready, wo_t_ready, wo_ready = sem("wo_h_ready"), sem("wo_t_ready"), sem("wo_ready")
        x_in, res_in = sem("x_in"), sem("res_in")
        co_in, co_sub, co_sum = [sem("co_in0"), sem("co_in1")], sem("co_sub"), sem("co_sum")
        cototal_ready, coeff_ready = sem("cototal_ready"), sem("coeff_ready")
        x_h_ready, x_l_ready, qkv_ready = sem("x_h_ready"), sem("x_l_ready"), sem("qkv_ready")
        rope_ready, qk_ready, blkT_ready = sem("rope_ready"), sem("qk_ready"), sem("blkT_ready")
        qT_ready, bd_ready, v_two_ready = sem("qT_ready"), sem("bd_ready"), sem("v_two_ready")
        scores_ready, masked, nbias_ready = sem("scores_ready"), sem("masked"), sem("nbias_ready")
        exp_done, rinv_ready, norm_done = sem("exp_done"), sem("rinv_ready"), sem("norm_done")
        pT_ready, pT_copied = sem("pT_ready"), sem("pT_copied")
        pv_ready, oT_h_ready, oT_l_ready = sem("pv_ready"), sem("oT_h_ready"), sem("oT_l_ready")
        oT_used, oproj_ready, y_done = sem("oT_used"), sem("oproj_ready"), sem("y_done")
        stats_done, moments_done, varep_done = sem("stats_done"), sem("moments_done"), sem("varep_done")
        rstd_ready, ln_done = sem("rstd_ready"), sem("ln_done")

        xnT_turned, xnT_h_ready, xnT_l_ready = sem("xnT_turned"), sem("xnT_h_ready"), sem("xnT_l_ready")
        wq_in, wd_in = [sem(f"wq_in{i}") for i in range(2)], [sem(f"wd_in{i}") for i in range(NE)]
        wq_h_ready, wq_l_ready = sem("wq_h_ready"), sem("wq_l_ready")
        wd_h_ready, wd_l_ready, wd_used = sem("wd_h_ready"), sem("wd_l_ready"), sem("wd_used")
        vg_h_ready, vg_ready = sem("vg_h_ready"), sem("vg_ready")
        q_ready, q_copied = sem("q_ready"), sem("q_copied")
        pT_h_ready, pT_l_ready = sem("pT_h_ready"), sem("pT_l_ready")
        cross_pv, aT_h_ready, aT_l_ready = sem("cross_pv"), sem("aT_h_ready"), sem("aT_l_ready")
        cross_y, cross_added = sem("cross_y"), sem("cross_added")
        x2T_turned, x2T_h_ready, x2T_l_ready = sem("x2T_turned"), sem("x2T_h_ready"), sem("x2T_l_ready")
        f_in, fd_ready, sign_ready, wf_ready = sem("f_in"), sem("fd_ready"), sem("sign_ready"), sem("wf_ready")
        w13_h_ready, w13_l_ready = sem("w13_h_ready"), sem("w13_l_ready")
        w2_h_ready, w2_l_ready = sem("w2_h_ready"), sem("w2_l_ready")
        gu_ready, silu_done, hf_done = sem("gu_ready"), sem("silu_done"), sem("hf_done")
        hT_h_ready, hT_l_ready = sem("hT_h_ready"), sem("hT_l_ready")
        ffn_ready, ffn_added, out_done = sem("ffn_ready"), sem("ffn_added"), sem("out_done")

        def slot_of(b, g):
            return b * 8 + g

        LN0 = 1
        A_UNITS = NB * NG

        block = ctx.enter_context(nc.Block())

        @block.sync
        def _(sp):
            def co_load(n):
                if n >= 2:
                    sp.wait_ge(co_sum, n - 1)
                cols = bass.ts(n % 4, COW)
                sp.dma_start(cw[:, n % 2], fw_d[n // 4][:, :, cols]).then_inc(co_in[n % 2], 16)
                sp.dma_start(cm[:, n % 2], fm_d[n // 4][:, :, cols]).then_inc(co_in[n % 2], 16)

            sp.dma_start(consts[:, :], consts_d).then_inc(consts_in, 16)
            for c in range(8):
                if c >= 2:
                    sp.wait_ge(wkv_l_ready, c - 1)
                sp.dma_start(wkv_r[:, c % 2, :], wkv_d[c]).then_inc(wkv_in[c % 2], 16)
                if c == 0:
                    sp.dma_start(cT_r[:, :, :], ctxT_d[0]).then_inc(ctx_in, 16)
            sp.wait_ge(ctx_l_ready, 4)
            sp.dma_start(cT_r[:, :, :], ctxT_d[1]).then_inc(ctx_in, 16)
            for n in range(21):
                co_load(n)
            sp.wait_ge(kv_ready, 24)
            for k in range(KT):
                if k >= 2:
                    sp.wait_ge(wqkv_l_ready, k - 1)
                sp.dma_start(wqkv_r[:, k % 2, :], wqkv_d[:, k, :]).then_inc(wqkv_in[k % 2], 16)
            for n in range(21, NCO):
                co_load(n)
            sp.wait_ge(kv_ready, 32)
            sp.wait_ge(co_sum, NCO)
            sp.dma_start(xT_r[:, :, :], xT_d[0]).then_inc(x_in, 16)
            sp.dma_start(res[:, :], x_d[0]).then_inc(res_in, 16)

            def wo_load(c):
                if c >= 2:
                    sp.wait_ge(wo_ready, c - 1)
                sp.dma_start(wo_r[:, c % 2, :], wo_d[:, c, :]).then_inc(wo_in[c % 2], 16)

            def x_load(b):
                sp.wait_ge(x_l_ready, b)
                sp.dma_start(xT_r[:, :, :], xT_d[b]).then_inc(x_in, 16)

            def res_load(b):
                sp.wait_ge(y_done, b)
                sp.dma_start(res[:, :], x_d[b]).then_inc(res_in, 16)

            wo_load(0)
            wo_load(1)
            x_load(1)
            for c in range(2, 2 * NE):
                wo_load(c)
            with sp.Fori(2, NB) as b:
                x_load(b)
                res_load(b - 1)

            def wq_load(g, e):
                if counted(4 * g + e - 1):
                    sp.wait_ge(wq_l_ready, 4 * g + e - 1)
                sp.dma_start(wq_r[:, e % 2, :], wq_d[g * NE + e]).then_inc(wq_in[e % 2], 16)

            def wd_load(g, e):
                if counted(4 * (g - 1) + e + 1):
                    sp.wait_ge(wd_l_ready, 4 * (g - 1) + e + 1)
                sp.dma_start(wd_r[:, e, :], wd_d[g * NE + e]).then_inc(wd_in[e], 16)

            sp.wait_ge(qkv_ready, NB)
            wq_load(0, 0)
            wq_load(0, 1)
            for e in range(NE):
                wd_load(0, e)
            res_load(NB - 1)
            wq_load(0, 2)
            wq_load(0, 3)
            with sp.Fori(1, NG) as g:
                wq_load(g, 0)
                wq_load(g, 1)
                for e in range(NE):
                    wd_load(g, e)
                wq_load(g, 2)
                wq_load(g, 3)

            def f_load(p):
                if not (isinstance(p, int) and p == 0):
                    sp.wait_ge(wf_ready, 3 * p)
                sp.dma_start(fw[:, :, :], fw_d[p]).then_inc(f_in, 16)
                sp.dma_start(fm[:, :, :], fm_d[p]).then_inc(f_in, 16)

            sp.wait_ge(vg_ready, 8 * NG)
            f_load(0)
            with sp.Fori(1, NP) as p:
                f_load(p)
            for b in range(NB):
                sp.wait_ge(ln_done, LN0 + 2 * NB + b + 1)
                sp.dma_start(out_d[b], xs[:, b, :]).then_inc(out_done, 16)
            sp.wait_ge(out_done, 16 * NB)

        @block.tensor
        def _(pe):
            def split_product(out, lh, ll, rh, rl, first, last):
                pe.matmul(out, lh, rh, start=first, stop=False)
                pe.matmul(out, lh, rl, start=False, stop=False)
                return pe.matmul(out, ll, rh, start=False, stop=last)

            pe.wait_ge(consts_in, 16)
            for h in range(2):
                for i in range(16):
                    t = 16 * h + i
                    if i < 8:
                        if counted(8 * (h - 1) + i + 1):
                            pe.wait_ge(v_copied, 8 * (h - 1) + i + 1)
                    else:
                        pe.wait_ge(k_copied, 8 * h + i - 8 + 1)
                    if i == 0:
                        pe.wait_ge(ctx_h_ready, 4 * h + 4)
                        pe.wait_ge(ctx_l_ready, 4 * h + 4)
                    for k in range(KT):
                        first, last = k == 0, k == KT - 1
                        if h == 0 and i in (0, 8):
                            pe.wait_ge(wkv_h_ready, (4 if i else 0) + k + 1)
                            pe.wait_ge(wkv_l_ready, (4 if i else 0) + k + 1)
                        if i < 8:
                            cols = bass.ts(i, P)
                            mm = split_product(bank[t % 8][:, :], wk_h[:, k, cols], wk_l[:, k, cols],
                                               cT_h[:, k, :], cT_l[:, k, :], first, last)
                        else:
                            tok, cols = bass.ts((i - 8) // 2, P), bass.ts(i % 2, 512)
                            mm = split_product(bank[t % 8][:, :], cT_h[:, k, tok], cT_l[:, k, tok],
                                               wv_h[:, k, cols], wv_l[:, k, cols], first, last)
                    mm.then_inc(kv_ready, 1)

            pe.wait_ge(cototal_ready, 1)
            pe.wait_ge(v_copied, 16)
            pe.matmul(bank[7][:, 0:4], ones, csum3[:, 0:4], start=True, stop=True).then_inc(cototal_ready, 1)

            def project_qkv(b):
                pe.wait_ge(x_h_ready, b + 1)
                pe.wait_ge(x_l_ready, b + 1)
                if counted(4 * b):
                    pe.wait_ge(qT_ready, 4 * b)
                if counted(4 * b):
                    pe.wait_ge(bd_ready, 4 * b)
                for out, cols in ((bank[0][:, 0:512], slice(0, 512)), (bank[1][:, 0:256], slice(512, QKV))):
                    for k in range(KT):
                        mm = split_product(out, xT_h[:, k, :], xT_l[:, k, :], wqkv_h[:, k, cols],
                                           wqkv_l[:, k, cols], k == 0, k == KT - 1)
                mm.then_inc(qkv_ready, 1)

            def turn_block(b, j):
                pe.wait_ge(qk_ready, 2 * b + 2)
                if counted(4 * b + j - 1):
                    pe.wait_ge(qT_ready, 4 * b + j - 1)
                if counted(4 * b + j - 1):
                    pe.wait_ge(bd_ready, 4 * b + j - 1)
                pe.transpose(bank[j % 2][:, 0:P], q_tok[:, bass.ts(j, P)], ident)
                pe.transpose(bank[j % 2][:, P:2 * P], k_rep[:, bass.ts(j, P)], ident).then_inc(blkT_ready, 1)

            def self_scores(b, g):
                s, j = slot_of(b, g), g // 2
                pe.wait_ge(qT_ready, 4 * b + j + 1)
                pe.wait_ge(bd_ready, 4 * b + j + 1)
                if counted(s - 1):
                    pe.wait_ge(masked, s - 1)
                pe.matmul(bank[2 + g % 2][:, :], qT[:, j, :],
                          bd[:, j, bass.ts(g % 2, NE), :], start=True, stop=True).then_inc(scores_ready, 1)

            def turn_probs(s, g):
                pe.wait_ge(norm_done, s + 1)
                if counted(s - 1):
                    pe.wait_ge(pT_copied, s - 1)
                for e in range(NE):
                    mm = pe.transpose(bank[4 + g % 2][:, bass.ts(e, P)], prob[:, g % 4, e, :], ident)
                mm.then_inc(pT_ready, 1)

            def self_values(b, q):
                pe.wait_ge(pT_copied, 8 * b + 4 * q + 4)
                pe.wait_ge(v_two_ready, b + 1)
                if counted(2 * b + q):
                    pe.wait_ge(oT_l_ready, 2 * b + q)
                for j in range(4):
                    mm = pe.matmul(bank[6][32 * j:32 * j + 32, :],
                                   v_two[:, 4 * q + j, :, :].rearrange("p a d -> p (a d)"),
                                   pT[:, j, :], start=True, stop=True)
                mm.then_inc(pv_ready, 1)

            def self_out(b, q):
                pe.wait_ge(oT_l_ready, 2 * b + q + 1)
                pe.wait_ge(wo_ready, 4 * q + 4)
                if q == 0:
                    if counted(b):
                        pe.wait_ge(y_done, b)
                    pe.wait_ge(coeff_ready, 1)
                for e in range(NE):
                    pe.matmul(bank[7][:, :], oT_h[:, e, :], wo_s[:, 4 * q + e, :],
                              start=(q == 0 and e == 0), stop=False)
                    mm = pe.matmul(bank[7][:, :], oT_l[:, e, :], wo_s[:, 4 * q + e, :],
                                   start=False, stop=(q == 1 and e == NE - 1))
                mm.then_inc(oT_used, 1)

            def self_iteration(b, first, last):
                for g in range(8):
                    s = slot_of(b, g)
                    if g < 6:
                        self_scores(b, g + 2)
                    elif not last:
                        self_scores(b + 1, g - 6)
                    if g == 0 and not first:
                        self_values(b - 1, 1)
                    if g == 4:
                        self_values(b, 0)
                    turn_probs(s, g)
                    if g == 1 and not first:
                        self_out(b - 1, 1)
                    if g == 5:
                        self_out(b, 0)
                    if not last:
                        if g == 1:
                            project_qkv(b + 1)
                        if g >= 4:
                            turn_block(b + 1, g - 4)

            pe.wait_ge(wqkv_h_ready, KT)
            pe.wait_ge(wqkv_l_ready, KT)
            project_qkv(0)
            for j in range(4):
                turn_block(0, j)
            self_scores(0, 0)
            self_scores(0, 1)
            self_iteration(0, True, False)
            with pe.Fori(1, NB - 1) as b:
                self_iteration(b, False, False)
            self_iteration(NB - 1, False, True)
            self_values(NB - 1, 1)
            self_out(NB - 1, 1)

            def turn_rows(b, lns, ready):
                pe.wait_ge(ln_done, LN0 + lns)
                for k in range(KT):
                    mm = pe.transpose(bank[b][:, bass.ts(k, P)], xs[:, b, bass.ts(k, P)], ident)
                mm.then_inc(ready, 1)

            def q_tile(g, r):
                n, h, e = 8 * g + r, r // 4, r % 4
                if counted(n):
                    pe.wait_ge(q_copied, n)
                pe.wait_ge(wq_l_ready, 4 * g + e + 1)
                for k in range(KT):
                    tok = bass.ts(h, 512)
                    mm = split_product(bank[0][:, :], wq_h[:, e, k, :], wq_l[:, e, k, :], xnT_h[:, k, tok],
                                       xnT_l[:, k, tok], k == 0, k == KT - 1)
                mm.then_inc(q_ready, 1)

            def cross_scores(g, b):
                s = 8 * g + b
                pe.wait_ge(q_copied, 8 * g + (4 if b < 4 else 8))
                pe.wait_ge(masked, A_UNITS + s - 1)
                for e in range(NE):
                    mm = pe.matmul(bank[1 + b % 2][:, bass.ts(e, P)], qc[:, e, bass.ts(b, P)],
                                   kT[:, g, bass.ts(b, P)], start=(e == 0), stop=(e == NE - 1),
                                   skip_group_check=True)
                mm.then_inc(scores_ready, 1)

            def cross_turn(s, b):
                pe.wait_ge(norm_done, A_UNITS + s + 1)
                if counted(s - 1):
                    pe.wait_ge(pT_l_ready, s - 1)
                for e in range(NE):
                    mm = pe.transpose(bank[3 + b % 2][:, bass.ts(e, P)], prob[:, b % 4, e, :], ident)
                mm.then_inc(pT_ready, 1)

            def cross_values(s, b):
                pe.wait_ge(pT_l_ready, s + 1)
                pe.wait_ge(vg_ready, s + 1)
                if counted(s):
                    pe.wait_ge(aT_l_ready, s)
                split_product(bank[5][:, :], vg_h[:, b, :], vg_l[:, b, :], pT_h[:, :], pT_l[:, :], True, True)\
                    .then_inc(cross_pv, 1)

            def cross_out(g, b):
                s = 8 * g + b
                pe.wait_ge(aT_l_ready, s + 1)
                if counted(s - 1):
                    pe.wait_ge(cross_added, s - 1)
                for e in range(NE):
                    if b == 0:
                        pe.wait_ge(wd_l_ready, 4 * g + e + 1)
                    mm = split_product(bank[6 + b % 2][:, :], aT_h[:, b % 2, bass.ts(e, P)],
                                       aT_l[:, b % 2, bass.ts(e, P)], wd_h[:, e, :], wd_l[:, e, :],
                                       e == 0, e == NE - 1)
                    if b == 7 and e < NE - 1:
                        mm.then_inc(wd_used, 1)
                mm.then_inc(cross_y, 1)

            def cross_iteration(g, first, last):
                for b in range(NB):
                    s = 8 * g + b
                    cross_turn(s, b)
                    if b < 6:
                        cross_scores(g, b + 2)
                    elif not last:
                        cross_scores(g + 1, b - 6)
                    if b > 0:
                        cross_out(g, b - 1)
                    elif not first:
                        cross_out(g - 1, 7)
                    cross_values(s, b)
                    if b < 2:
                        q_tile(g, 6 + b)
                    elif not last:
                        q_tile(g + 1, b - 2)

            for b in range(NB):
                if b == 7:
                    pe.wait_ge(y_done, NB)
                turn_rows(b, b + 1, xnT_turned)
            for r in range(6):
                if r in (0, 4):
                    pe.wait_ge(xnT_h_ready, 4 if r == 0 else 8)
                    pe.wait_ge(xnT_l_ready, 4 if r == 0 else 8)
                q_tile(0, r)
                if r >= 4:
                    cross_scores(0, r - 4)
            cross_iteration(0, True, False)
            with pe.Fori(1, NG - 1) as g:
                cross_iteration(g, False, False)
            cross_iteration(NG - 1, False, True)
            cross_out(NG - 1, 7)

            for b in range(NB):
                if b == 6:
                    pe.wait_ge(cross_added, 63)
                if b == 7:
                    pe.wait_ge(cross_added, 64)
                turn_rows(b, NB + b + 1, x2T_turned)

            def gate_up(p, h, c):
                u = 2 * h + c
                pe.wait_ge(w13_l_ready, 2 * p + c + 1)
                if counted(4 * p + u - 1):
                    pe.wait_ge(silu_done, 4 * p + u - 1)
                if counted(4 * p + u - 1):
                    pe.wait_ge(hf_done, 4 * p + u - 1)
                for m in range(2):
                    for k in range(KT):
                        i, tok = bass.ts(c, P), bass.ts(h, 512)
                        mm = split_product(bank[2 * m + u % 2][:, :], w13_h[:, m, k, i], w13_l[:, m, k, i],
                                           x2T_h[:, k, tok], x2T_l[:, k, tok], k == 0, k == KT - 1)
                mm.then_inc(gu_ready, 1)

            def ffn_out(p, h):
                pe.wait_ge(hT_l_ready, 4 * p + 2 * h + 2)
                pe.wait_ge(w2_l_ready, p + 1)
                for t in range(4):
                    if counted(8 * p + 4 * h + t - 3):
                        pe.wait_ge(ffn_added, 8 * p + 4 * h + t - 3)
                    for c in range(2):
                        tok = bass.ts(t, P)
                        mm = split_product(bank[4 + t][:, :], hT_h[:, h, c, tok], hT_l[:, h, c, tok],
                                           w2_h[:, c, :], w2_l[:, c, :], c == 0, c == 1)
                    mm.then_inc(ffn_ready, 1)

            def ffn_piece(p, first):
                gate_up(p, 0, 0)
                gate_up(p, 0, 1)
                if not first:
                    ffn_out(p - 1, 1)
                if first:
                    pe.wait_ge(x2T_h_ready, 8)
                    pe.wait_ge(x2T_l_ready, 8)
                gate_up(p, 1, 0)
                gate_up(p, 1, 1)
                ffn_out(p, 0)

            pe.wait_ge(x2T_h_ready, 4)
            pe.wait_ge(x2T_l_ready, 4)
            ffn_piece(0, True)
            with pe.Fori(1, NP) as p:
                ffn_piece(p, False)
            ffn_out(NP - 1, 1)


        @block.scalar
        def _(act):
            def wkv_round(c):
                act.wait_ge(wkv_in[c % 2], 16 * (c // 2 + 1))
                dst = wk_h if c < 4 else wv_h
                act.activation(dst[:, c % 4, :], wkv_r[:, c % 2, :], ACT.Copy).then_inc(wkv_h_ready, 1)

            def ctx_round(h, j):
                act.wait_ge(ctx_in, 16 * (h + 1))
                if counted(16 * (h - 1) + 16):
                    act.wait_ge(kv_ready, 16 * (h - 1) + 16)
                tok = bass.ts(j, P)
                act.activation(cT_h[:, :, tok], cT_r[:, :, tok], ACT.Copy).then_inc(ctx_h_ready, 1)

            def key_out(h, i):
                act.wait_ge(kv_ready, 16 * h + i + 1)
                act.activation(kT[:, i, bass.ts(h, 512)], bank[i][:, :], ACT.Copy).then_inc(k_copied, 1)

            wkv_round(0)
            for j in range(4):
                ctx_round(0, j)
            for c in range(1, 4):
                wkv_round(c)
            for i in range(8):
                if i < 4:
                    wkv_round(4 + i)
                key_out(0, i)
            for j in range(4):
                ctx_round(1, j)
            for i in range(8):
                key_out(1, i)
            act.wait_ge(kv_ready, 24)
            for k in range(KT):
                act.wait_ge(wqkv_in[k % 2], 16 * (k // 2 + 1))
                act.activation(wqkv_h[:, k, :], wqkv_r[:, k % 2, :], ACT.Copy).then_inc(wqkv_h_ready, 1)

            def x_round(b):
                act.wait_ge(x_in, 16 * (b + 1))
                if counted(b):
                    act.wait_ge(qkv_ready, b)
                act.activation(xT_h[:, :, :], xT_r[:, :, :], ACT.Copy).then_inc(x_h_ready, 1)

            def wo_round(c):
                act.wait_ge(wo_in[c % 2], 16 * (c // 2 + 1))
                if counted(c):
                    act.wait_ge(wo_t_ready, c)
                act.activation(wo_h[:, :], wo_r[:, c % 2, :], ACT.Copy).then_inc(wo_h_ready, 1)
                act.wait_ge(wo_h_ready, c + 1)
                if counted(c):
                    act.wait_ge(wo_ready, c)
                act.activation(wo_t[:, :], wo_h[:, :].bitcast(F32), ACT.Copy, scale=half[:, 1:2])\
                   .then_inc(wo_t_ready, 1)

            def block_out(b, j):
                act.wait_ge(blkT_ready, 4 * b + j + 1)
                if counted(8 * (b - 1) + 2 * j + 2):
                    act.wait_ge(scores_ready, 8 * (b - 1) + 2 * j + 2)
                act.activation(qT[:, j, :], bank[j % 2][:, 0:P], ACT.Copy).then_inc(qT_ready, 1)

            def exps(s, i, scale):
                act.wait_ge(nbias_ready, s + 1)
                for e in range(NE):
                    a = act.activation(prob[:, i, e, :], prob[:, i, e, :], ACT.Exp, bias=nbias[:, i, e:e + 1],
                                       scale=scale, accum_out=rsum[:, i, e:e + 1])
                a.then_inc(exp_done, 1)

            def self_turned(b, g):
                s = slot_of(b, g)
                act.wait_ge(pT_ready, s + 1)
                if counted(2 * b + g // 4):
                    act.wait_ge(pv_ready, 2 * b + g // 4)
                act.activation(pT[:, g % 4, :], bank[4 + g % 2][:, :], ACT.Copy).then_inc(pT_copied, 1)

            def heads_round(b, q):
                n = 2 * b + q
                act.wait_ge(pv_ready, n + 1)
                if counted(n):
                    act.wait_ge(oT_used, n)
                act.activation(oT_h[:, :, :].rearrange("p e t -> p (e t)"), bank[6][:, :], ACT.Copy)\
                   .then_inc(oT_h_ready, 1)

            def self_iteration(b, first, last):
                for g in range(8):
                    s = slot_of(b, g)
                    if not (last and g == 7):
                        exps(s + 1, (g + 1) % 4, SELF_SCALE)
                    if g == 0 and not first:
                        heads_round(b - 1, 1)
                    if g == 4:
                        heads_round(b, 0)
                    self_turned(b, g)
                    if g == 0 and not last:
                        x_round(b + 1)
                    if not last:
                        if g >= 4:
                            block_out(b + 1, g - 4)
                    if first and g < 4:
                        wo_round(2 * g)
                        wo_round(2 * g + 1)

            act.wait_ge(kv_ready, 32)
            x_round(0)
            for j in range(4):
                block_out(0, j)
            exps(0, 0, SELF_SCALE)
            self_iteration(0, True, False)
            with act.Fori(1, NB - 1) as b:
                self_iteration(b, False, False)
            self_iteration(NB - 1, False, True)
            heads_round(NB - 1, 1)

            def rows_round(b, turned, dst, ready):
                act.wait_ge(turned, b + 1)
                act.activation(dst[:, :, bass.ts(b, P)], bank[b][:, :].rearrange("p (k t) -> p k t", k=KT),
                               ACT.Copy).then_inc(ready, 1)

            def wd_round(g, e, first):
                act.wait_ge(wd_in[e], 16 * (g + 1))
                if not first:
                    if e < NE - 1:
                        act.wait_ge(wd_used, 3 * (g - 1) + e + 1)
                    else:
                        act.wait_ge(cross_y, 8 * g)
                act.activation(wd_h[:, e, :], wd_r[:, e, :], ACT.Copy).then_inc(wd_h_ready, 1)

            def q_out(g, r, first):
                n, h, e = 8 * g + r, r // 4, r % 4
                act.wait_ge(q_ready, n + 1)
                if not first:
                    act.wait_ge(scores_ready, A_UNITS + 8 * (g - 1) + 4 * h + 4)
                act.activation(qc[:, e, bass.ts(h, 512)], bank[0][:, :], ACT.Copy).then_inc(q_copied, 1)

            def probs_round(s, b):
                act.wait_ge(pT_ready, A_UNITS + s + 1)
                if counted(s):
                    act.wait_ge(cross_pv, s)
                act.activation(pT_h[:, :], bank[3 + b % 2][:, :], ACT.Copy).then_inc(pT_h_ready, 1)

            def attended_round(s, b):
                act.wait_ge(cross_pv, s + 1)
                if counted(s - 1):
                    act.wait_ge(cross_y, s - 1)
                act.activation(aT_h[:, b % 2, :], bank[5][:, :], ACT.Copy).then_inc(aT_h_ready, 1)

            def cross_iteration(g, first, last):
                for b in range(NB):
                    s = 8 * g + b
                    probs_round(s, b)
                    if not (last and b == 7):
                        exps(A_UNITS + s + 1, (b + 1) % 4, CROSS_SCALE)
                    attended_round(s, b)
                    if b == 0 and not first:
                        for e in range(NE):
                            wd_round(g, e, False)
                    if b < 2:
                        q_out(g, 6 + b, first)
                    elif not last:
                        q_out(g + 1, b - 2, False)
                    if last and 3 <= b <= 5:
                        sign(0, b - 3)

            def sign(p, m):
                n = 3 * p + m
                act.wait_ge(fd_ready, n + 1)
                act.activation(fd[:, m % 2, :], fd[:, m % 2, :], ACT.Sign).then_inc(sign_ready, 1)

            act.wait_ge(oT_used, 16)
            act.wait_ge(y_done, NB)
            for b in range(NB):
                rows_round(b, xnT_turned, xnT_h, xnT_h_ready)
                if b in (3, 5):
                    wd_round(0, b - 3, True)
                    wd_round(0, b - 2, True)
            for r in range(6):
                q_out(0, r, True)
            exps(A_UNITS, 0, CROSS_SCALE)
            cross_iteration(0, True, False)
            with act.Fori(1, NG - 1) as g:
                cross_iteration(g, False, False)
            cross_iteration(NG - 1, False, True)

            act.wait_ge(cross_y, 64)
            for b in range(NB):
                rows_round(b, x2T_turned, x2T_h, x2T_h_ready)

            def gate(p, u):
                act.wait_ge(gu_ready, 4 * p + u + 1)
                if counted(4 * p + u - 1):
                    act.wait_ge(hf_done, 4 * p + u - 1)
                act.activation(silu[:, u % 2, :], bank[u % 2][:, :], ACT.Silu).then_inc(silu_done, 1)

            def hidden_round(p, u, first):
                act.wait_ge(hf_done, 4 * p + u + 1)
                if not first:
                    act.wait_ge(ffn_ready, 8 * (p - 1) + 4 * (u // 2) + 4)
                act.activation(hT_h[:, u // 2, u % 2, :], hf[:, u % 2, :], ACT.Copy).then_inc(hT_h_ready, 1)

            def ffn_piece(p, first, last):
                for u in range(4):
                    gate(p, u)
                    hidden_round(p, u, first)
                    if u < 3 and not last:
                        sign(p + 1, u)

            ffn_piece(0, True, False)
            with act.Fori(1, NP - 1) as p:
                ffn_piece(p, False, False)
            ffn_piece(NP - 1, False, True)


        @block.gpsimd
        def _(pool):
            def normalise(s, i):
                pool.wait_ge(rinv_ready, s + 1)
                pool.tensor_tensor(prob[:, i], prob[:, i], bcast(rinv[:, i, :], P, True), ALU.mult)\
                    .then_inc(norm_done, 1)

            def rope_sums(b):
                pool.wait_ge(rope_ready, b + 1)
                if counted(4 * b):
                    pool.wait_ge(blkT_ready, 4 * b)
                pool.tensor_tensor(q_tok[:, :], rope1[:, 0:512], rope2[:, 0:512], ALU.add).then_inc(qk_ready, 1)
                k1, k2 = (r[:, 512:640].rearrange("p (g a d) -> p g a d", a=1, d=HD).to_broadcast([P, NG, NE, HD])
                          for r in (rope1, rope2))
                pool.tensor_tensor(k_rep[:, :].rearrange("p (g e d) -> p g e d", g=NG, e=NE), k1, k2, ALU.add)\
                    .then_inc(qk_ready, 1)

            def deviation(n, b, count=1):
                pool.wait_ge(varep_done, n + 1)
                pool.tensor_tensor(rstd[:, b:b + count], varep[:, b:b + count],
                                   cpow.to_broadcast([P, count]), ALU.pow).then_inc(rstd_ready, 1)

            def co_subtract(n):
                pool.wait_ge(co_in[n % 2], 32 * (n // 2 + 1))
                pool.tensor_tensor(cw[:, n % 2], cw[:, n % 2], cm[:, n % 2], ALU.subtract).then_inc(co_sub, 1)

            def self_iteration(b, first, last):
                for g in range(8):
                    if not (last and g == 7):
                        normalise(slot_of(b, g) + 1, (g + 1) % 4)
                    if g == 3 and not first:
                        deviation(b - 1, 0)
                    if g == 3 and not last:
                        rope_sums(b + 1)

            pool.wait_ge(consts_in, 16)
            for n in range(NCO):
                co_subtract(n)
            pool.wait_ge(kv_ready, 32)
            rope_sums(0)
            normalise(0, 0)
            self_iteration(0, True, False)
            with pool.Fori(1, NB - 1) as b:
                self_iteration(b, False, False)
            self_iteration(NB - 1, False, True)

            def wq_rest(g, e):
                pool.wait_ge(wq_h_ready, 4 * g + e + 1)
                pool.tensor_tensor(wq_l[:, e, :, :].rearrange("p k d -> p (k d)"), wq_r[:, e % 2, :],
                                   wq_h[:, e, :, :].rearrange("p k d -> p (k d)").bitcast(F32), ALU.subtract)\
                    .then_inc(wq_l_ready, 1)

            def difference(p, m):
                n = 3 * p + m
                if m == 0:
                    pool.wait_ge(f_in, 32 * (p + 1))
                if counted(n - 1):
                    pool.wait_ge(wf_ready, n - 1)
                pool.tensor_tensor(fd[:, m % 2, :], fw[:, m, :], fm[:, m, :], ALU.subtract).then_inc(fd_ready, 1)

            def cross_iteration(g, first, last):
                for b in range(NB):
                    s = 8 * g + b
                    if not (last and b == 7):
                        normalise(A_UNITS + s + 1, (b + 1) % 4)
                    if b < NE and not last:
                        wq_rest(g + 1, b)
                    if last and b >= 2:
                        deviation(NB + b - 2, b - 2)
                    if last and 3 <= b <= 5:
                        difference(0, b - 3)

            for e in range(NE):
                wq_rest(0, e)
            deviation(NB - 1, 0)
            normalise(A_UNITS, 0)
            cross_iteration(0, True, False)
            with pool.Fori(1, NG - 1) as g:
                cross_iteration(g, False, False)
            cross_iteration(NG - 1, False, True)
            deviation(2 * NB - 2, NB - 2)
            deviation(2 * NB - 1, NB - 1)

            with pool.Fori(1, NP) as p:
                for m in range(3):
                    difference(p, m)
            for n, b in ((0, 0), (1, 4)):
                deviation(2 * NB + n, b, 4)

        @block.vector
        def _(dve):
            def co_reduce(n):
                dve.wait_ge(co_sub, n + 1)
                dve.tensor_reduce(csum[:, n, :], cw[:, n % 2], AXX, ALU.add, apply_absolute_value=True)\
                   .then_inc(co_sum, 1)

            dve.wait_ge(consts_in, 16)

            def wkv_rest(c):
                dve.wait_ge(wkv_h_ready, c + 1)
                h, l = (wk_h, wk_l) if c < 4 else (wv_h, wv_l)
                dve.tensor_tensor(l[:, c % 4, :], wkv_r[:, c % 2, :], h[:, c % 4, :].bitcast(F32), ALU.subtract)\
                   .then_inc(wkv_l_ready, 1)

            def ctx_rest(h, j):
                dve.wait_ge(ctx_h_ready, 4 * h + j + 1)
                tok = bass.ts(j, P)
                dve.tensor_tensor(cT_l[:, :, tok], cT_r[:, :, tok], cT_h[:, :, tok].bitcast(F32), ALU.subtract)\
                   .then_inc(ctx_l_ready, 1)

            def value_out(h, i):
                dve.wait_ge(kv_ready, 16 * h + 8 + i + 1)
                dve.tensor_copy(vv[:, 4 * h + i // 2, bass.ts(i % 2, 512)], bank[i][:, :]).then_inc(v_copied, 1)

            wkv_rest(0)
            for j in range(4):
                ctx_rest(0, j)
            for c in range(1, 8):
                wkv_rest(c)
                if c >= 5:
                    co_reduce(c - 5)
            for i in range(8):
                value_out(0, i)
                co_reduce(3 + i)
            for j in range(4):
                ctx_rest(1, j)
            for n in range(11, 19):
                co_reduce(n)
            dve.wait_ge(kv_ready, 24)
            for k in range(KT):
                dve.wait_ge(wqkv_h_ready, k + 1)
                dve.tensor_tensor(wqkv_l[:, k, :], wqkv_r[:, k % 2, :], wqkv_h[:, k, :].bitcast(F32), ALU.subtract)\
                   .then_inc(wqkv_l_ready, 1)
            for i in range(8):
                value_out(1, i)
                co_reduce(19 + i)
            for n in range(27, NCO):
                co_reduce(n)
            dve.wait_ge(co_sum, NCO)
            dve.memset(csum3[:, 3:4], 0.0).then_inc(ln_done, LN0)
            dve.tensor_reduce(csum3[:, 0:3], csum[:, :, :].rearrange("p n m -> p m n"), AXX, ALU.add)\
               .then_inc(cototal_ready, 1)
            dve.wait_ge(cototal_ready, 2)
            dve.tensor_scalar(coeff[:, :], bank[7][:, 0:3], 1.0 / (INTER * DM), None, ALU.mult)\
               .then_inc(coeff_ready, 1)

            def x_rest(b):
                dve.wait_ge(x_h_ready, b + 1)
                dve.tensor_tensor(xT_l[:, :, :], xT_r[:, :, :], xT_h[:, :, :].bitcast(F32), ALU.subtract)\
                   .then_inc(x_l_ready, 1)

            def wo_rest(c):
                dve.wait_ge(wo_t_ready, c + 1)
                dve.scalar_tensor_tensor(out=wo_s[:, c, :], in0=wo_r[:, c % 2, :], scalar=half[:, 0:1],
                                         in1=wo_t[:, :], op0=ALU.mult, op1=ALU.add).then_inc(wo_ready, 1)

            def rope(b):
                dve.wait_ge(qkv_ready, b + 1)
                if counted(2 * b):
                    dve.wait_ge(qk_ready, 2 * b)
                q, k = bank[0][:, 0:512], bank[1][:, 0:P]
                for src, at, n in ((q, 0, 32), (k, 512, 8)):
                    r1 = rope1[:, at:at + 16 * n].rearrange("p (h d) -> p h d", d=HD)
                    r2 = rope2[:, at:at + 16 * n].rearrange("p (h d) -> p h d", d=HD)
                    src = src.rearrange("p (h d) -> p h d", d=HD)
                    dve.tensor_tensor(r1, src, bcast(rcos, n, False), ALU.mult)
                    dve.tensor_tensor(r2[:, :, 0:8], src[:, :, 8:16], bcast(rsin[:, 0:8], n, False), ALU.mult)
                    dve.tensor_tensor(r2[:, :, 8:16], src[:, :, 0:8], bcast(rsin[:, 8:16], n, False), ALU.mult)
                dve.tensor_copy(v_tok[:, :], bank[1][:, P:2 * P]).then_inc(rope_ready, 1)

            def values_twice(b):
                dve.wait_ge(rope_ready, b + 1)
                if counted(2 * b):
                    dve.wait_ge(pv_ready, 2 * b)
                v = v_tok[:, :].rearrange("p (g a d) -> p g a d", a=1, d=HD).to_broadcast([P, NG, 2, HD])
                dve.tensor_copy(v_two[:, :, :, :], v).then_inc(v_two_ready, 1)

            def block_diagonal(b, j):
                dve.wait_ge(qT_ready, 4 * b + j + 1)
                if counted(8 * (b - 1) + 2 * j + 2):
                    dve.wait_ge(scores_ready, 8 * (b - 1) + 2 * j + 2)
                dve.tensor_tensor(bd[:, j, :, :], bcast(bank[j % 2][:, P:2 * P], 8, False),
                                  bcast(bmask, P, True), ALU.mult).then_inc(bd_ready, 1)

            def mask_and_max(s, i, score_bank, scale):
                dve.wait_ge(scores_ready, s + 1)
                if counted(s - 3):
                    dve.wait_ge(pT_ready, s - 3)
                dve.memset(gate_mark[:, :], 0.0)
                for e in range(NE):
                    m = dve.tensor_tensor_reduce(prob[:, i, e, :], score_bank[:, bass.ts(e, P)], cmask, 1.0,
                                                 -3.4e38, ALU.add, ALU.max, rmax[:, i, e:e + 1])
                m.then_inc(masked, 1)
                dve.wait_ge(masked, s + 1)
                dve.tensor_scalar(nbias[:, i, :], rmax[:, i, :], -scale, None, ALU.mult).then_inc(nbias_ready, 1)

            def inverse_sums(s, i):
                dve.wait_ge(exp_done, s + 1)
                if counted(s - 3):
                    dve.wait_ge(norm_done, s - 3)
                dve.reciprocal(rinv[:, i, :], rsum[:, i, :]).then_inc(rinv_ready, 1)

            def heads_rest(b, q):
                dve.wait_ge(oT_h_ready, 2 * b + q + 1)
                dve.tensor_tensor(oT_l[:, :, :].rearrange("p e t -> p (e t)"), bank[6][:, :],
                                  oT_h[:, :, :].rearrange("p e t -> p (e t)").bitcast(F32), ALU.subtract)\
                   .then_inc(oT_l_ready, 1)

            def moments_of(n, b, i, rows_ready, count):
                dve.wait_ge(rows_ready, count)
                if i == 0:
                    dve.wait_ge(ln_done, LN0 + n)
                dve.memset(gate_mark[:, :], 0.0)
                dve.bn_stats(stats[:, i, :], xs[:, b, :]).then_inc(stats_done, 1)
                dve.wait_ge(stats_done, n + 1)
                dve.memset(gate_mark[:, :], 0.0)
                dve.bn_aggr(moments[:, i, :], stats[:, i, :]).then_inc(moments_done, 1)
                dve.wait_ge(moments_done, n + 1)
                dve.tensor_scalar(varep[:, i:i + 1], moments[:, i, 1:2], EPS, None, ALU.add).then_inc(varep_done, 1)

            def layer_norm(n, b, i):
                dve.wait_ge(rstd_ready, n + 1)
                dve.tensor_scalar(xs[:, b, :], xs[:, b, :], moments[:, i, 0:1], rstd[:, i:i + 1], ALU.subtract,
                                  ALU.mult).then_inc(ln_done, 1)

            def self_residual(b):
                dve.wait_ge(oT_used, 2 * b + 2)
                dve.wait_ge(res_in, 16 * (b + 1))
                dve.tensor_tensor(xs[:, b, :], bank[7][:, :], res[:, :], ALU.add).then_inc(y_done, 1)

            def self_iteration(b, first, last):
                for g in range(8):
                    s = slot_of(b, g)
                    if not (last and g >= 6):
                        mask_and_max(s + 2, (g + 2) % 4, bank[2 + g % 2], SELF_SCALE)
                    if not (last and g == 7):
                        inverse_sums(s + 1, (g + 1) % 4)
                    if g == 0 and not first:
                        heads_rest(b - 1, 1)
                    if g == 4:
                        heads_rest(b, 0)
                    if not first:
                        if g == 1:
                            values_twice(b)
                        if g == 2:
                            self_residual(b - 1)
                            moments_of(b - 1, b - 1, 0, y_done, b)
                        if g == 4:
                            layer_norm(b - 1, b - 1, 0)
                    if first and g < 4:
                        wo_rest(2 * g)
                        wo_rest(2 * g + 1)
                    if not last:
                        if g == 0:
                            x_rest(b + 1)
                        if g == 2:
                            rope(b + 1)
                        if g >= 4:
                            block_diagonal(b + 1, g - 4)

            x_rest(0)
            rope(0)
            values_twice(0)
            for j in range(4):
                block_diagonal(0, j)
            mask_and_max(0, 0, bank[2], SELF_SCALE)
            mask_and_max(1, 1, bank[3], SELF_SCALE)
            inverse_sums(0, 0)
            self_iteration(0, True, False)
            with dve.Fori(1, NB - 1) as b:
                self_iteration(b, False, False)
            self_iteration(NB - 1, False, True)
            heads_rest(NB - 1, 1)
            self_residual(NB - 1)
            moments_of(NB - 1, NB - 1, 0, y_done, NB)

            def rows_rest(b, h_ready, h, l, ready):
                dve.wait_ge(h_ready, b + 1)
                tok = bass.ts(b, P)
                dve.tensor_tensor(l[:, :, tok], bank[b][:, :].rearrange("p (k t) -> p k t", k=KT),
                                  h[:, :, tok].bitcast(F32), ALU.subtract).then_inc(ready, 1)

            def wq_round(g, e, first):
                dve.wait_ge(wq_in[e % 2], 16 * (2 * g + e // 2 + 1))
                if not first:
                    dve.wait_ge(q_ready, 8 * (g - 1) + 4 + e + 1)
                dve.tensor_copy(wq_h[:, e, :, :].rearrange("p k d -> p (k d)"), wq_r[:, e % 2, :])\
                   .then_inc(wq_h_ready, 1)

            def wd_rest(g, e):
                dve.wait_ge(wd_h_ready, 4 * g + e + 1)
                dve.tensor_tensor(wd_l[:, e, :], wd_r[:, e, :], wd_h[:, e, :].bitcast(F32), ALU.subtract)\
                   .then_inc(wd_l_ready, 1)

            def values_split(g, b, first):
                s = 8 * g + b
                if not first:
                    dve.wait_ge(cross_pv, s - 7)
                src = vv[:, b, bass.ts(g, P)]
                dve.tensor_copy(vg_h[:, b, :], src).then_inc(vg_h_ready, 1)
                dve.wait_ge(vg_h_ready, s + 1)
                dve.tensor_tensor(vg_l[:, b, :], src, vg_h[:, b, :].bitcast(F32), ALU.subtract)\
                   .then_inc(vg_ready, 1)

            def probs_rest(s, b):
                dve.wait_ge(pT_h_ready, s + 1)
                dve.tensor_tensor(pT_l[:, :], bank[3 + b % 2][:, :], pT_h[:, :].bitcast(F32), ALU.subtract)\
                   .then_inc(pT_l_ready, 1)

            def attended_rest(s, b):
                dve.wait_ge(aT_h_ready, s + 1)
                dve.tensor_tensor(aT_l[:, b % 2, :], bank[5][:, :], aT_h[:, b % 2, :].bitcast(F32),
                                  ALU.subtract).then_inc(aT_l_ready, 1)

            def cross_add(g, b):
                s = 8 * g + b
                dve.wait_ge(cross_y, s + 1)
                dve.wait_ge(ln_done, LN0 + b + 1)
                dve.tensor_tensor(xs[:, b, :], bank[6 + b % 2][:, :], xs[:, b, :], ALU.add)\
                   .then_inc(cross_added, 1)

            def rebuild(p, m):
                n = 3 * p + m
                dve.wait_ge(sign_ready, n + 1)
                if m < 2:
                    if counted(2 * p):
                        dve.wait_ge(w13_l_ready, 2 * p)
                else:
                    if counted(p):
                        dve.wait_ge(w2_l_ready, p)
                dve.scalar_tensor_tensor(out=wf[:, m, :], in0=fd[:, m % 2, :], scalar=coeff[:, m:m + 1],
                                         in1=fm[:, m, :], op0=ALU.mult, op1=ALU.add).then_inc(wf_ready, 1)

            def w13_split(p, c, first):
                dve.wait_ge(wf_ready, 3 * p + 2)
                if not first:
                    dve.wait_ge(gu_ready, 4 * (p - 1) + 3 + c)
                i = bass.ts(c, P)
                for m in range(2):
                    src = wf[:, m, :].rearrange("p (k i) -> p k i", k=KT)[:, :, i]
                    dve.tensor_copy(w13_h[:, m, :, i], src).then_inc(w13_h_ready, 1)
                for m in range(2):
                    src = wf[:, m, :].rearrange("p (k i) -> p k i", k=KT)[:, :, i]
                    dve.wait_ge(w13_h_ready, 4 * p + 2 * c + m + 1)
                    w = dve.tensor_tensor(w13_l[:, m, :, i], src, w13_h[:, m, :, i].bitcast(F32), ALU.subtract)
                w.then_inc(w13_l_ready, 1)

            def w2_split(p, first):
                dve.wait_ge(wf_ready, 3 * p + 3)
                if not first:
                    dve.wait_ge(ffn_ready, 8 * p)
                h, l = (w[:, :, :].rearrange("p c n -> p (c n)") for w in (w2_h, w2_l))
                dve.tensor_copy(h, wf[:, 2, :]).then_inc(w2_h_ready, 1)
                dve.wait_ge(w2_h_ready, p + 1)
                dve.tensor_tensor(l, wf[:, 2, :], h.bitcast(F32), ALU.subtract).then_inc(w2_l_ready, 1)

            def cross_iteration(g, first, last):
                for b in range(NB):
                    s = 8 * g + b
                    if not (last and b >= 6):
                        mask_and_max(A_UNITS + s + 2, (b + 2) % 4, bank[1 + b % 2], CROSS_SCALE)
                    probs_rest(s, b)
                    if b > 0:
                        cross_add(g, b - 1)
                    elif not first:
                        cross_add(g - 1, 7)
                    if not (last and b == 7):
                        inverse_sums(A_UNITS + s + 1, (b + 1) % 4)
                    attended_rest(s, b)
                    if b == 0 and not first:
                        for e in range(NE):
                            wd_rest(g, e)
                    if not last:
                        if b < NE:
                            wq_round(g + 1, b, False)
                        values_split(g + 1, b, False)
                    else:
                        if b >= 1:
                            moments_of(NB + b - 1, b - 1, b - 1, cross_added, s)
                        if b >= 2:
                            layer_norm(NB + b - 2, b - 2, b - 2)
                        if 3 <= b <= 5:
                            rebuild(0, b - 3)
                        if b >= 6:
                            w13_split(0, b - 6, True)

            dve.wait_ge(qkv_ready, NB)
            for e in range(NE):
                wq_round(0, e, True)
            for b in range(NB):
                values_split(0, b, True)
            layer_norm(NB - 1, NB - 1, 0)
            for b in range(NB):
                rows_rest(b, xnT_h_ready, xnT_h, xnT_l, xnT_l_ready)
            for e in range(NE):
                wd_rest(0, e)
            mask_and_max(A_UNITS, 0, bank[1], CROSS_SCALE)
            mask_and_max(A_UNITS + 1, 1, bank[2], CROSS_SCALE)
            inverse_sums(A_UNITS, 0)
            cross_iteration(0, True, False)
            with dve.Fori(1, NG - 1) as g:
                cross_iteration(g, False, False)
            cross_iteration(NG - 1, False, True)
            layer_norm(2 * NB - 2, NB - 2, NB - 2)
            cross_add(NG - 1, 7)
            moments_of(2 * NB - 1, NB - 1, NB - 1, cross_added, 64)
            layer_norm(2 * NB - 1, NB - 1, NB - 1)

            w2_split(0, True)
            for b in range(NB):
                rows_rest(b, x2T_h_ready, x2T_h, x2T_l, x2T_l_ready)

            def hidden(p, u):
                dve.wait_ge(silu_done, 4 * p + u + 1)
                if counted(4 * p + u - 1):
                    dve.wait_ge(hT_l_ready, 4 * p + u - 1)
                dve.tensor_tensor(hf[:, u % 2, :], bank[2 + u % 2][:, :], silu[:, u % 2, :], ALU.mult)\
                   .then_inc(hf_done, 1)

            def hidden_rest(p, u):
                dve.wait_ge(hT_h_ready, 4 * p + u + 1)
                dve.tensor_tensor(hT_l[:, u // 2, u % 2, :], hf[:, u % 2, :],
                                  hT_h[:, u // 2, u % 2, :].bitcast(F32), ALU.subtract).then_inc(hT_l_ready, 1)

            def ffn_add(p, h, t):
                n, b = 8 * p + 4 * h + t, 4 * h + t
                dve.wait_ge(ffn_ready, n + 1)
                dve.wait_ge(ln_done, LN0 + 2 * NB)
                dve.tensor_tensor(xs[:, b, :], bank[4 + t][:, :], xs[:, b, :], ALU.add).then_inc(ffn_added, 1)

            def ffn_piece(p, first, last):
                for u in range(4):
                    hidden(p, u)
                    hidden_rest(p, u)
                    if u == 1 and not first:
                        for t in range(4):
                            ffn_add(p - 1, 1, t)
                        w2_split(p, False)
                    if not last:
                        if u < 3:
                            rebuild(p + 1, u)
                        if u >= 2:
                            w13_split(p + 1, u - 2, False)
                for t in range(4):
                    ffn_add(p, 0, t)

            ffn_piece(0, True, False)
            with dve.Fori(1, NP - 1) as p:
                ffn_piece(p, False, False)
            ffn_piece(NP - 1, False, True)
            for h in range(2):
                n = 2 * NB + 4 * h
                for t in range(4):
                    if h:
                        ffn_add(NP - 1, 1, t)
                    b = 4 * h + t
                    dve.wait_ge(ffn_added, 8 * NP - 8 + b + 1)
                    dve.bn_stats(stats[:, b, :], xs[:, b, :]).then_inc(stats_done, 1)
                for t in range(4):
                    dve.wait_ge(stats_done, n + t + 1)
                    dve.bn_aggr(moments[:, 4 * h + t, :], stats[:, 4 * h + t, :]).then_inc(moments_done, 1)
                dve.wait_ge(moments_done, n + 4)
                dve.tensor_scalar(varep[:, 4 * h:4 * h + 4], moments[:, 4 * h:4 * h + 4, 1], EPS, None, ALU.add)\
                   .then_inc(varep_done, 1)
                dve.wait_ge(rstd_ready, 2 * NB + h + 1)
                for b in range(4 * h, 4 * h + 4):
                    dve.tensor_scalar(xs[:, b, :], xs[:, b, :], moments[:, b, 0:1], rstd[:, b:b + 1],
                                      ALU.subtract, ALU.mult).then_inc(ln_done, 1)


def constants():
    c = np.zeros((P, C_ALL), np.float32)
    r = np.arange(P)
    c[:, C_ID:C_ID + P] = np.eye(P)
    c[:, C_MASK:C_MASK + P] = np.where(r[None, :] <= r[:, None], 0.0, NEG)
    c[:, C_BM:C_BM + 8] = (r[:, None] // HD) == np.arange(8)[None, :]
    freq = (1.0 / np.float32(10000.0) ** (np.arange(0, HD, 2, dtype=np.float32) / np.float32(HD))).astype(np.float32)
    angle = r.astype(np.float32)[:, None] * freq[None, :]
    cos, sin = np.cos(angle), np.sin(angle)
    c[:, C_COS:C_COS + HD] = np.concatenate([cos, cos], 1)
    c[:, C_SIN:C_SIN + HD] = np.concatenate([-sin, sin], 1)
    second = (r // HD) % 2
    c[:, C_HALF] = second
    c[:, C_HALF + 1] = 1 - 2 * second
    c[:, C_EPS] = EPS
    c[:, C_POW] = -0.5
    c[:, C_ONE:C_ONE + P] = 1.0
    return c


def kernel(x, ctx_4096, L0_attn_w_qkv, L0_attn_w_o, L0_xattn_Wq, L0_xattn_Wk, L0_xattn_Wv, L0_xattn_Wd,
           L0_ffn_w1, L0_ffn_mean_w1, L0_ffn_w2, L0_ffn_mean_w2, L0_ffn_w3, L0_ffn_mean_w3):
    import concourse.bacc as bacc
    from concourse.bass_utils import run_bass_kernel_spmd

    def arr(a):
        return np.asarray(a)

    x, c4 = arr(x), arr(ctx_4096)
    turn = np.concatenate([np.arange(0, HD, 2), np.arange(1, HD, 2)])
    cols = np.concatenate([(np.arange(40)[:, None] * HD + turn[None, :]).ravel(), np.arange(640, QKV)])
    wqkv = arr(L0_attn_w_qkv)[:, cols]

    def w13(w):
        return arr(w).reshape(NP, PIECE, KT, P).transpose(0, 3, 2, 1).reshape(NP, P, 1024)

    def w2(w):
        return arr(w).T.reshape(NP, 2, P, DM).transpose(0, 2, 1, 3).reshape(NP, P, 1024)

    wo = arr(L0_attn_w_o).reshape(2, 4, NE, 1, HD, DM)
    wo = np.concatenate([wo, wo], 3).transpose(1, 3, 4, 0, 2, 5)
    arrays = {
        "consts": constants(),
        "x": x,
        "xT": x.reshape(NB, P, KT, P).transpose(0, 3, 2, 1),
        "ctxT": c4.reshape(2, 512, KT, P).transpose(0, 3, 2, 1),
        "wkv": np.concatenate([arr(L0_xattn_Wk).T.reshape(KT, P, 1024), arr(L0_xattn_Wv).T.reshape(KT, P, 1024)]),
        "wqkv": wqkv.reshape(KT, P, QKV).transpose(1, 0, 2),
        "wo": wo.reshape(P, 2 * NE, DM),
        "wq": arr(L0_xattn_Wq).reshape(NG * NE, P, KT, P).transpose(0, 3, 2, 1).reshape(NG * NE, P, 512),
        "wd": arr(L0_xattn_Wd).T.reshape(NG * NE, P, DM),
        "fw": np.stack([w13(L0_ffn_w1), w13(L0_ffn_w3), w2(L0_ffn_w2)], 2),
        "fm": np.stack([w13(L0_ffn_mean_w1), w13(L0_ffn_mean_w3), w2(L0_ffn_mean_w2)], 2),
    }
    arrays = {n + "_dram": np.ascontiguousarray(a) for n, a in arrays.items()}
    nc = bacc.Bacc("TRN2", target_bir_lowering=False, num_devices=1)
    args = [nc.dram_tensor(n, a.shape, mybir.dt.from_np(a.dtype), kind="ExternalInput").ap()
            for n, a in arrays.items()]
    out = nc.dram_tensor("out", (NB, P, DM), F32, kind="ExternalOutput").ap()
    decoder_layer(nc, *args, out)
    r = run_bass_kernel_spmd(nc, [arrays], core_ids=[0])
    return r.results[0]["out"]
```

```python
from contextlib import ExitStack

import numpy as np

import concourse.bass as bass
from concourse import mybir

F32 = mybir.dt.float32
F32R = mybir.dt.float32r
ALU = mybir.AluOpType
ACT = mybir.ActivationFunctionType
AXX = mybir.AxisListType.X

P = 128
NB = 8
DM = 512
KT = DM // P
NG = 8
NE = 4
HD = 16
QKV = 768
INTER = 1792
PIECE = 256
NP = INTER // PIECE
NCO = NP * NB
COW = 1024 // NB
SELF_SCALE = 0.25
CROSS_SCALE = float(P) ** -0.5
NEG = -3.0e38
EPS = 1e-5

C_ID, C_MASK, C_BM, C_COS, C_SIN, C_HALF, C_EPS, C_POW, C_ONE = 0, 128, 256, 264, 280, 296, 298, 299, 300
C_ALL = 428


def counted(value):
    return not (isinstance(value, int) and value <= 0)


def bcast(ap, n, inner):
    if inner:
        a = ap.rearrange("p (a b) -> p a b", b=1)
        return a.to_broadcast([a.shape[0], a.shape[1], n])
    a = ap.rearrange("p (b a) -> p b a", b=1)
    return a.to_broadcast([a.shape[0], n, a.shape[2]])


def decoder_layer(nc, consts_d, x_d, xT_d, ctxT_d, wkv_d, wqkv_d, wo_d, wq_d, wd_d, fw_d, fm_d, out_d):
    with ExitStack() as ctx:
        def sb(name, shape, dt=F32, stack=ctx):
            return stack.enter_context(nc.sbuf_tensor(name, shape, dt))

        consts = sb("consts", [P, C_ALL])
        ident = consts[:, C_ID:C_ID + P]
        cmask = consts[:, C_MASK:C_MASK + P]
        bmask = consts[:, C_BM:C_BM + 8]
        rcos = consts[:, C_COS:C_COS + HD]
        rsin = consts[:, C_SIN:C_SIN + HD]
        half = consts[:, C_HALF:C_HALF + 2]
        ceps = consts[:, C_EPS:C_EPS + 1]
        cpow = consts[:, C_POW:C_POW + 1]
        ones = consts[:, C_ONE:C_ONE + P]
        xs = sb("xs", [P, NB, DM])
        csum = sb("csum", [P, NCO, 3])
        csum3 = sb("csum3", [P, 4])
        coeff = sb("coeff", [P, 3])
        stats = sb("stats", [P, NB, 6])
        moments = sb("moments", [P, NB, 2])
        varep = sb("varep", [P, NB])
        rstd = sb("rstd", [P, NB])
        rmax = sb("rmax", [P, 4, NE])
        nbias = sb("nbias", [P, 4, NE])
        rsum = sb("rsum", [P, 4, NE])
        rinv = sb("rinv", [P, 4, NE])
        gate_mark = sb("gate_mark", [P, 1])
        co_mark = sb("co_mark", [P, 1])
        prob = sb("prob", [P, 4, NE, P])

        with ExitStack() as r_kv:
            kT = sb("kT", [P, NG, NB * P], F32, r_kv)
            vv = sb("vv", [P, NB, NG * P], F32, r_kv)
            with ExitStack() as r1:
                wk_h = sb("wk_h", [P, KT, 1024], F32R, r1)
                wk_l = sb("wk_l", [P, KT, 1024], F32R, r1)
            with ExitStack() as r1:
                wqkv_h = sb("wqkv_h", [P, KT, QKV], F32R, r1)
                wqkv_l = sb("wqkv_l", [P, KT, QKV], F32R, r1)
                wqkv_r = sb("wqkv_r", [P, 2, QKV], F32, r1)
                qT = sb("qT", [P, NE, P], F32, r1)
                v_tok = sb("v_tok", [P, P], F32, r1)
                v_two = sb("v_two", [P, NG, 2, HD], F32, r1)
            with ExitStack() as r1:
                wq_h = sb("wq_h", [P, NE, KT, P], F32R, r1)
                wq_l = sb("wq_l", [P, NE, KT, P], F32R, r1)
                wq_r = sb("wq_r", [P, 2, KT * P], F32, r1)
                wd_r = sb("wd_r", [P, NE, DM], F32, r1)
                vg_h = sb("vg_h", [P, NB, P], F32R, r1)
                vg_l = sb("vg_l", [P, NB, P], F32R, r1)
            sb("region1", [P, 9216], F32, r_kv)
            with ExitStack() as r2:
                wv_h = sb("wv_h", [P, KT, 1024], F32R, r2)
                wv_l = sb("wv_l", [P, KT, 1024], F32R, r2)
                cT_h1 = sb("cT_h1", [P, KT, DM], F32R, r2)
                cT_l1 = sb("cT_l1", [P, KT, DM], F32R, r2)
                wkv_r = sb("wkv_r", [P, 2, 1024], F32, r2)
                cT_r = sb("cT_r", [P, KT, DM], F32, r2)
                cT_h0 = sb("cT_h0", [P, KT, DM], F32R, r2)
                cT_l0 = sb("cT_l0", [P, KT, DM], F32R, r2)
                cT_h, cT_l = (cT_h0, cT_h1), (cT_l0, cT_l1)
            with ExitStack() as r2:
                wo_s = sb("wo_s", [P, 2 * NE, DM], F32R, r2)
                pT = sb("pT", [P, NE, DM], F32, r2)
                oT_h = sb("oT_h", [P, NE, P], F32R, r2)
                oT_l = sb("oT_l", [P, NE, P], F32R, r2)
                wo_r = sb("wo_r", [P, 2, DM], F32, r2)
                wo_h = sb("wo_h", [P, DM], F32R, r2)
                wo_t = sb("wo_t", [P, DM], F32, r2)
                res = sb("res", [P, DM], F32, r2)
                sb("a_gap", [P, 2560], F32, r2)
                bd = sb("bd", [P, NE, 8, P], F32, r2)
                xT_r = sb("xT_r", [P, KT, P], F32, r2)
                xT_h = sb("xT_h", [P, KT, P], F32R, r2)
                xT_l = sb("xT_l", [P, KT, P], F32R, r2)
                rope1 = sb("rope1", [P, 640], F32, r2)
                rope2 = sb("rope2", [P, 640], F32, r2)
                q_tok = sb("q_tok", [P, DM], F32, r2)
                k_rep = sb("k_rep", [P, DM], F32, r2)
            with ExitStack() as r2:
                xnT_h = sb("xnT_h", [P, KT, NB * P], F32R, r2)
                xnT_l = sb("xnT_l", [P, KT, NB * P], F32R, r2)
                qc = sb("qc", [P, NE, NB * P], F32, r2)
                wd_h = sb("wd_h", [P, NE, DM], F32R, r2)
                wd_l = sb("wd_l", [P, NE, DM], F32R, r2)
                pT_h = sb("pT_h", [P, DM], F32R, r2)
                pT_l = sb("pT_l", [P, DM], F32R, r2)
                aT_h = sb("aT_h", [P, 2, DM], F32R, r2)
                aT_l = sb("aT_l", [P, 2, DM], F32R, r2)
                cw = sb("cw", [P, 3, COW], F32, r2)
                cm = sb("cm", [P, 3, COW], F32, r2)
        with ExitStack() as r_ffn:
            x2T_h = sb("x2T_h", [P, KT, NB * P], F32R, r_ffn)
            x2T_l = sb("x2T_l", [P, KT, NB * P], F32R, r_ffn)
            fw = sb("fw", [P, 3, 1024], F32, r_ffn)
            fm = sb("fm", [P, 3, 1024], F32, r_ffn)
            fd = sb("fd", [P, 2, 1024], F32, r_ffn)
            wf = sb("wf", [P, 3, 1024], F32, r_ffn)
            w13_h = sb("w13_h", [P, 2, KT, PIECE], F32R, r_ffn)
            w13_l = sb("w13_l", [P, 2, KT, PIECE], F32R, r_ffn)
            w2_h = sb("w2_h", [P, 2, DM], F32R, r_ffn)
            w2_l = sb("w2_l", [P, 2, DM], F32R, r_ffn)
            silu = sb("silu", [P, 2, DM], F32, r_ffn)
            hf = sb("hf", [P, 2, DM], F32, r_ffn)
            hT_h = sb("hT_h", [P, 2, 2, DM], F32R, r_ffn)
            hT_l = sb("hT_l", [P, 2, 2, DM], F32R, r_ffn)
        bank = [ctx.enter_context(nc.psum_tensor(f"bank{i}", [P, 512], F32)) for i in range(8)]

        def sem(name):
            return ctx.enter_context(nc.semaphore(name))

        consts_in = sem("consts_in")
        wkv_in = [sem(f"wkv_in{i}") for i in range(2)]
        ctx_in = [sem(f"ctx_in{k}") for k in range(KT)]
        wkv_h_ready, wkv_l_ready = sem("wkv_h_ready"), sem("wkv_l_ready")
        ctx_h_ready, ctx_l_ready = sem("ctx_h_ready"), sem("ctx_l_ready")
        kv_ready, k_copied, v_copied = sem("kv_ready"), sem("k_copied"), sem("v_copied")
        wqkv_in = [sem(f"wqkv_in{i}") for i in range(2)]
        wqkv_h_ready, wqkv_l_ready = sem("wqkv_h_ready"), sem("wqkv_l_ready")
        wo_in = [sem(f"wo_in{i}") for i in range(2)]
        wo_h_ready, wo_t_ready, wo_ready = sem("wo_h_ready"), sem("wo_t_ready"), sem("wo_ready")
        x_in, res_in = sem("x_in"), sem("res_in")
        co_in, co_sub, co_sum = sem("co_in"), sem("co_sub"), sem("co_sum")
        cototal_ready, coeff_ready = sem("cototal_ready"), sem("coeff_ready")
        x_h_ready, x_l_ready, qkv_ready = sem("x_h_ready"), sem("x_l_ready"), sem("qkv_ready")
        rope_ready, qk_ready, blkT_ready = sem("rope_ready"), sem("qk_ready"), sem("blkT_ready")
        qT_ready, bd_ready, v_two_ready = sem("qT_ready"), sem("bd_ready"), sem("v_two_ready")
        scores_ready, masked, nbias_ready = sem("scores_ready"), sem("masked"), sem("nbias_ready")
        exp_done, rinv_ready, norm_done = sem("exp_done"), sem("rinv_ready"), sem("norm_done")
        pT_ready, pT_copied = sem("pT_ready"), sem("pT_copied")
        pv_ready, oT_h_ready, oT_l_ready = sem("pv_ready"), sem("oT_h_ready"), sem("oT_l_ready")
        oT_used, oproj_ready, y_done = sem("oT_used"), sem("oproj_ready"), sem("y_done")
        stats_done, moments_done, varep_done = sem("stats_done"), sem("moments_done"), sem("varep_done")
        rstd_ready, ln_done = sem("rstd_ready"), sem("ln_done")

        xnT_turned, xnT_h_ready, xnT_l_ready = sem("xnT_turned"), sem("xnT_h_ready"), sem("xnT_l_ready")
        wq_in, wd_in = [sem(f"wq_in{i}") for i in range(2)], [sem(f"wd_in{i}") for i in range(NE)]
        wq_h_ready, wq_l_ready = sem("wq_h_ready"), sem("wq_l_ready")
        wd_h_ready, wd_l_ready, wd_used = sem("wd_h_ready"), sem("wd_l_ready"), sem("wd_used")
        vg_h_ready, vg_ready = sem("vg_h_ready"), sem("vg_ready")
        q_ready, q_copied = sem("q_ready"), sem("q_copied")
        pT_h_ready, pT_l_ready = sem("pT_h_ready"), sem("pT_l_ready")
        cross_pv, aT_h_ready, aT_l_ready = sem("cross_pv"), sem("aT_h_ready"), sem("aT_l_ready")
        cross_y, cross_added = sem("cross_y"), sem("cross_added")
        x2T_turned, x2T_h_ready, x2T_l_ready = sem("x2T_turned"), sem("x2T_h_ready"), sem("x2T_l_ready")
        f_in, fd_ready, sign_ready, wf_ready = sem("f_in"), sem("fd_ready"), sem("sign_ready"), sem("wf_ready")
        w13_h_ready, w13_l_ready = sem("w13_h_ready"), sem("w13_l_ready")
        w2_h_ready, w2_l_ready = sem("w2_h_ready"), sem("w2_l_ready")
        gu_ready, silu_done, hf_done = sem("gu_ready"), sem("silu_done"), sem("hf_done")
        hT_h_ready, hT_l_ready = sem("hT_h_ready"), sem("hT_l_ready")
        ffn_ready, ffn_added, out_done = sem("ffn_ready"), sem("ffn_added"), sem("out_done")

        def slot_of(b, g):
            return b * 8 + g

        LN0 = 1
        A_UNITS = NB * NG

        block = ctx.enter_context(nc.Block())

        @block.sync
        def _(sp):
            for c in range(8):
                if c >= 2:
                    sp.wait_ge(wkv_l_ready, c - 1)
                sp.dma_start(wkv_r[:, c % 2, :], wkv_d[c]).then_inc(wkv_in[c % 2], 16)
                if c < KT:
                    sp.dma_start(cT_r[:, c, :], ctxT_d[0, :, c, :]).then_inc(ctx_in[c], 16)
            sp.dma_start(consts[:, :], consts_d).then_inc(consts_in, 16)
            for k in range(KT):
                sp.wait_ge(ctx_l_ready, k + 1)
                sp.dma_start(cT_r[:, k, :], ctxT_d[1, :, k, :]).then_inc(ctx_in[k], 16)
            sp.wait_ge(kv_ready, 16)
            sp.dma_start(xT_r[:, :, :], xT_d[0]).then_inc(x_in, 16)
            sp.wait_ge(kv_ready, 24)
            for k in range(KT):
                if k >= 2:
                    sp.wait_ge(wqkv_l_ready, k - 1)
                sp.dma_start(wqkv_r[:, k % 2, :], wqkv_d[:, k, :]).then_inc(wqkv_in[k % 2], 16)

            def wo_load(c):
                if c >= 2:
                    sp.wait_ge(wo_ready, c - 1)
                sp.dma_start(wo_r[:, c % 2, :], wo_d[:, c, :]).then_inc(wo_in[c % 2], 16)

            def x_load(b):
                sp.wait_ge(x_l_ready, b)
                sp.dma_start(xT_r[:, :, :], xT_d[b]).then_inc(x_in, 16)

            def res_load(b):
                sp.wait_ge(y_done, b)
                sp.dma_start(res[:, :], x_d[b]).then_inc(res_in, 16)

            x_load(1)
            sp.wait_ge(kv_ready, 32)
            sp.dma_start(res[:, :], x_d[0]).then_inc(res_in, 16)
            wo_load(0)
            wo_load(1)
            for c in range(2, 2 * NE):
                wo_load(c)
            with sp.Fori(2, NB) as b:
                x_load(b)
                res_load(b - 1)

            def wq_load(g, e):
                if counted(4 * g + e - 1):
                    sp.wait_ge(wq_l_ready, 4 * g + e - 1)
                sp.dma_start(wq_r[:, e % 2, :], wq_d[g * NE + e]).then_inc(wq_in[e % 2], 16)

            def wd_load(g, e):
                if counted(4 * (g - 1) + e + 1):
                    sp.wait_ge(wd_l_ready, 4 * (g - 1) + e + 1)
                sp.dma_start(wd_r[:, e, :], wd_d[g * NE + e]).then_inc(wd_in[e], 16)

            sp.wait_ge(qkv_ready, NB)
            wq_load(0, 0)
            wq_load(0, 1)
            for e in range(NE):
                wd_load(0, e)
            res_load(NB - 1)
            wq_load(0, 2)
            wq_load(0, 3)

            def co_load(g, b):
                n = 8 * g + b
                if counted(n):
                    sp.wait_ge(co_sum, n)
                sp.dma_start(cw[:, :, :], fw_d[g][:, :, bass.ts(b, COW)]).then_inc(co_in, 16)
                sp.dma_start(cm[:, :, :], fm_d[g][:, :, bass.ts(b, COW)]).then_inc(co_in, 16)

            def cross_loads(g):
                for b in range(NB):
                    if b < NE:
                        wq_load(g + 1, b)
                    co_load(g, b)
                    if b == 1:
                        for e in range(NE):
                            wd_load(g + 1, e)

            sp.wait_ge(blkT_ready, 4 * NB)
            cross_loads(0)
            with sp.Fori(1, NG - 1) as g:
                cross_loads(g)

            def f_load(p):
                if not (isinstance(p, int) and p == 0):
                    sp.wait_ge(wf_ready, 3 * p)
                sp.dma_start(fw[:, :, :], fw_d[p]).then_inc(f_in, 16)
                sp.dma_start(fm[:, :, :], fm_d[p]).then_inc(f_in, 16)

            sp.wait_ge(vg_ready, 8 * NG)
            f_load(0)
            with sp.Fori(1, NP) as p:
                f_load(p)
            for b in range(NB):
                sp.wait_ge(ln_done, LN0 + 2 * NB + b + 1)
                sp.dma_start(out_d[b], xs[:, b, :]).then_inc(out_done, 16)
            sp.wait_ge(out_done, 16 * NB)

        @block.tensor
        def _(pe):
            def split_product(out, lh, ll, rh, rl, first, last):
                pe.matmul(out, lh, rh, start=first, stop=False)
                pe.matmul(out, lh, rl, start=False, stop=False)
                return pe.matmul(out, ll, rh, start=False, stop=last)

            for k in range(KT):
                pe.wait_ge(wkv_h_ready, k + 1)
                pe.wait_ge(wkv_l_ready, k + 1)
                pe.wait_ge(ctx_h_ready, k + 1)
                pe.wait_ge(ctx_l_ready, k + 1)
                for i in range(8):
                    cols = bass.ts(i, P)
                    mm = split_product(bank[i][:, :], wk_h[:, k, cols], wk_l[:, k, cols],
                                       cT_h[0][:, k, :], cT_l[0][:, k, :], k == 0, k == KT - 1)
                    if k == KT - 1:
                        mm.then_inc(kv_ready, 1)

            def key_tile(i):
                pe.wait_ge(v_copied, i + 1)
                cols = bass.ts(i, P)
                for k in range(KT):
                    mm = split_product(bank[i][:, :], wk_h[:, k, cols], wk_l[:, k, cols],
                                       cT_h[1][:, k, :], cT_l[1][:, k, :], k == 0, k == KT - 1)
                mm.then_inc(kv_ready, 1)

            def value_tile(h, i):
                pe.wait_ge(k_copied, 8 * h + i + 1)
                tok, cols = bass.ts(i // 2, P), bass.ts(i % 2, 512)
                for k in range(KT):
                    if h == 0 and i == 0:
                        pe.wait_ge(wkv_h_ready, KT + k + 1)
                        pe.wait_ge(wkv_l_ready, KT + k + 1)
                    mm = split_product(bank[i][:, :], cT_h[h][:, k, tok], cT_l[h][:, k, tok],
                                       wv_h[:, k, cols], wv_l[:, k, cols], k == 0, k == KT - 1)
                mm.then_inc(kv_ready, 1)

            for i in range(8):
                value_tile(0, i)
            pe.wait_ge(ctx_h_ready, 8)
            pe.wait_ge(ctx_l_ready, 8)
            for i in range(8):
                key_tile(i)
            for i in range(5):
                value_tile(1, i)

            def project_qkv(b, lo, hi):
                for n in range(lo, hi):
                    k = n % KT
                    if n == 0:
                        pe.wait_ge(x_h_ready, b + 1)
                        pe.wait_ge(x_l_ready, b + 1)
                        if counted(4 * b):
                            pe.wait_ge(qT_ready, 4 * b - 1)
                            pe.wait_ge(bd_ready, 4 * b - 1)
                    if n == KT and counted(4 * b):
                        pe.wait_ge(qT_ready, 4 * b)
                        pe.wait_ge(bd_ready, 4 * b)
                    out, cols = (bank[0][:, 0:512], slice(0, 512)) if n < KT else (bank[1][:, 0:256], slice(512, QKV))
                    mm = split_product(out, xT_h[:, k, :], xT_l[:, k, :], wqkv_h[:, k, cols],
                                       wqkv_l[:, k, cols], k == 0, k == KT - 1)
                if hi == 2 * KT:
                    mm.then_inc(qkv_ready, 1)

            def turn_block(b, j):
                pe.wait_ge(qk_ready, 2 * b + 2)
                if counted(4 * b + j - 1):
                    pe.wait_ge(qT_ready, 4 * b + j - 1)
                if counted(4 * b + j - 1):
                    pe.wait_ge(bd_ready, 4 * b + j - 1)
                pe.transpose(bank[j % 2][:, 0:P], q_tok[:, bass.ts(j, P)], ident)
                pe.transpose(bank[j % 2][:, P:2 * P], k_rep[:, bass.ts(j, P)], ident).then_inc(blkT_ready, 1)

            def self_scores(b, g):
                s, j = slot_of(b, g), g // 2
                pe.wait_ge(qT_ready, 4 * b + j + 1)
                pe.wait_ge(bd_ready, 4 * b + j + 1)
                if counted(s - 1):
                    pe.wait_ge(masked, s - 1)
                pe.matmul(bank[2 + g % 2][:, :], qT[:, j, :],
                          bd[:, j, bass.ts(g % 2, NE), :], start=True, stop=True).then_inc(scores_ready, 1)

            def turn_probs(s, g):
                pe.wait_ge(norm_done, s + 1)
                if counted(s - 1):
                    pe.wait_ge(pT_copied, s - 1)
                for e in range(NE):
                    mm = pe.transpose(bank[4 + g % 2][:, bass.ts(e, P)], prob[:, g % 4, e, :], ident)
                mm.then_inc(pT_ready, 1)

            def self_values(b, q):
                pe.wait_ge(pT_copied, 8 * b + 4 * q + 4)
                pe.wait_ge(v_two_ready, b + 1)
                if counted(2 * b + q):
                    pe.wait_ge(oT_l_ready, 2 * b + q)
                for j in range(4):
                    mm = pe.matmul(bank[6][32 * j:32 * j + 32, :],
                                   v_two[:, 4 * q + j, :, :].rearrange("p a d -> p (a d)"),
                                   pT[:, j, :], start=True, stop=True)
                mm.then_inc(pv_ready, 1)

            def self_out(b, q):
                pe.wait_ge(oT_l_ready, 2 * b + q + 1)
                pe.wait_ge(wo_ready, 4 * q + 4)
                if q == 0 and counted(b):
                    pe.wait_ge(y_done, b)
                for e in range(NE):
                    pe.matmul(bank[7][:, :], oT_h[:, e, :], wo_s[:, 4 * q + e, :],
                              start=(q == 0 and e == 0), stop=False)
                    mm = pe.matmul(bank[7][:, :], oT_l[:, e, :], wo_s[:, 4 * q + e, :],
                                   start=False, stop=(q == 1 and e == NE - 1))
                mm.then_inc(oT_used, 1)

            def self_iteration(b, first, last):
                for g in range(8):
                    s = slot_of(b, g)
                    if g < 6:
                        self_scores(b, g + 2)
                    elif not last:
                        self_scores(b + 1, g - 6)
                    if g == 0 and not first:
                        self_values(b - 1, 1)
                    if g == 4:
                        self_values(b, 0)
                    turn_probs(s, g)
                    if g == 1 and not first:
                        self_out(b - 1, 1)
                    if g == 5:
                        self_out(b, 0)
                    if not last:
                        if g == 2:
                            project_qkv(b + 1, 0, 3)
                        if g == 3:
                            project_qkv(b + 1, 3, 8)
                        if g >= 5:
                            turn_block(b + 1, g - 5)
                    if g == 1 and not first:
                        turn_block(b, 3)

            pe.wait_ge(wqkv_h_ready, KT)
            pe.wait_ge(wqkv_l_ready, KT)
            pe.wait_ge(v_copied, 8 + 2)
            project_qkv(0, 0, 8)
            value_tile(1, 5)
            value_tile(1, 6)
            pe.wait_ge(consts_in, 16)
            turn_block(0, 0)
            turn_block(0, 1)
            value_tile(1, 7)
            turn_block(0, 2)
            turn_block(0, 3)
            pe.wait_ge(v_copied, 16)
            self_scores(0, 0)
            self_scores(0, 1)
            self_iteration(0, True, False)
            with pe.Fori(1, NB - 1) as b:
                self_iteration(b, False, False)
            self_iteration(NB - 1, False, True)
            self_values(NB - 1, 1)
            self_out(NB - 1, 1)

            def turn_rows(b, lns, ready):
                pe.wait_ge(ln_done, LN0 + lns)
                for k in range(KT):
                    mm = pe.transpose(bank[b][:, bass.ts(k, P)], xs[:, b, bass.ts(k, P)], ident)
                mm.then_inc(ready, 1)

            def q_tile(g, r):
                n, h, e = 8 * g + r, r // 4, r % 4
                if counted(n):
                    pe.wait_ge(q_copied, n)
                pe.wait_ge(wq_l_ready, 4 * g + e + 1)
                for k in range(KT):
                    tok = bass.ts(h, 512)
                    mm = split_product(bank[0][:, :], wq_h[:, e, k, :], wq_l[:, e, k, :], xnT_h[:, k, tok],
                                       xnT_l[:, k, tok], k == 0, k == KT - 1)
                mm.then_inc(q_ready, 1)

            def cross_scores(g, b):
                s = 8 * g + b
                pe.wait_ge(q_copied, 8 * g + (4 if b < 4 else 8))
                pe.wait_ge(masked, A_UNITS + s - 1)
                for e in range(NE):
                    mm = pe.matmul(bank[1 + b % 2][:, bass.ts(e, P)], qc[:, e, bass.ts(b, P)],
                                   kT[:, g, bass.ts(b, P)], start=(e == 0), stop=(e == NE - 1),
                                   skip_group_check=True)
                mm.then_inc(scores_ready, 1)

            def cross_turn(s, b):
                pe.wait_ge(norm_done, A_UNITS + s + 1)
                if counted(s - 1):
                    pe.wait_ge(pT_l_ready, s - 1)
                for e in range(NE):
                    mm = pe.transpose(bank[3 + b % 2][:, bass.ts(e, P)], prob[:, b % 4, e, :], ident)
                mm.then_inc(pT_ready, 1)

            def cross_values(s, b):
                pe.wait_ge(pT_l_ready, s + 1)
                pe.wait_ge(vg_ready, s + 1)
                if counted(s):
                    pe.wait_ge(aT_l_ready, s)
                split_product(bank[5][:, :], vg_h[:, b, :], vg_l[:, b, :], pT_h[:, :], pT_l[:, :], True, True)\
                    .then_inc(cross_pv, 1)

            def cross_out(g, b):
                s = 8 * g + b
                pe.wait_ge(aT_l_ready, s + 1)
                if counted(s - 1):
                    pe.wait_ge(cross_added, s - 1)
                for e in range(NE):
                    if b == 0:
                        pe.wait_ge(wd_l_ready, 4 * g + e + 1)
                    mm = split_product(bank[6 + b % 2][:, :], aT_h[:, b % 2, bass.ts(e, P)],
                                       aT_l[:, b % 2, bass.ts(e, P)], wd_h[:, e, :], wd_l[:, e, :],
                                       e == 0, e == NE - 1)
                    if b == 7 and e < NE - 1:
                        mm.then_inc(wd_used, 1)
                mm.then_inc(cross_y, 1)

            def cross_iteration(g, first, last):
                for b in range(NB):
                    s = 8 * g + b
                    cross_turn(s, b)
                    if last and b == 2:
                        pe.wait_ge(cototal_ready, 1)
                        pe.wait_ge(q_copied, 8 * NG)
                        pe.matmul(bank[0][:, 0:4], ones, csum3[:, 0:4], start=True, stop=True)\
                            .then_inc(cototal_ready, 1)
                    if b > 0:
                        cross_out(g, b - 1)
                    elif not first:
                        cross_out(g - 1, 7)
                    cross_values(s, b)
                    if b < 6:
                        cross_scores(g, b + 2)
                    elif not last:
                        cross_scores(g + 1, b - 6)
                    if b < 2:
                        q_tile(g, 6 + b)
                    elif not last:
                        q_tile(g + 1, b - 2)

            for b in range(NB):
                if b == 7:
                    pe.wait_ge(y_done, NB)
                turn_rows(b, b + 1, xnT_turned)
            for r in range(6):
                if r in (0, 4):
                    pe.wait_ge(xnT_h_ready, 4 if r == 0 else 8)
                    pe.wait_ge(xnT_l_ready, 4 if r == 0 else 8)
                q_tile(0, r)
                if r >= 4:
                    cross_scores(0, r - 4)
            cross_iteration(0, True, False)
            with pe.Fori(1, NG - 1) as g:
                cross_iteration(g, False, False)
            cross_iteration(NG - 1, False, True)
            cross_out(NG - 1, 7)

            for b in range(NB):
                if b == 6:
                    pe.wait_ge(cross_added, 63)
                if b == 7:
                    pe.wait_ge(cross_added, 64)
                turn_rows(b, NB + b + 1, x2T_turned)

            def gate_up(p, h, c):
                u = 2 * h + c
                pe.wait_ge(w13_l_ready, 2 * p + c + 1)
                if counted(4 * p + u - 1):
                    pe.wait_ge(silu_done, 4 * p + u - 1)
                if counted(4 * p + u - 1):
                    pe.wait_ge(hf_done, 4 * p + u - 1)
                for m in range(2):
                    for k in range(KT):
                        i, tok = bass.ts(c, P), bass.ts(h, 512)
                        mm = split_product(bank[2 * m + u % 2][:, :], w13_h[:, m, k, i], w13_l[:, m, k, i],
                                           x2T_h[:, k, tok], x2T_l[:, k, tok], k == 0, k == KT - 1)
                mm.then_inc(gu_ready, 1)

            def ffn_out(p, h):
                pe.wait_ge(hT_l_ready, 4 * p + 2 * h + 2)
                pe.wait_ge(w2_l_ready, p + 1)
                for t in range(4):
                    if counted(8 * p + 4 * h + t - 3):
                        pe.wait_ge(ffn_added, 8 * p + 4 * h + t - 3)
                    for c in range(2):
                        tok = bass.ts(t, P)
                        mm = split_product(bank[4 + t][:, :], hT_h[:, h, c, tok], hT_l[:, h, c, tok],
                                           w2_h[:, c, :], w2_l[:, c, :], c == 0, c == 1)
                    mm.then_inc(ffn_ready, 1)

            def ffn_piece(p, first):
                gate_up(p, 0, 0)
                gate_up(p, 0, 1)
                if not first:
                    ffn_out(p - 1, 1)
                if first:
                    pe.wait_ge(x2T_h_ready, 8)
                    pe.wait_ge(x2T_l_ready, 8)
                gate_up(p, 1, 0)
                gate_up(p, 1, 1)
                ffn_out(p, 0)

            pe.wait_ge(x2T_h_ready, 4)
            pe.wait_ge(x2T_l_ready, 4)
            ffn_piece(0, True)
            with pe.Fori(1, NP) as p:
                ffn_piece(p, False)
            ffn_out(NP - 1, 1)


        @block.scalar
        def _(act):
            def wkv_round(c):
                act.wait_ge(wkv_in[c % 2], 16 * (c // 2 + 1))
                dst = wk_h if c < 4 else wv_h
                act.activation(dst[:, c % 4, :], wkv_r[:, c % 2, :], ACT.Copy).then_inc(wkv_h_ready, 1)

            def ctx_round(h, k):
                act.wait_ge(ctx_in[k], 16 * (h + 1))
                act.activation(cT_h[h][:, k, :], cT_r[:, k, :], ACT.Copy).then_inc(ctx_h_ready, 1)

            def key_out(h, i):
                act.wait_ge(kv_ready, 16 * h + i + 1)
                act.activation(kT[:, i, bass.ts(h, 512)], bank[i][:, :], ACT.Copy).then_inc(k_copied, 1)

            for k in range(KT):
                wkv_round(k)
                ctx_round(0, k)
            for c in range(KT, 2 * KT):
                wkv_round(c)
            for i in range(8):
                key_out(0, i)
            for k in range(KT):
                ctx_round(1, k)
            for i in range(8):
                key_out(1, i)

            def x_round(b):
                act.wait_ge(x_in, 16 * (b + 1))
                if counted(b):
                    act.wait_ge(qkv_ready, b)
                act.activation(xT_h[:, :, :], xT_r[:, :, :], ACT.Copy).then_inc(x_h_ready, 1)

            def wo_round(c):
                act.wait_ge(wo_in[c % 2], 16 * (c // 2 + 1))
                if counted(c):
                    act.wait_ge(wo_t_ready, c)
                act.activation(wo_h[:, :], wo_r[:, c % 2, :], ACT.Copy).then_inc(wo_h_ready, 1)
                act.wait_ge(wo_h_ready, c + 1)
                if counted(c):
                    act.wait_ge(wo_ready, c)
                act.activation(wo_t[:, :], wo_h[:, :].bitcast(F32), ACT.Copy, scale=half[:, 1:2])\
                   .then_inc(wo_t_ready, 1)

            def block_out(b, j):
                act.wait_ge(blkT_ready, 4 * b + j + 1)
                if counted(8 * (b - 1) + 2 * j + 2):
                    act.wait_ge(scores_ready, 8 * (b - 1) + 2 * j + 2)
                act.activation(qT[:, j, :], bank[j % 2][:, 0:P], ACT.Copy).then_inc(qT_ready, 1)

            def exps(s, i, scale):
                act.wait_ge(nbias_ready, s + 1)
                for e in range(NE):
                    a = act.activation(prob[:, i, e, :], prob[:, i, e, :], ACT.Exp, bias=nbias[:, i, e:e + 1],
                                       scale=scale, accum_out=rsum[:, i, e:e + 1])
                a.then_inc(exp_done, 1)

            def self_turned(b, g):
                s = slot_of(b, g)
                act.wait_ge(pT_ready, s + 1)
                if counted(2 * b + g // 4):
                    act.wait_ge(pv_ready, 2 * b + g // 4)
                act.activation(pT[:, g % 4, :], bank[4 + g % 2][:, :], ACT.Copy).then_inc(pT_copied, 1)

            def heads_round(b, q):
                n = 2 * b + q
                act.wait_ge(pv_ready, n + 1)
                if counted(n):
                    act.wait_ge(oT_used, n)
                act.activation(oT_h[:, :, :].rearrange("p e t -> p (e t)"), bank[6][:, :], ACT.Copy)\
                   .then_inc(oT_h_ready, 1)

            def self_iteration(b, first, last):
                for g in range(8):
                    s = slot_of(b, g)
                    if not (last and g == 7):
                        exps(s + 1, (g + 1) % 4, SELF_SCALE)
                    if g == 0 and not first:
                        heads_round(b - 1, 1)
                    if g == 4:
                        heads_round(b, 0)
                    self_turned(b, g)
                    if g == 0 and not last:
                        x_round(b + 1)
                    if not last:
                        if g >= 5:
                            block_out(b + 1, g - 5)
                    if g == 1 and not first:
                        block_out(b, 3)
                    if first and g < 4:
                        wo_round(2 * g)
                        wo_round(2 * g + 1)

            x_round(0)
            for k in range(KT):
                act.wait_ge(wqkv_in[k % 2], 16 * (k // 2 + 1))
                act.activation(wqkv_h[:, k, :], wqkv_r[:, k % 2, :], ACT.Copy).then_inc(wqkv_h_ready, 1)
            for j in range(4):
                block_out(0, j)
            exps(0, 0, SELF_SCALE)
            self_iteration(0, True, False)
            with act.Fori(1, NB - 1) as b:
                self_iteration(b, False, False)
            self_iteration(NB - 1, False, True)
            heads_round(NB - 1, 1)

            def rows_round(b, turned, dst, ready):
                act.wait_ge(turned, b + 1)
                act.activation(dst[:, :, bass.ts(b, P)], bank[b][:, :].rearrange("p (k t) -> p k t", k=KT),
                               ACT.Copy).then_inc(ready, 1)

            def wd_round(g, e, first):
                act.wait_ge(wd_in[e], 16 * (g + 1))
                if not first:
                    if e < NE - 1:
                        act.wait_ge(wd_used, 3 * (g - 1) + e + 1)
                    else:
                        act.wait_ge(cross_y, 8 * g)
                act.activation(wd_h[:, e, :], wd_r[:, e, :], ACT.Copy).then_inc(wd_h_ready, 1)

            def q_out(g, r, first):
                n, h, e = 8 * g + r, r // 4, r % 4
                act.wait_ge(q_ready, n + 1)
                if not first:
                    act.wait_ge(scores_ready, A_UNITS + 8 * (g - 1) + 4 * h + 4)
                act.activation(qc[:, e, bass.ts(h, 512)], bank[0][:, :], ACT.Copy).then_inc(q_copied, 1)

            def probs_round(s, b):
                act.wait_ge(pT_ready, A_UNITS + s + 1)
                if counted(s):
                    act.wait_ge(cross_pv, s)
                act.activation(pT_h[:, :], bank[3 + b % 2][:, :], ACT.Copy).then_inc(pT_h_ready, 1)

            def attended_round(s, b):
                act.wait_ge(cross_pv, s + 1)
                if counted(s - 1):
                    act.wait_ge(cross_y, s - 1)
                act.activation(aT_h[:, b % 2, :], bank[5][:, :], ACT.Copy).then_inc(aT_h_ready, 1)

            def cross_iteration(g, first, last):
                for b in range(NB):
                    s = 8 * g + b
                    probs_round(s, b)
                    if not (last and b == 7):
                        exps(A_UNITS + s + 1, (b + 1) % 4, CROSS_SCALE)
                    attended_round(s, b)
                    if b == 0 and not first:
                        for e in range(NE):
                            wd_round(g, e, False)
                    if b < 2:
                        q_out(g, 6 + b, first)
                    elif not last:
                        q_out(g + 1, b - 2, False)
                    if last and 3 <= b <= 5:
                        sign(0, b - 3)

            def sign(p, m):
                n = 3 * p + m
                act.wait_ge(fd_ready, n + 1)
                act.activation(fd[:, m % 2, :], fd[:, m % 2, :], ACT.Sign).then_inc(sign_ready, 1)

            act.wait_ge(oT_used, 16)
            act.wait_ge(y_done, NB)
            for b in range(NB):
                rows_round(b, xnT_turned, xnT_h, xnT_h_ready)
                if b in (3, 5):
                    wd_round(0, b - 3, True)
                    wd_round(0, b - 2, True)
            for r in range(6):
                q_out(0, r, True)
            exps(A_UNITS, 0, CROSS_SCALE)
            cross_iteration(0, True, False)
            with act.Fori(1, NG - 1) as g:
                cross_iteration(g, False, False)
            cross_iteration(NG - 1, False, True)

            act.wait_ge(cross_y, 64)
            for b in range(NB):
                rows_round(b, x2T_turned, x2T_h, x2T_h_ready)

            def gate(p, u):
                act.wait_ge(gu_ready, 4 * p + u + 1)
                if counted(4 * p + u - 1):
                    act.wait_ge(hf_done, 4 * p + u - 1)
                act.activation(silu[:, u % 2, :], bank[u % 2][:, :], ACT.Silu).then_inc(silu_done, 1)

            def hidden_round(p, u, first):
                act.wait_ge(hf_done, 4 * p + u + 1)
                if not first:
                    act.wait_ge(ffn_ready, 8 * (p - 1) + 4 * (u // 2) + 4)
                act.activation(hT_h[:, u // 2, u % 2, :], hf[:, u % 2, :], ACT.Copy).then_inc(hT_h_ready, 1)

            def ffn_piece(p, first, last):
                for u in range(4):
                    gate(p, u)
                    hidden_round(p, u, first)
                    if u < 3 and not last:
                        sign(p + 1, u)

            ffn_piece(0, True, False)
            with act.Fori(1, NP - 1) as p:
                ffn_piece(p, False, False)
            ffn_piece(NP - 1, False, True)


        @block.gpsimd
        def _(pool):
            def normalise(s, i):
                pool.wait_ge(rinv_ready, s + 1)
                pool.tensor_tensor(prob[:, i], prob[:, i], bcast(rinv[:, i, :], P, True), ALU.mult)\
                    .then_inc(norm_done, 1)

            def x_rest(b):
                pool.wait_ge(x_h_ready, b + 1)
                pool.tensor_tensor(xT_l[:, :, :], xT_r[:, :, :], xT_h[:, :, :].bitcast(F32), ALU.subtract)\
                    .then_inc(x_l_ready, 1)

            def rope_sums(b):
                pool.wait_ge(rope_ready, b + 1)
                if counted(4 * b):
                    pool.wait_ge(blkT_ready, 4 * b)
                pool.tensor_tensor(q_tok[:, :], rope1[:, 0:512], rope2[:, 0:512], ALU.add).then_inc(qk_ready, 1)
                k1, k2 = (r[:, 512:640].rearrange("p (g a d) -> p g a d", a=1, d=HD).to_broadcast([P, NG, NE, HD])
                          for r in (rope1, rope2))
                pool.tensor_tensor(k_rep[:, :].rearrange("p (g e d) -> p g e d", g=NG, e=NE), k1, k2, ALU.add)\
                    .then_inc(qk_ready, 1)

            def deviation(n, b, count=1):
                pool.wait_ge(varep_done, n + 1)
                pool.tensor_tensor(rstd[:, b:b + count], varep[:, b:b + count],
                                   cpow.to_broadcast([P, count]), ALU.pow).then_inc(rstd_ready, 1)

            def co_subtract(n):
                pool.wait_ge(co_in, 32 * (n + 1))
                pool.tensor_tensor(cw[:, :, :], cw[:, :, :], cm[:, :, :], ALU.subtract).then_inc(co_sub, 1)

            def self_iteration(b, first, last):
                for g in range(8):
                    if not (last and g == 7):
                        normalise(slot_of(b, g) + 1, (g + 1) % 4)
                    if g == 2 and not first:
                        deviation(b - 1, 0)
                    if g == 0 and not last:
                        x_rest(b + 1)
                    if g == 4 and not last:
                        rope_sums(b + 1)

            pool.wait_ge(consts_in, 16)
            x_rest(0)
            rope_sums(0)
            normalise(0, 0)
            self_iteration(0, True, False)
            with pool.Fori(1, NB - 1) as b:
                self_iteration(b, False, False)
            self_iteration(NB - 1, False, True)

            def wq_rest(g, e):
                pool.wait_ge(wq_h_ready, 4 * g + e + 1)
                pool.tensor_tensor(wq_l[:, e, :, :].rearrange("p k d -> p (k d)"), wq_r[:, e % 2, :],
                                   wq_h[:, e, :, :].rearrange("p k d -> p (k d)").bitcast(F32), ALU.subtract)\
                    .then_inc(wq_l_ready, 1)

            def difference(p, m):
                n = 3 * p + m
                if m == 0:
                    pool.wait_ge(f_in, 32 * (p + 1))
                if counted(n - 1):
                    pool.wait_ge(wf_ready, n - 1)
                pool.tensor_tensor(fd[:, m % 2, :], fw[:, m, :], fm[:, m, :], ALU.subtract).then_inc(fd_ready, 1)

            def cross_iteration(g, first, last):
                for b in range(NB):
                    s = 8 * g + b
                    if not last:
                        co_subtract(s)
                    if not (last and b == 7):
                        normalise(A_UNITS + s + 1, (b + 1) % 4)
                    if b < NE and not last:
                        wq_rest(g + 1, b)
                    if last and b >= 2:
                        deviation(NB + b - 2, b - 2)
                    if last and 3 <= b <= 5:
                        difference(0, b - 3)

            for e in range(NE):
                wq_rest(0, e)
            deviation(NB - 1, 0)
            normalise(A_UNITS, 0)
            cross_iteration(0, True, False)
            with pool.Fori(1, NG - 1) as g:
                cross_iteration(g, False, False)
            cross_iteration(NG - 1, False, True)
            deviation(2 * NB - 2, NB - 2)
            deviation(2 * NB - 1, NB - 1)

            with pool.Fori(1, NP) as p:
                for m in range(3):
                    difference(p, m)
            for n, b in ((0, 0), (1, 4)):
                deviation(2 * NB + n, b, 4)

        @block.vector
        def _(dve):
            dve.memset(csum3[:, 3:4], 0.0).then_inc(ln_done, LN0)

            def wkv_rest(c):
                dve.wait_ge(wkv_h_ready, c + 1)
                h, l = (wk_h, wk_l) if c < 4 else (wv_h, wv_l)
                dve.tensor_tensor(l[:, c % 4, :], wkv_r[:, c % 2, :], h[:, c % 4, :].bitcast(F32), ALU.subtract)\
                   .then_inc(wkv_l_ready, 1)

            def ctx_rest(h, k):
                dve.wait_ge(ctx_h_ready, 4 * h + k + 1)
                dve.tensor_tensor(cT_l[h][:, k, :], cT_r[:, k, :], cT_h[h][:, k, :].bitcast(F32), ALU.subtract)\
                   .then_inc(ctx_l_ready, 1)

            def value_out(h, i):
                dve.wait_ge(kv_ready, 16 * h + 8 + i + 1)
                dve.tensor_copy(vv[:, 4 * h + i // 2, bass.ts(i % 2, 512)], bank[i][:, :]).then_inc(v_copied, 1)

            for k in range(KT):
                wkv_rest(k)
                ctx_rest(0, k)
            for c in range(KT, 2 * KT):
                wkv_rest(c)
            for i in range(8):
                value_out(0, i)
                if i % 2 == 1:
                    ctx_rest(1, i // 2)

            def wo_rest(c):
                dve.wait_ge(wo_t_ready, c + 1)
                dve.scalar_tensor_tensor(out=wo_s[:, c, :], in0=wo_r[:, c % 2, :], scalar=half[:, 0:1],
                                         in1=wo_t[:, :], op0=ALU.mult, op1=ALU.add).then_inc(wo_ready, 1)

            def rope(b):
                dve.wait_ge(qkv_ready, b + 1)
                if counted(2 * b):
                    dve.wait_ge(qk_ready, 2 * b)
                q, k = bank[0][:, 0:512], bank[1][:, 0:P]
                for src, at, n in ((q, 0, 32), (k, 512, 8)):
                    r1 = rope1[:, at:at + 16 * n].rearrange("p (h d) -> p h d", d=HD)
                    r2 = rope2[:, at:at + 16 * n].rearrange("p (h d) -> p h d", d=HD)
                    src = src.rearrange("p (h d) -> p h d", d=HD)
                    dve.tensor_tensor(r1, src, bcast(rcos, n, False), ALU.mult)
                    dve.tensor_tensor(r2[:, :, 0:8], src[:, :, 8:16], bcast(rsin[:, 0:8], n, False), ALU.mult)
                    dve.tensor_tensor(r2[:, :, 8:16], src[:, :, 0:8], bcast(rsin[:, 8:16], n, False), ALU.mult)
                dve.tensor_copy(v_tok[:, :], bank[1][:, P:2 * P]).then_inc(rope_ready, 1)

            def values_twice(b):
                dve.wait_ge(rope_ready, b + 1)
                if counted(2 * b):
                    dve.wait_ge(pv_ready, 2 * b)
                v = v_tok[:, :].rearrange("p (g a d) -> p g a d", a=1, d=HD).to_broadcast([P, NG, 2, HD])
                dve.tensor_copy(v_two[:, :, :, :], v).then_inc(v_two_ready, 1)

            def block_diagonal(b, j):
                dve.wait_ge(qT_ready, 4 * b + j + 1)
                if counted(8 * (b - 1) + 2 * j + 2):
                    dve.wait_ge(scores_ready, 8 * (b - 1) + 2 * j + 2)
                dve.tensor_tensor(bd[:, j, :, :], bcast(bank[j % 2][:, P:2 * P], 8, False),
                                  bcast(bmask, P, True), ALU.mult).then_inc(bd_ready, 1)

            def mask_and_max(s, i, score_bank, scale):
                dve.wait_ge(scores_ready, s + 1)
                if counted(s - 3):
                    dve.wait_ge(pT_ready, s - 3)
                dve.memset(gate_mark[:, :], 0.0)
                for e in range(NE):
                    m = dve.tensor_tensor_reduce(prob[:, i, e, :], score_bank[:, bass.ts(e, P)], cmask, 1.0,
                                                 -3.4e38, ALU.add, ALU.max, rmax[:, i, e:e + 1])
                m.then_inc(masked, 1)
                dve.wait_ge(masked, s + 1)
                dve.tensor_scalar(nbias[:, i, :], rmax[:, i, :], -scale, None, ALU.mult).then_inc(nbias_ready, 1)

            def inverse_sums(s, i):
                dve.wait_ge(exp_done, s + 1)
                if counted(s - 3):
                    dve.wait_ge(norm_done, s - 3)
                dve.reciprocal(rinv[:, i, :], rsum[:, i, :]).then_inc(rinv_ready, 1)

            def heads_rest(b, q):
                dve.wait_ge(oT_h_ready, 2 * b + q + 1)
                dve.tensor_tensor(oT_l[:, :, :].rearrange("p e t -> p (e t)"), bank[6][:, :],
                                  oT_h[:, :, :].rearrange("p e t -> p (e t)").bitcast(F32), ALU.subtract)\
                   .then_inc(oT_l_ready, 1)

            def moments_of(n, b, i, rows_ready, count):
                dve.wait_ge(rows_ready, count)
                if i == 0:
                    dve.wait_ge(ln_done, LN0 + n)
                dve.memset(gate_mark[:, :], 0.0)
                dve.bn_stats(stats[:, i, :], xs[:, b, :]).then_inc(stats_done, 1)
                dve.wait_ge(stats_done, n + 1)
                dve.memset(gate_mark[:, :], 0.0)
                dve.bn_aggr(moments[:, i, :], stats[:, i, :]).then_inc(moments_done, 1)
                dve.wait_ge(moments_done, n + 1)
                dve.tensor_scalar(varep[:, i:i + 1], moments[:, i, 1:2], EPS, None, ALU.add).then_inc(varep_done, 1)

            def layer_norm(n, b, i):
                dve.wait_ge(rstd_ready, n + 1)
                dve.tensor_scalar(xs[:, b, :], xs[:, b, :], moments[:, i, 0:1], rstd[:, i:i + 1], ALU.subtract,
                                  ALU.mult).then_inc(ln_done, 1)

            def self_residual(b):
                dve.wait_ge(oT_used, 2 * b + 2)
                dve.wait_ge(res_in, 16 * (b + 1))
                dve.tensor_tensor(xs[:, b, :], bank[7][:, :], res[:, :], ALU.add).then_inc(y_done, 1)

            def self_iteration(b, first, last):
                for g in range(8):
                    s = slot_of(b, g)
                    if not (last and g >= 6):
                        mask_and_max(s + 2, (g + 2) % 4, bank[2 + g % 2], SELF_SCALE)
                    if not (last and g == 7):
                        inverse_sums(s + 1, (g + 1) % 4)
                    if g == 0 and not first:
                        heads_rest(b - 1, 1)
                    if g == 4:
                        heads_rest(b, 0)
                    if not first:
                        if g == 1:
                            values_twice(b)
                        if g == 2:
                            self_residual(b - 1)
                            moments_of(b - 1, b - 1, 0, y_done, b)
                        if g == 3:
                            layer_norm(b - 1, b - 1, 0)
                    if first and g < 4:
                        wo_rest(2 * g)
                        wo_rest(2 * g + 1)
                    if not last:
                        if g == 4:
                            rope(b + 1)
                        if g >= 5:
                            block_diagonal(b + 1, g - 5)
                    if g == 1 and not first:
                        block_diagonal(b, 3)

            for k in range(KT):
                value_out(1, k)
                dve.wait_ge(wqkv_h_ready, k + 1)
                dve.tensor_tensor(wqkv_l[:, k, :], wqkv_r[:, k % 2, :], wqkv_h[:, k, :].bitcast(F32), ALU.subtract)\
                   .then_inc(wqkv_l_ready, 1)
            value_out(1, 4)
            dve.wait_ge(consts_in, 16)
            rope(0)
            value_out(1, 5)
            value_out(1, 6)
            block_diagonal(0, 0)
            block_diagonal(0, 1)
            value_out(1, 7)
            block_diagonal(0, 2)
            block_diagonal(0, 3)
            values_twice(0)
            mask_and_max(0, 0, bank[2], SELF_SCALE)
            mask_and_max(1, 1, bank[3], SELF_SCALE)
            inverse_sums(0, 0)
            self_iteration(0, True, False)
            with dve.Fori(1, NB - 1) as b:
                self_iteration(b, False, False)
            self_iteration(NB - 1, False, True)
            heads_rest(NB - 1, 1)
            self_residual(NB - 1)
            moments_of(NB - 1, NB - 1, 0, y_done, NB)

            def rows_rest(b, h_ready, h, l, ready):
                dve.wait_ge(h_ready, b + 1)
                tok = bass.ts(b, P)
                dve.tensor_tensor(l[:, :, tok], bank[b][:, :].rearrange("p (k t) -> p k t", k=KT),
                                  h[:, :, tok].bitcast(F32), ALU.subtract).then_inc(ready, 1)

            def wq_round(g, e, first):
                dve.wait_ge(wq_in[e % 2], 16 * (2 * g + e // 2 + 1))
                if not first:
                    dve.wait_ge(q_ready, 8 * (g - 1) + 4 + e + 1)
                dve.tensor_copy(wq_h[:, e, :, :].rearrange("p k d -> p (k d)"), wq_r[:, e % 2, :])\
                   .then_inc(wq_h_ready, 1)

            def wd_rest(g, e):
                dve.wait_ge(wd_h_ready, 4 * g + e + 1)
                dve.tensor_tensor(wd_l[:, e, :], wd_r[:, e, :], wd_h[:, e, :].bitcast(F32), ALU.subtract)\
                   .then_inc(wd_l_ready, 1)

            def values_split(g, b, first):
                s = 8 * g + b
                if not first:
                    dve.wait_ge(cross_pv, s - 7)
                src = vv[:, b, bass.ts(g, P)]
                dve.tensor_copy(vg_h[:, b, :], src).then_inc(vg_h_ready, 1)
                dve.wait_ge(vg_h_ready, s + 1)
                dve.tensor_tensor(vg_l[:, b, :], src, vg_h[:, b, :].bitcast(F32), ALU.subtract)\
                   .then_inc(vg_ready, 1)

            def probs_rest(s, b):
                dve.wait_ge(pT_h_ready, s + 1)
                dve.tensor_tensor(pT_l[:, :], bank[3 + b % 2][:, :], pT_h[:, :].bitcast(F32), ALU.subtract)\
                   .then_inc(pT_l_ready, 1)

            def attended_rest(s, b):
                dve.wait_ge(aT_h_ready, s + 1)
                dve.tensor_tensor(aT_l[:, b % 2, :], bank[5][:, :], aT_h[:, b % 2, :].bitcast(F32),
                                  ALU.subtract).then_inc(aT_l_ready, 1)

            def cross_add(g, b):
                s = 8 * g + b
                dve.wait_ge(cross_y, s + 1)
                dve.wait_ge(ln_done, LN0 + b + 1)
                dve.tensor_tensor(xs[:, b, :], bank[6 + b % 2][:, :], xs[:, b, :], ALU.add)\
                   .then_inc(cross_added, 1)

            def rebuild(p, m):
                n = 3 * p + m
                dve.wait_ge(sign_ready, n + 1)
                if m < 2:
                    if counted(2 * p):
                        dve.wait_ge(w13_l_ready, 2 * p)
                else:
                    if counted(p):
                        dve.wait_ge(w2_l_ready, p)
                if isinstance(p, int) and p == 0:
                    dve.wait_ge(coeff_ready, 1)
                dve.scalar_tensor_tensor(out=wf[:, m, :], in0=fd[:, m % 2, :], scalar=coeff[:, m:m + 1],
                                         in1=fm[:, m, :], op0=ALU.mult, op1=ALU.add).then_inc(wf_ready, 1)

            def w13_split(p, c, first):
                dve.wait_ge(wf_ready, 3 * p + 2)
                if not first:
                    dve.wait_ge(gu_ready, 4 * (p - 1) + 3 + c)
                i = bass.ts(c, P)
                for m in range(2):
                    src = wf[:, m, :].rearrange("p (k i) -> p k i", k=KT)[:, :, i]
                    dve.tensor_copy(w13_h[:, m, :, i], src).then_inc(w13_h_ready, 1)
                for m in range(2):
                    src = wf[:, m, :].rearrange("p (k i) -> p k i", k=KT)[:, :, i]
                    dve.wait_ge(w13_h_ready, 4 * p + 2 * c + m + 1)
                    w = dve.tensor_tensor(w13_l[:, m, :, i], src, w13_h[:, m, :, i].bitcast(F32), ALU.subtract)
                w.then_inc(w13_l_ready, 1)

            def w2_split(p, first):
                dve.wait_ge(wf_ready, 3 * p + 3)
                if not first:
                    dve.wait_ge(ffn_ready, 8 * p)
                h, l = (w[:, :, :].rearrange("p c n -> p (c n)") for w in (w2_h, w2_l))
                dve.tensor_copy(h, wf[:, 2, :]).then_inc(w2_h_ready, 1)
                dve.wait_ge(w2_h_ready, p + 1)
                dve.tensor_tensor(l, wf[:, 2, :], h.bitcast(F32), ALU.subtract).then_inc(w2_l_ready, 1)

            def co_reduce(n):
                dve.wait_ge(co_sub, n + 1)
                dve.memset(co_mark[:, :], 0.0)
                dve.tensor_reduce(csum[:, n, :], cw[:, :, :], AXX, ALU.add, apply_absolute_value=True)\
                   .then_inc(co_sum, 1)

            def cross_iteration(g, first, last):
                for b in range(NB):
                    s = 8 * g + b
                    probs_rest(s, b)
                    if not (last and b == 7):
                        inverse_sums(A_UNITS + s + 1, (b + 1) % 4)
                    if not last:
                        co_reduce(s)
                    if b > 0:
                        cross_add(g, b - 1)
                    elif not first:
                        cross_add(g - 1, 7)
                    attended_rest(s, b)
                    if not (last and b >= 6):
                        mask_and_max(A_UNITS + s + 2, (b + 2) % 4, bank[1 + b % 2], CROSS_SCALE)
                    if b == 0 and not first:
                        for e in range(NE):
                            wd_rest(g, e)
                    if not last:
                        if b < NE:
                            wq_round(g + 1, b, False)
                        values_split(g + 1, b, False)
                    else:
                        if b == 0:
                            dve.wait_ge(co_sum, NCO)
                            dve.tensor_reduce(csum3[:, 0:3], csum[:, :, :].rearrange("p n m -> p m n"), AXX,
                                              ALU.add).then_inc(cototal_ready, 1)
                        if b == 3:
                            dve.wait_ge(cototal_ready, 2)
                            dve.tensor_scalar(coeff[:, :], bank[0][:, 0:3], 1.0 / (INTER * DM), None, ALU.mult)\
                               .then_inc(coeff_ready, 1)
                        if b >= 1:
                            moments_of(NB + b - 1, b - 1, b - 1, cross_added, s)
                        if b >= 2:
                            layer_norm(NB + b - 2, b - 2, b - 2)
                        if 3 <= b <= 5:
                            rebuild(0, b - 3)
                        if b >= 6:
                            w13_split(0, b - 6, True)

            dve.wait_ge(qkv_ready, NB)
            for e in range(NE):
                wq_round(0, e, True)
            for b in range(NB):
                values_split(0, b, True)
            layer_norm(NB - 1, NB - 1, 0)
            for b in range(NB):
                rows_rest(b, xnT_h_ready, xnT_h, xnT_l, xnT_l_ready)
            for e in range(NE):
                wd_rest(0, e)
            mask_and_max(A_UNITS, 0, bank[1], CROSS_SCALE)
            mask_and_max(A_UNITS + 1, 1, bank[2], CROSS_SCALE)
            inverse_sums(A_UNITS, 0)
            cross_iteration(0, True, False)
            with dve.Fori(1, NG - 1) as g:
                cross_iteration(g, False, False)
            cross_iteration(NG - 1, False, True)
            layer_norm(2 * NB - 2, NB - 2, NB - 2)
            cross_add(NG - 1, 7)
            moments_of(2 * NB - 1, NB - 1, NB - 1, cross_added, 64)
            layer_norm(2 * NB - 1, NB - 1, NB - 1)

            w2_split(0, True)
            for b in range(NB):
                rows_rest(b, x2T_h_ready, x2T_h, x2T_l, x2T_l_ready)

            def hidden(p, u):
                dve.wait_ge(silu_done, 4 * p + u + 1)
                if counted(4 * p + u - 1):
                    dve.wait_ge(hT_l_ready, 4 * p + u - 1)
                dve.tensor_tensor(hf[:, u % 2, :], bank[2 + u % 2][:, :], silu[:, u % 2, :], ALU.mult)\
                   .then_inc(hf_done, 1)

            def hidden_rest(p, u):
                dve.wait_ge(hT_h_ready, 4 * p + u + 1)
                dve.tensor_tensor(hT_l[:, u // 2, u % 2, :], hf[:, u % 2, :],
                                  hT_h[:, u // 2, u % 2, :].bitcast(F32), ALU.subtract).then_inc(hT_l_ready, 1)

            def ffn_add(p, h, t):
                n, b = 8 * p + 4 * h + t, 4 * h + t
                dve.wait_ge(ffn_ready, n + 1)
                dve.wait_ge(ln_done, LN0 + 2 * NB)
                dve.tensor_tensor(xs[:, b, :], bank[4 + t][:, :], xs[:, b, :], ALU.add).then_inc(ffn_added, 1)

            def ffn_piece(p, first, last):
                for u in range(4):
                    hidden(p, u)
                    hidden_rest(p, u)
                    if u == 1 and not first:
                        for t in range(4):
                            ffn_add(p - 1, 1, t)
                        w2_split(p, False)
                    if not last:
                        if u < 3:
                            rebuild(p + 1, u)
                        if u >= 2:
                            w13_split(p + 1, u - 2, False)
                for t in range(4):
                    ffn_add(p, 0, t)

            ffn_piece(0, True, False)
            with dve.Fori(1, NP - 1) as p:
                ffn_piece(p, False, False)
            ffn_piece(NP - 1, False, True)
            for h in range(2):
                n = 2 * NB + 4 * h
                for t in range(4):
                    if h:
                        ffn_add(NP - 1, 1, t)
                    b = 4 * h + t
                    dve.wait_ge(ffn_added, 8 * NP - 8 + b + 1)
                    dve.bn_stats(stats[:, b, :], xs[:, b, :]).then_inc(stats_done, 1)
                for t in range(4):
                    dve.wait_ge(stats_done, n + t + 1)
                    dve.bn_aggr(moments[:, 4 * h + t, :], stats[:, 4 * h + t, :]).then_inc(moments_done, 1)
                dve.wait_ge(moments_done, n + 4)
                dve.tensor_scalar(varep[:, 4 * h:4 * h + 4], moments[:, 4 * h:4 * h + 4, 1], EPS, None, ALU.add)\
                   .then_inc(varep_done, 1)
                dve.wait_ge(rstd_ready, 2 * NB + h + 1)
                for b in range(4 * h, 4 * h + 4):
                    dve.tensor_scalar(xs[:, b, :], xs[:, b, :], moments[:, b, 0:1], rstd[:, b:b + 1],
                                      ALU.subtract, ALU.mult).then_inc(ln_done, 1)


def constants():
    c = np.zeros((P, C_ALL), np.float32)
    r = np.arange(P)
    c[:, C_ID:C_ID + P] = np.eye(P)
    c[:, C_MASK:C_MASK + P] = np.where(r[None, :] <= r[:, None], 0.0, NEG)
    c[:, C_BM:C_BM + 8] = (r[:, None] // HD) == np.arange(8)[None, :]
    freq = (1.0 / np.float32(10000.0) ** (np.arange(0, HD, 2, dtype=np.float32) / np.float32(HD))).astype(np.float32)
    angle = r.astype(np.float32)[:, None] * freq[None, :]
    cos, sin = np.cos(angle), np.sin(angle)
    c[:, C_COS:C_COS + HD] = np.concatenate([cos, cos], 1)
    c[:, C_SIN:C_SIN + HD] = np.concatenate([-sin, sin], 1)
    second = (r // HD) % 2
    c[:, C_HALF] = second
    c[:, C_HALF + 1] = 1 - 2 * second
    c[:, C_EPS] = EPS
    c[:, C_POW] = -0.5
    c[:, C_ONE:C_ONE + P] = 1.0
    return c


def kernel(x, ctx_4096, L0_attn_w_qkv, L0_attn_w_o, L0_xattn_Wq, L0_xattn_Wk, L0_xattn_Wv, L0_xattn_Wd,
           L0_ffn_w1, L0_ffn_mean_w1, L0_ffn_w2, L0_ffn_mean_w2, L0_ffn_w3, L0_ffn_mean_w3):
    import concourse.bacc as bacc
    from concourse.bass_utils import run_bass_kernel_spmd

    def arr(a):
        return np.asarray(a)

    x, c4 = arr(x), arr(ctx_4096)
    turn = np.concatenate([np.arange(0, HD, 2), np.arange(1, HD, 2)])
    cols = np.concatenate([(np.arange(40)[:, None] * HD + turn[None, :]).ravel(), np.arange(640, QKV)])
    wqkv = arr(L0_attn_w_qkv)[:, cols]

    def w13(w):
        return arr(w).reshape(NP, PIECE, KT, P).transpose(0, 3, 2, 1).reshape(NP, P, 1024)

    def w2(w):
        return arr(w).T.reshape(NP, 2, P, DM).transpose(0, 2, 1, 3).reshape(NP, P, 1024)

    wo = arr(L0_attn_w_o).reshape(2, 4, NE, 1, HD, DM)
    wo = np.concatenate([wo, wo], 3).transpose(1, 3, 4, 0, 2, 5)
    arrays = {
        "consts": constants(),
        "x": x,
        "xT": x.reshape(NB, P, KT, P).transpose(0, 3, 2, 1),
        "ctxT": c4.reshape(2, 512, KT, P).transpose(0, 3, 2, 1),
        "wkv": np.concatenate([arr(L0_xattn_Wk).T.reshape(KT, P, 1024), arr(L0_xattn_Wv).T.reshape(KT, P, 1024)]),
        "wqkv": wqkv.reshape(KT, P, QKV).transpose(1, 0, 2),
        "wo": wo.reshape(P, 2 * NE, DM),
        "wq": arr(L0_xattn_Wq).reshape(NG * NE, P, KT, P).transpose(0, 3, 2, 1).reshape(NG * NE, P, 512),
        "wd": arr(L0_xattn_Wd).T.reshape(NG * NE, P, DM),
        "fw": np.stack([w13(L0_ffn_w1), w13(L0_ffn_w3), w2(L0_ffn_w2)], 2),
        "fm": np.stack([w13(L0_ffn_mean_w1), w13(L0_ffn_mean_w3), w2(L0_ffn_mean_w2)], 2),
    }
    arrays = {n + "_dram": np.ascontiguousarray(a) for n, a in arrays.items()}
    nc = bacc.Bacc("TRN2", target_bir_lowering=False, num_devices=1)
    args = [nc.dram_tensor(n, a.shape, mybir.dt.from_np(a.dtype), kind="ExternalInput").ap()
            for n, a in arrays.items()]
    out = nc.dram_tensor("out", (NB, P, DM), F32, kind="ExternalOutput").ap()
    decoder_layer(nc, *args, out)
    r = run_bass_kernel_spmd(nc, [arrays], core_ids=[0])
    return r.results[0]["out"]
```

```python
from contextlib import ExitStack

import numpy as np

import concourse.bass as bass
from concourse import mybir

F32 = mybir.dt.float32
F32R = mybir.dt.float32r
ALU = mybir.AluOpType
ACT = mybir.ActivationFunctionType
AXX = mybir.AxisListType.X

P = 128
NB = 8
DM = 512
KT = DM // P
NG = 8
NE = 4
HD = 16
QKV = 768
INTER = 1792
PIECE = 256
NP = INTER // PIECE
NCO = NP * NB
COW = 1024 // NB
SELF_SCALE = 0.25
CROSS_SCALE = float(P) ** -0.5
NEG = -3.0e38
EPS = 1e-5

C_ID, C_MASK, C_BM, C_COS, C_SIN, C_HALF, C_EPS, C_POW, C_ONE = 0, 128, 256, 264, 280, 296, 298, 299, 300
C_ALL = 428


def counted(value):
    return not (isinstance(value, int) and value <= 0)


def bcast(ap, n, inner):
    if inner:
        a = ap.rearrange("p (a b) -> p a b", b=1)
        return a.to_broadcast([a.shape[0], a.shape[1], n])
    a = ap.rearrange("p (b a) -> p b a", b=1)
    return a.to_broadcast([a.shape[0], n, a.shape[2]])


def decoder_layer(nc, consts_d, x_d, xT_d, ctxT_d, wkv_d, wqkv_d, wo_d, wq_d, wd_d, fw_d, fm_d, out_d):
    with ExitStack() as ctx:
        def sb(name, shape, dt=F32, stack=ctx):
            return stack.enter_context(nc.sbuf_tensor(name, shape, dt))

        consts = sb("consts", [P, C_ALL])
        ident = consts[:, C_ID:C_ID + P]
        cmask = consts[:, C_MASK:C_MASK + P]
        bmask = consts[:, C_BM:C_BM + 8]
        rcos = consts[:, C_COS:C_COS + HD]
        rsin = consts[:, C_SIN:C_SIN + HD]
        half = consts[:, C_HALF:C_HALF + 2]
        cpow = consts[:, C_POW:C_POW + 1]
        ones = consts[:, C_ONE:C_ONE + P]
        xs = sb("xs", [P, NB, DM])
        csum = sb("csum", [P, NCO, 3])
        csum3 = sb("csum3", [P, 4])
        coeff = sb("coeff", [P, 3])
        stats = sb("stats", [P, NB, 6])
        moments = sb("moments", [P, NB, 2])
        varep = sb("varep", [P, NB])
        rstd = sb("rstd", [P, NB])
        shift = sb("shift", [P, NB])
        rmax = sb("rmax", [P, 4, NE])
        nbias = sb("nbias", [P, 4, NE])
        rsum = sb("rsum", [P, 4, NE])
        rinv = sb("rinv", [P, 4, NE])
        gate_mark = sb("gate_mark", [P, 1])
        co_mark = sb("co_mark", [P, 1])
        prob = sb("prob", [P, 4, NE, P])

        with ExitStack() as r_kv:
            kT = sb("kT", [P, NG, NB * P], F32, r_kv)
            vv = sb("vv", [P, NB, NG * P], F32, r_kv)
            with ExitStack() as r1:
                wk_h = sb("wk_h", [P, KT, 1024], F32R, r1)
                wk_l = sb("wk_l", [P, KT, 1024], F32R, r1)
            with ExitStack() as r1:
                wqkv_h = sb("wqkv_h", [P, KT, QKV], F32R, r1)
                wqkv_l = sb("wqkv_l", [P, KT, QKV], F32R, r1)
                wqkv_r = sb("wqkv_r", [P, 2, QKV], F32, r1)
                qT = sb("qT", [P, NE, P], F32, r1)
                v_tok = sb("v_tok", [P, P], F32, r1)
                v_two = sb("v_two", [P, NG, 2, HD], F32, r1)
            with ExitStack() as r1:
                wq_h = sb("wq_h", [P, NE, KT, P], F32R, r1)
                wq_l = sb("wq_l", [P, NE, KT, P], F32R, r1)
                wq_r = sb("wq_r", [P, 2, KT * P], F32, r1)
                vg_h = sb("vg_h", [P, NB, P], F32R, r1)
                vg_l = sb("vg_l", [P, NB, P], F32R, r1)
                wd_r = sb("wd_r", [P, NE, DM], F32, r1)
            sb("region1", [P, 9216], F32, r_kv)
            with ExitStack() as r2:
                wv_h = sb("wv_h", [P, KT, 1024], F32R, r2)
                wv_l = sb("wv_l", [P, KT, 1024], F32R, r2)
                cT_h1 = sb("cT_h1", [P, KT, DM], F32R, r2)
                cT_l1 = sb("cT_l1", [P, KT, DM], F32R, r2)
                wkv_r = sb("wkv_r", [P, 2, 1024], F32, r2)
                cT_r = sb("cT_r", [P, KT, DM], F32, r2)
                cT_h0 = sb("cT_h0", [P, KT, DM], F32R, r2)
                cT_l0 = sb("cT_l0", [P, KT, DM], F32R, r2)
                cT_h, cT_l = (cT_h0, cT_h1), (cT_l0, cT_l1)
            with ExitStack() as r2:
                wo_s = sb("wo_s", [P, 2 * NE, DM], F32R, r2)
                pT = sb("pT", [P, NE, DM], F32, r2)
                oT_h = sb("oT_h", [P, NE, P], F32R, r2)
                oT_l = sb("oT_l", [P, NE, P], F32R, r2)
                wo_r = sb("wo_r", [P, 2, DM], F32, r2)
                wo_h = sb("wo_h", [P, DM], F32R, r2)
                wo_t = sb("wo_t", [P, DM], F32, r2)
                res = sb("res", [P, DM], F32, r2)
                sb("a_gap", [P, 2560], F32, r2)
                bd = sb("bd", [P, NE, 8, P], F32, r2)
                xT_r = sb("xT_r", [P, KT, P], F32, r2)
                xT_h = sb("xT_h", [P, KT, P], F32R, r2)
                xT_l = sb("xT_l", [P, KT, P], F32R, r2)
                rope1 = sb("rope1", [P, 640], F32, r2)
                rope2 = sb("rope2", [P, 640], F32, r2)
                q_tok = sb("q_tok", [P, DM], F32, r2)
                k_rep = sb("k_rep", [P, DM], F32, r2)
            with ExitStack() as r2:
                xnT_h1 = sb("xnT_h1", [P, KT, DM], F32R, r2)
                xnT_l1 = sb("xnT_l1", [P, KT, DM], F32R, r2)
                pT_h = sb("pT_h", [P, DM], F32R, r2)
                pT_l = sb("pT_l", [P, DM], F32R, r2)
                aT_h = sb("aT_h", [P, 2, DM], F32R, r2)
                aT_l = sb("aT_l", [P, 2, DM], F32R, r2)
                wd_h = sb("wd_h", [P, NE, DM], F32R, r2)
                cm = sb("cm", [P, 3, COW], F32, r2)
                sb("c_gap1", [P, 128], F32, r2)
                xnT_h0 = sb("xnT_h0", [P, KT, DM], F32R, r2)
                cw = sb("cw", [P, 3, COW], F32, r2)
                sb("c_gap2", [P, 128], F32, r2)
                qc = sb("qc", [P, NE, NB * P], F32, r2)
                xnT_l0 = sb("xnT_l0", [P, KT, DM], F32R, r2)
                wd_l = sb("wd_l", [P, NE, DM], F32R, r2)
                xnT_h, xnT_l = (xnT_h0, xnT_h1), (xnT_l0, xnT_l1)
        with ExitStack() as r_ffn:
            x2T_h = sb("x2T_h", [P, KT, NB * P], F32R, r_ffn)
            x2T_l = sb("x2T_l", [P, KT, NB * P], F32R, r_ffn)
            fw = sb("fw", [P, 3, 1024], F32, r_ffn)
            fm = sb("fm", [P, 3, 1024], F32, r_ffn)
            fd = sb("fd", [P, 2, 1024], F32, r_ffn)
            wf = sb("wf", [P, 3, 1024], F32, r_ffn)
            w13_h = sb("w13_h", [P, 2, KT, PIECE], F32R, r_ffn)
            w2_h = sb("w2_h", [P, 2, DM], F32R, r_ffn)
            w2_l = sb("w2_l", [P, 2, DM], F32R, r_ffn)
            w13_l = sb("w13_l", [P, 2, KT, PIECE], F32R, r_ffn)
            silu = sb("silu", [P, 2, DM], F32, r_ffn)
            hf = sb("hf", [P, 2, DM], F32, r_ffn)
            hT_h = sb("hT_h", [P, 2, 2, DM], F32R, r_ffn)
            hT_l = sb("hT_l", [P, 2, 2, DM], F32R, r_ffn)
        bank = [ctx.enter_context(nc.psum_tensor(f"bank{i}", [P, 512], F32)) for i in range(8)]

        def sem(name):
            return ctx.enter_context(nc.semaphore(name))

        consts_in = sem("consts_in")
        wkv_in = [sem(f"wkv_in{i}") for i in range(2)]
        ctx_in = [sem(f"ctx_in{k}") for k in range(KT)]
        wkv_h_ready, wkv_l_ready = sem("wkv_h_ready"), sem("wkv_l_ready")
        ctx_h_ready, ctx_l_ready = sem("ctx_h_ready"), sem("ctx_l_ready")
        kv_ready, k_copied, v_copied = sem("kv_ready"), sem("k_copied"), sem("v_copied")
        wqkv_in = [sem(f"wqkv_in{i}") for i in range(2)]
        wqkv_h_ready, wqkv_l_ready = sem("wqkv_h_ready"), sem("wqkv_l_ready")
        wo_in = [sem(f"wo_in{i}") for i in range(2)]
        wo_h_ready, wo_t_ready, wo_ready = sem("wo_h_ready"), sem("wo_t_ready"), sem("wo_ready")
        x_in, res_in = sem("x_in"), sem("res_in")
        co_in, co_sub, co_sum = sem("co_in"), sem("co_sub"), sem("co_sum")
        cototal_ready, coeff_ready = sem("cototal_ready"), sem("coeff_ready")
        x_h_ready, x_l_ready, qkv_ready = sem("x_h_ready"), sem("x_l_ready"), sem("qkv_ready")
        rope_ready, qk_ready, blkT_ready = sem("rope_ready"), sem("qk_ready"), sem("blkT_ready")
        k_rep_ready = sem("k_rep_ready")
        qT_ready, bd_ready, v_two_ready = sem("qT_ready"), sem("bd_ready"), sem("v_two_ready")
        scores_ready, masked, nbias_ready = sem("scores_ready"), sem("masked"), sem("nbias_ready")
        exp_done, rinv_ready, norm_done = sem("exp_done"), sem("rinv_ready"), sem("norm_done")
        pT_ready, pT_copied = sem("pT_ready"), sem("pT_copied")
        pv_ready, oT_h_ready, oT_l_ready = sem("pv_ready"), sem("oT_h_ready"), sem("oT_l_ready")
        oT_used, oproj_ready, y_done = sem("oT_used"), sem("oproj_ready"), sem("y_done")
        stats_done, moments_done, varep_done = sem("stats_done"), sem("moments_done"), sem("varep_done")
        rstd_ready, ln_done = sem("rstd_ready"), sem("ln_done")
        shift_ready = sem("shift_ready")

        xnT_turned, xnT_h_ready, xnT_l_ready = sem("xnT_turned"), sem("xnT_h_ready"), sem("xnT_l_ready")
        wq_in, wd_in = [sem(f"wq_in{i}") for i in range(2)], [sem(f"wd_in{i}") for i in range(NE)]
        wq_h_ready, wq_l_ready = sem("wq_h_ready"), sem("wq_l_ready")
        wd_h_ready, wd_l_ready, wd_used = sem("wd_h_ready"), sem("wd_l_ready"), sem("wd_used")
        vg_h_ready, vg_ready = sem("vg_h_ready"), sem("vg_ready")
        q_ready, q_copied = sem("q_ready"), sem("q_copied")
        pT_h_ready, pT_l_ready = sem("pT_h_ready"), sem("pT_l_ready")
        cross_pv, aT_h_ready, aT_l_ready = sem("cross_pv"), sem("aT_h_ready"), sem("aT_l_ready")
        cross_y, cross_added = sem("cross_y"), sem("cross_added")
        x2T_turned, x2T_h_ready, x2T_l_ready = sem("x2T_turned"), sem("x2T_h_ready"), sem("x2T_l_ready")
        f_in = [sem(f"f_in{m}") for m in range(3)]
        fd_ready, sign_ready, wf_ready = sem("fd_ready"), sem("sign_ready"), sem("wf_ready")
        w13_h_ready, w13_l_ready = sem("w13_h_ready"), sem("w13_l_ready")
        w2_h_ready, w2_l_ready = sem("w2_h_ready"), sem("w2_l_ready")
        gu_ready, silu_done, hf_done = sem("gu_ready"), sem("silu_done"), sem("hf_done")
        hT_h_ready, hT_l_ready = sem("hT_h_ready"), sem("hT_l_ready")
        ffn_ready, ffn_added, out_done = sem("ffn_ready"), sem("ffn_added"), sem("out_done")

        XN_BANK = (0, 1, 0, 1, 3, 4, 5, 6)
        X2_BANK = (0, 1, 0, 1, 4, 5, 6, 7)

        def half_rows(halves, b):
            return halves[b // 4][:, :, bass.ts(b % 4, P)]

        def slot_of(b, g):
            return b * 8 + g

        LN0 = 1
        A_UNITS = NB * NG

        block = ctx.enter_context(nc.Block())

        @block.sync
        def _(sp):
            for c in range(8):
                if c >= 2:
                    sp.wait_ge(wkv_l_ready, c - 1)
                sp.dma_start(wkv_r[:, c % 2, :], wkv_d[c]).then_inc(wkv_in[c % 2], 16)
                if c < KT:
                    sp.dma_start(cT_r[:, c, :], ctxT_d[0, :, c, :]).then_inc(ctx_in[c], 16)
            sp.dma_start(consts[:, :], consts_d).then_inc(consts_in, 16)
            for k in range(KT):
                sp.wait_ge(ctx_l_ready, k + 1)
                sp.dma_start(cT_r[:, k, :], ctxT_d[1, :, k, :]).then_inc(ctx_in[k], 16)
            sp.wait_ge(kv_ready, 16)
            sp.dma_start(xT_r[:, :, :], xT_d[0]).then_inc(x_in, 16)
            sp.wait_ge(kv_ready, 24)
            for k in range(KT):
                if k >= 2:
                    sp.wait_ge(wqkv_l_ready, k - 1)
                sp.dma_start(wqkv_r[:, k % 2, :], wqkv_d[:, k, :]).then_inc(wqkv_in[k % 2], 16)

            def wo_load(c):
                if c >= 2:
                    sp.wait_ge(wo_ready, c - 1)
                sp.dma_start(wo_r[:, c % 2, :], wo_d[:, c, :]).then_inc(wo_in[c % 2], 16)

            def x_load(b):
                sp.wait_ge(x_l_ready, b)
                sp.dma_start(xT_r[:, :, :], xT_d[b]).then_inc(x_in, 16)

            def res_load(b):
                sp.wait_ge(y_done, b)
                sp.dma_start(res[:, :], x_d[b]).then_inc(res_in, 16)

            x_load(1)
            sp.wait_ge(kv_ready, 32)
            sp.dma_start(res[:, :], x_d[0]).then_inc(res_in, 16)
            wo_load(0)
            wo_load(1)
            wo_load(2)
            x_load(2)
            for c in range(3, 2 * NE):
                wo_load(c)
            res_load(1)
            with sp.Fori(3, NB) as b:
                x_load(b)
                res_load(b - 1)

            def wq_load(g, e):
                if counted(4 * g + e - 1):
                    sp.wait_ge(wq_l_ready, 4 * g + e - 1)
                sp.dma_start(wq_r[:, e % 2, :], wq_d[g * NE + e]).then_inc(wq_in[e % 2], 16)

            def wd_load(g, e):
                if counted(4 * (g - 1) + e + 1):
                    sp.wait_ge(wd_l_ready, 4 * (g - 1) + e + 1)
                sp.dma_start(wd_r[:, e, :], wd_d[g * NE + e]).then_inc(wd_in[e], 16)

            sp.wait_ge(qkv_ready, NB)
            wq_load(0, 0)
            wq_load(0, 1)
            res_load(NB - 1)
            wq_load(0, 2)
            wq_load(0, 3)
            sp.wait_ge(pv_ready, 2 * NB)
            for e in range(NE):
                wd_load(0, e)

            def co_load(g, b):
                n = 8 * g + b
                if counted(n):
                    sp.wait_ge(co_sum, n)
                sp.dma_start(cw[:, :, :], fw_d[g][:, :, bass.ts(b, COW)]).then_inc(co_in, 16)
                sp.dma_start(cm[:, :, :], fm_d[g][:, :, bass.ts(b, COW)]).then_inc(co_in, 16)

            def cross_loads(g):
                for b in range(NB):
                    if b < NE:
                        wq_load(g + 1, b)
                    co_load(g, b)
                    if b == 1:
                        for e in range(NE):
                            wd_load(g + 1, e)

            sp.wait_ge(y_done, NB)
            cross_loads(0)
            with sp.Fori(1, NG - 1) as g:
                cross_loads(g)

            def f_load(p):
                for m in range(3):
                    if counted(p):
                        sp.wait_ge(wf_ready, 3 * p - 2 + m)
                    sp.dma_start(fw[:, m, :], fw_d[p][:, m, :]).then_inc(f_in[m], 16)
                    sp.dma_start(fm[:, m, :], fm_d[p][:, m, :]).then_inc(f_in[m], 16)

            sp.wait_ge(vg_ready, 8 * NG)
            f_load(0)
            with sp.Fori(1, NP) as p:
                f_load(p)
            for b in range(NB):
                sp.wait_ge(ln_done, LN0 + 2 * NB + b + 1)
                sp.dma_start(out_d[b], xs[:, b, :]).then_inc(out_done, 16)
            sp.wait_ge(out_done, 16 * NB)

        @block.tensor
        def _(pe):
            def split_product(out, lh, ll, rh, rl, first, last):
                pe.matmul(out, lh, rh, start=first, stop=False)
                pe.matmul(out, lh, rl, start=False, stop=False)
                return pe.matmul(out, ll, rh, start=False, stop=last)

            for k in range(KT):
                pe.wait_ge(wkv_h_ready, k + 1)
                pe.wait_ge(wkv_l_ready, k + 1)
                pe.wait_ge(ctx_h_ready, k + 1)
                pe.wait_ge(ctx_l_ready, k + 1)
                for i in range(8):
                    cols = bass.ts(i, P)
                    mm = split_product(bank[i][:, :], wk_h[:, k, cols], wk_l[:, k, cols],
                                       cT_h[0][:, k, :], cT_l[0][:, k, :], k == 0, k == KT - 1)
                    if k == KT - 1:
                        mm.then_inc(kv_ready, 1)

            def key_tile(i):
                pe.wait_ge(v_copied, i + 1)
                cols = bass.ts(i, P)
                for k in range(KT):
                    mm = split_product(bank[i][:, :], wk_h[:, k, cols], wk_l[:, k, cols],
                                       cT_h[1][:, k, :], cT_l[1][:, k, :], k == 0, k == KT - 1)
                mm.then_inc(kv_ready, 1)

            def value_tile(h, i):
                pe.wait_ge(k_copied, 8 * h + i + 1)
                tok, cols = bass.ts(i // 2, P), bass.ts(i % 2, 512)
                for k in range(KT):
                    if h == 0 and i == 0:
                        pe.wait_ge(wkv_h_ready, KT + k + 1)
                        pe.wait_ge(wkv_l_ready, KT + k + 1)
                    mm = split_product(bank[i][:, :], cT_h[h][:, k, tok], cT_l[h][:, k, tok],
                                       wv_h[:, k, cols], wv_l[:, k, cols], k == 0, k == KT - 1)
                mm.then_inc(kv_ready, 1)

            for i in range(8):
                value_tile(0, i)
            pe.wait_ge(ctx_h_ready, 8)
            pe.wait_ge(ctx_l_ready, 8)
            for i in range(8):
                key_tile(i)
            for i in range(5):
                value_tile(1, i)

            def turn_rows(b, i, lns, ready):
                pe.wait_ge(ln_done, LN0 + lns)
                for k in range(KT):
                    mm = pe.transpose(bank[i][:, bass.ts(k, P)], xs[:, b, bass.ts(k, P)], ident)
                mm.then_inc(ready, 1)

            def q_tile(g, r):
                n, h, e = 8 * g + r, r // 4, r % 4
                pe.wait_ge(q_copied, n)
                pe.wait_ge(wq_l_ready, 4 * g + e + 1)
                for k in range(KT):
                    mm = split_product(bank[0][:, :], wq_h[:, e, k, :], wq_l[:, e, k, :], xnT_h[h][:, k, :],
                                       xnT_l[h][:, k, :], k == 0, k == KT - 1)
                mm.then_inc(q_ready, 1)

            def early_rows(b):
                if b == 0:
                    pe.wait_ge(qT_ready, 4 * NB)
                    pe.wait_ge(bd_ready, 4 * NB)
                if b >= 2:
                    pe.wait_ge(xnT_l_ready, b - 1)
                turn_rows(b, XN_BANK[b], b + 1, xnT_turned)

            def early_q_tile(r):
                if r == 0:
                    pe.wait_ge(xnT_h_ready, 4)
                    pe.wait_ge(xnT_l_ready, 4)
                if r >= 2:
                    pe.wait_ge(q_copied, r - 1)
                pe.wait_ge(wq_l_ready, r + 1)
                for k in range(KT):
                    mm = split_product(bank[r % 2][:, :], wq_h[:, r, k, :], wq_l[:, r, k, :], xnT_h[0][:, k, :],
                                       xnT_l[0][:, k, :], k == 0, k == KT - 1)
                mm.then_inc(q_ready, 1)

            def project_qkv(b, lo, hi):
                for n in range(lo, hi):
                    k = n % KT
                    if n == 0:
                        pe.wait_ge(x_h_ready, b + 1)
                        pe.wait_ge(x_l_ready, b + 1)
                        if counted(4 * b):
                            pe.wait_ge(qT_ready, 4 * b - 1)
                            pe.wait_ge(bd_ready, 4 * b - 1)
                    if n == KT and counted(4 * b):
                        pe.wait_ge(qT_ready, 4 * b)
                        pe.wait_ge(bd_ready, 4 * b)
                    out, cols = (bank[0][:, 0:512], slice(0, 512)) if n < KT else (bank[1][:, 0:256], slice(512, QKV))
                    mm = split_product(out, xT_h[:, k, :], xT_l[:, k, :], wqkv_h[:, k, cols],
                                       wqkv_l[:, k, cols], k == 0, k == KT - 1)
                if hi == 2 * KT:
                    mm.then_inc(qkv_ready, 1)

            def turn_block(b, j):
                pe.wait_ge(qk_ready, b + 1)
                pe.wait_ge(k_rep_ready, b + 1)
                if counted(4 * b + j - 1):
                    pe.wait_ge(qT_ready, 4 * b + j - 1)
                if counted(4 * b + j - 1):
                    pe.wait_ge(bd_ready, 4 * b + j - 1)
                pe.transpose(bank[j % 2][:, 0:P], q_tok[:, bass.ts(j, P)], ident)
                pe.transpose(bank[j % 2][:, P:2 * P], k_rep[:, bass.ts(j, P)], ident).then_inc(blkT_ready, 1)

            def self_scores(b, g):
                s, j = slot_of(b, g), g // 2
                pe.wait_ge(qT_ready, 4 * b + j + 1)
                pe.wait_ge(bd_ready, 4 * b + j + 1)
                if counted(s - 1):
                    pe.wait_ge(masked, s - 1)
                pe.matmul(bank[2 + g % 2][:, :], qT[:, j, :],
                          bd[:, j, bass.ts(g % 2, NE), :], start=True, stop=True).then_inc(scores_ready, 1)

            def turn_probs(s, g):
                pe.wait_ge(norm_done, s + 1)
                if counted(s - 1):
                    pe.wait_ge(pT_copied, s - 1)
                for e in range(NE):
                    mm = pe.transpose(bank[4 + g % 2][:, bass.ts(e, P)], prob[:, g % 4, e, :], ident)
                mm.then_inc(pT_ready, 1)

            def self_values(b, q):
                pe.wait_ge(pT_copied, 8 * b + 4 * q + 4)
                pe.wait_ge(v_two_ready, b + 1)
                if counted(2 * b + q):
                    pe.wait_ge(oT_l_ready, 2 * b + q)
                for j in range(4):
                    mm = pe.matmul(bank[6][32 * j:32 * j + 32, :],
                                   v_two[:, 4 * q + j, :, :].rearrange("p a d -> p (a d)"),
                                   pT[:, j, :], start=True, stop=True)
                mm.then_inc(pv_ready, 1)

            def self_out(b, q):
                pe.wait_ge(oT_l_ready, 2 * b + q + 1)
                pe.wait_ge(wo_ready, 4 * q + 4)
                if q == 0 and counted(b):
                    pe.wait_ge(y_done, b)
                for e in range(NE):
                    pe.matmul(bank[7][:, :], oT_h[:, e, :], wo_s[:, 4 * q + e, :],
                              start=(q == 0 and e == 0), stop=False)
                    mm = pe.matmul(bank[7][:, :], oT_l[:, e, :], wo_s[:, 4 * q + e, :],
                                   start=False, stop=(q == 1 and e == NE - 1))
                mm.then_inc(oT_used, 1)

            def self_iteration(b, first, last):
                for g in range(8):
                    s = slot_of(b, g)
                    if g < 6:
                        self_scores(b, g + 2)
                    elif not last:
                        self_scores(b + 1, g - 6)
                    if g == 0 and not first:
                        self_values(b - 1, 1)
                    if g == 4:
                        self_values(b, 0)
                    if not last:
                        if g == 2:
                            project_qkv(b + 1, 0, 2)
                        if g == 4:
                            turn_block(b + 1, 0)
                        if g == 5:
                            turn_block(b + 1, 1)
                        if g == 6:
                            turn_block(b + 1, 2)
                    if g == 1 and not first:
                        self_out(b - 1, 1)
                    turn_probs(s, g)
                    if g == 5:
                        self_out(b, 0)
                    if not last:
                        if g == 2:
                            project_qkv(b + 1, 2, 8)
                    if g == 0 and not first:
                        turn_block(b, 3)
                    if last and 2 <= g <= 5:
                        early_rows(g - 2)
                    if last and g >= 6:
                        early_q_tile(g - 6)

            pe.wait_ge(wqkv_h_ready, KT)
            pe.wait_ge(wqkv_l_ready, KT)
            pe.wait_ge(v_copied, 8 + 2)
            project_qkv(0, 0, 8)
            value_tile(1, 5)
            value_tile(1, 6)
            pe.wait_ge(consts_in, 16)
            turn_block(0, 0)
            turn_block(0, 1)
            value_tile(1, 7)
            self_scores(0, 0)
            self_scores(0, 1)
            turn_block(0, 2)
            turn_block(0, 3)
            pe.wait_ge(v_copied, 16)
            self_iteration(0, True, False)
            with pe.Fori(1, NB - 1) as b:
                self_iteration(b, False, False)
            self_iteration(NB - 1, False, True)
            self_values(NB - 1, 1)
            early_q_tile(2)
            self_out(NB - 1, 1)
            early_q_tile(3)

            def cross_scores(g, b):
                s = 8 * g + b
                pe.wait_ge(q_copied, 8 * g + (4 if b < 4 else 8))
                pe.wait_ge(masked, A_UNITS + s - 1)
                for e in range(NE):
                    mm = pe.matmul(bank[1 + b % 2][:, bass.ts(e, P)], qc[:, e, bass.ts(b, P)],
                                   kT[:, g, bass.ts(b, P)], start=(e == 0), stop=(e == NE - 1),
                                   skip_group_check=True)
                mm.then_inc(scores_ready, 1)

            def cross_turn(s, b):
                pe.wait_ge(norm_done, A_UNITS + s + 1)
                if counted(s - 1):
                    pe.wait_ge(pT_l_ready, s - 1)
                for e in range(NE):
                    mm = pe.transpose(bank[3 + b % 2][:, bass.ts(e, P)], prob[:, b % 4, e, :], ident)
                mm.then_inc(pT_ready, 1)

            def cross_values(s, b):
                pe.wait_ge(pT_l_ready, s + 1)
                pe.wait_ge(vg_ready, s + 1)
                if counted(s):
                    pe.wait_ge(aT_l_ready, s)
                split_product(bank[5][:, :], vg_h[:, b, :], vg_l[:, b, :], pT_h[:, :], pT_l[:, :], True, True)\
                    .then_inc(cross_pv, 1)

            def cross_out(g, b):
                s = 8 * g + b
                pe.wait_ge(aT_l_ready, s + 1)
                if counted(s - 1):
                    pe.wait_ge(cross_added, s - 1)
                for e in range(NE):
                    if b == 0:
                        pe.wait_ge(wd_l_ready, 4 * g + e + 1)
                    mm = split_product(bank[6 + b % 2][:, :], aT_h[:, b % 2, bass.ts(e, P)],
                                       aT_l[:, b % 2, bass.ts(e, P)], wd_h[:, e, :], wd_l[:, e, :],
                                       e == 0, e == NE - 1)
                    if b == 7 and e < NE - 1:
                        mm.then_inc(wd_used, 1)
                mm.then_inc(cross_y, 1)

            def cross_iteration(g, first, last):
                for b in range(NB):
                    s = 8 * g + b
                    cross_turn(s, b)
                    if last and b == 2:
                        pe.wait_ge(cototal_ready, 1)
                        pe.wait_ge(q_copied, 8 * NG)
                        pe.matmul(bank[0][:, 0:4], ones, csum3[:, 0:4], start=True, stop=True)\
                            .then_inc(cototal_ready, 1)
                    if b > 0:
                        cross_out(g, b - 1)
                    elif not first:
                        cross_out(g - 1, 7)
                    cross_values(s, b)
                    if b < 6:
                        cross_scores(g, b + 2)
                    elif not last:
                        cross_scores(g + 1, b - 6)
                    if b < 2:
                        q_tile(g, 6 + b)
                    elif not last:
                        q_tile(g + 1, b - 2)
                    if last and b >= 6:
                        for i in (2 * (b - 6), 2 * (b - 6) + 1):
                            if i == 0:
                                pe.wait_ge(coeff_ready, 1)
                            elif i == 1:
                                pe.wait_ge(masked, A_UNITS + 63)
                            else:
                                pe.wait_ge(x2T_l_ready, i - 1)
                            turn_rows(i, X2_BANK[i], NB + i + 1, x2T_turned)

            pe.wait_ge(masked, A_UNITS)
            pe.wait_ge(pT_copied, A_UNITS)
            for b in range(4, 7):
                turn_rows(b, XN_BANK[b], b + 1, xnT_turned)
            cross_scores(0, 0)
            cross_scores(0, 1)
            pe.wait_ge(oT_l_ready, 2 * NB)
            pe.wait_ge(y_done, NB)
            turn_rows(7, XN_BANK[7], NB, xnT_turned)
            pe.wait_ge(xnT_h_ready, NB)
            pe.wait_ge(xnT_l_ready, NB)
            q_tile(0, 4)
            q_tile(0, 5)
            cross_iteration(0, True, False)
            with pe.Fori(1, NG - 1) as g:
                cross_iteration(g, False, False)
            cross_iteration(NG - 1, False, True)
            cross_out(NG - 1, 7)

            pe.wait_ge(pT_l_ready, 64)
            turn_rows(4, X2_BANK[4], NB + 5, x2T_turned)
            pe.wait_ge(aT_l_ready, 64)
            turn_rows(5, X2_BANK[5], NB + 6, x2T_turned)

            def gate_up(p, h, c):
                u = 2 * h + c
                pe.wait_ge(w13_l_ready, 2 * p + c + 1)
                if counted(4 * p + u - 1):
                    pe.wait_ge(silu_done, 4 * p + u - 1)
                if counted(4 * p + u - 1):
                    pe.wait_ge(hf_done, 4 * p + u - 1)
                for m in range(2):
                    for k in range(KT):
                        i, tok = bass.ts(c, P), bass.ts(h, 512)
                        mm = split_product(bank[2 * m + u % 2][:, :], w13_h[:, m, k, i], w13_l[:, m, k, i],
                                           x2T_h[:, k, tok], x2T_l[:, k, tok], k == 0, k == KT - 1)
                mm.then_inc(gu_ready, 1)

            def ffn_out(p, h):
                pe.wait_ge(hT_l_ready, 4 * p + 2 * h + 2)
                pe.wait_ge(w2_l_ready, p + 1)
                for t in range(4):
                    if counted(8 * p + 4 * h + t - 3):
                        pe.wait_ge(ffn_added, 8 * p + 4 * h + t - 3)
                    for c in range(2):
                        tok = bass.ts(t, P)
                        mm = split_product(bank[4 + t][:, :], hT_h[:, h, c, tok], hT_l[:, h, c, tok],
                                           w2_h[:, c, :], w2_l[:, c, :], c == 0, c == 1)
                    mm.then_inc(ffn_ready, 1)

            def ffn_piece(p, first):
                gate_up(p, 0, 0)
                if first:
                    pe.wait_ge(cross_added, 64)
                    turn_rows(6, X2_BANK[6], NB + 7, x2T_turned)
                    turn_rows(7, X2_BANK[7], NB + 8, x2T_turned)
                gate_up(p, 0, 1)
                if not first:
                    ffn_out(p - 1, 1)
                if first:
                    pe.wait_ge(x2T_h_ready, 8)
                    pe.wait_ge(x2T_l_ready, 8)
                gate_up(p, 1, 0)
                gate_up(p, 1, 1)
                ffn_out(p, 0)

            pe.wait_ge(x2T_h_ready, 4)
            pe.wait_ge(x2T_l_ready, 4)
            ffn_piece(0, True)
            with pe.Fori(1, NP) as p:
                ffn_piece(p, False)
            ffn_out(NP - 1, 1)


        @block.scalar
        def _(act):
            def wkv_round(c):
                act.wait_ge(wkv_in[c % 2], 16 * (c // 2 + 1))
                dst = wk_h if c < 4 else wv_h
                act.activation(dst[:, c % 4, :], wkv_r[:, c % 2, :], ACT.Copy).then_inc(wkv_h_ready, 1)

            def ctx_round(h, k):
                act.wait_ge(ctx_in[k], 16 * (h + 1))
                act.activation(cT_h[h][:, k, :], cT_r[:, k, :], ACT.Copy).then_inc(ctx_h_ready, 1)

            def key_out(h, i):
                act.wait_ge(kv_ready, 16 * h + i + 1)
                act.activation(kT[:, i, bass.ts(h, 512)], bank[i][:, :], ACT.Copy).then_inc(k_copied, 1)

            for k in range(KT):
                wkv_round(k)
                ctx_round(0, k)
            for c in range(KT, 2 * KT):
                wkv_round(c)
            for i in range(8):
                key_out(0, i)
            for k in range(KT):
                ctx_round(1, k)
            for i in range(8):
                key_out(1, i)

            def rows_round(b, i, turned, dst, ready):
                act.wait_ge(turned, b + 1)
                act.activation(dst, bank[i][:, :].rearrange("p (k t) -> p k t", k=KT), ACT.Copy).then_inc(ready, 1)

            def xn_round(b):
                rows_round(b, XN_BANK[b], xnT_turned, half_rows(xnT_h, b), xnT_h_ready)

            def x2_round(b):
                rows_round(b, X2_BANK[b], x2T_turned, x2T_h[:, :, bass.ts(b, P)], x2T_h_ready)

            def q_out(g, r, first, i=0):
                n, h, e = 8 * g + r, r // 4, r % 4
                act.wait_ge(q_ready, n + 1)
                if first:
                    act.wait_ge(scores_ready, A_UNITS)
                else:
                    act.wait_ge(scores_ready, A_UNITS + 8 * (g - 1) + 4 * h + 4)
                act.activation(qc[:, e, bass.ts(h, 512)], bank[i][:, :], ACT.Copy).then_inc(q_copied, 1)

            def x_round(b):
                act.wait_ge(x_in, 16 * (b + 1))
                if counted(b):
                    act.wait_ge(qkv_ready, b)
                act.activation(xT_h[:, :, :], xT_r[:, :, :], ACT.Copy).then_inc(x_h_ready, 1)

            def wo_round(c):
                act.wait_ge(wo_in[c % 2], 16 * (c // 2 + 1))
                if counted(c):
                    act.wait_ge(wo_t_ready, c)
                act.activation(wo_h[:, :], wo_r[:, c % 2, :], ACT.Copy).then_inc(wo_h_ready, 1)
                act.wait_ge(wo_h_ready, c + 1)
                if counted(c):
                    act.wait_ge(wo_ready, c)
                act.activation(wo_t[:, :], wo_h[:, :].bitcast(F32), ACT.Copy, scale=half[:, 1:2])\
                   .then_inc(wo_t_ready, 1)

            def block_out(b, j):
                act.wait_ge(blkT_ready, 4 * b + j + 1)
                if counted(8 * (b - 1) + 2 * j + 2):
                    act.wait_ge(scores_ready, 8 * (b - 1) + 2 * j + 2)
                act.activation(qT[:, j, :], bank[j % 2][:, 0:P], ACT.Copy).then_inc(qT_ready, 1)

            def exps(s, i, scale):
                act.wait_ge(nbias_ready, s + 1)
                for e in range(NE):
                    a = act.activation(prob[:, i, e, :], prob[:, i, e, :], ACT.Exp, bias=nbias[:, i, e:e + 1],
                                       scale=scale, accum_out=rsum[:, i, e:e + 1])
                a.then_inc(exp_done, 1)

            def self_turned(b, g):
                s = slot_of(b, g)
                act.wait_ge(pT_ready, s + 1)
                if counted(2 * b + g // 4):
                    act.wait_ge(pv_ready, 2 * b + g // 4)
                act.activation(pT[:, g % 4, :], bank[4 + g % 2][:, :], ACT.Copy).then_inc(pT_copied, 1)

            def heads_round(b, q):
                n = 2 * b + q
                act.wait_ge(pv_ready, n + 1)
                if counted(n):
                    act.wait_ge(oT_used, n)
                act.activation(oT_h[:, :, :].rearrange("p e t -> p (e t)"), bank[6][:, :], ACT.Copy)\
                   .then_inc(oT_h_ready, 1)

            def self_iteration(b, first, last):
                for g in range(8):
                    s = slot_of(b, g)
                    if not (last and g == 7):
                        exps(s + 1, (g + 1) % 4, SELF_SCALE)
                    if g == 0 and not first:
                        heads_round(b - 1, 1)
                    if g == 4:
                        heads_round(b, 0)
                    self_turned(b, g)
                    if g == 0 and not last:
                        x_round(b + 1)
                    if not last:
                        if g == 4:
                            block_out(b + 1, 0)
                        if g == 5:
                            block_out(b + 1, 1)
                        if g == 6:
                            block_out(b + 1, 2)
                    if g == 0 and not first:
                        block_out(b, 3)
                    if first:
                        wo_round(g)
                    if last and 2 <= g <= 5:
                        xn_round(g - 2)
                    if last and g == 7:
                        q_out(0, 0, True)

            x_round(0)
            for k in range(KT):
                act.wait_ge(wqkv_in[k % 2], 16 * (k // 2 + 1))
                act.activation(wqkv_h[:, k, :], wqkv_r[:, k % 2, :], ACT.Copy).then_inc(wqkv_h_ready, 1)
            block_out(0, 0)
            block_out(0, 1)
            exps(0, 0, SELF_SCALE)
            block_out(0, 2)
            block_out(0, 3)
            self_iteration(0, True, False)
            with act.Fori(1, NB - 1) as b:
                self_iteration(b, False, False)
            self_iteration(NB - 1, False, True)
            q_out(0, 1, True, 1)
            heads_round(NB - 1, 1)

            def wd_round(g, e, first):
                act.wait_ge(wd_in[e], 16 * (g + 1))
                if not first:
                    if e < NE - 1:
                        act.wait_ge(wd_used, 3 * (g - 1) + e + 1)
                    else:
                        act.wait_ge(cross_y, 8 * g)
                act.activation(wd_h[:, e, :], wd_r[:, e, :], ACT.Copy).then_inc(wd_h_ready, 1)

            def probs_round(s, b):
                act.wait_ge(pT_ready, A_UNITS + s + 1)
                if counted(s):
                    act.wait_ge(cross_pv, s)
                act.activation(pT_h[:, :], bank[3 + b % 2][:, :], ACT.Copy).then_inc(pT_h_ready, 1)

            def attended_round(s, b):
                act.wait_ge(cross_pv, s + 1)
                if counted(s - 1):
                    act.wait_ge(cross_y, s - 1)
                act.activation(aT_h[:, b % 2, :], bank[5][:, :], ACT.Copy).then_inc(aT_h_ready, 1)

            def cross_iteration(g, first, last):
                for b in range(NB):
                    s = 8 * g + b
                    probs_round(s, b)
                    if not (last and b == 7):
                        exps(A_UNITS + s + 1, (b + 1) % 4, CROSS_SCALE)
                    attended_round(s, b)
                    if b == 0 and not first:
                        for e in range(NE):
                            wd_round(g, e, False)
                    if b < 2:
                        q_out(g, 6 + b, first)
                    elif not last:
                        q_out(g + 1, b - 2, False)
                    if last and b >= 6:
                        w13_round(b - 6)
                    if last and b in (3, 4, 6):
                        sign(0, {3: 0, 4: 1, 6: 2}[b])
                    if last and b >= 6:
                        x2_round(2 * (b - 6))
                        x2_round(2 * (b - 6) + 1)

            def w13_round(c):
                act.wait_ge(wf_ready, 2)
                i = bass.ts(c, P)
                for m in range(2):
                    src = wf[:, m, :].rearrange("p (k i) -> p k i", k=KT)[:, :, i]
                    act.activation(w13_h[:, m, :, i], src, ACT.Copy).then_inc(w13_h_ready, 1)

            def sign(p, m):
                n = 3 * p + m
                act.wait_ge(fd_ready, n + 1)
                act.activation(fd[:, m % 2, :], fd[:, m % 2, :], ACT.Sign).then_inc(sign_ready, 1)

            q_out(0, 2, True)
            q_out(0, 3, True, 1)
            for b in range(4, NB):
                xn_round(b)
            exps(A_UNITS, 0, CROSS_SCALE)
            for e in range(NE):
                wd_round(0, e, True)
            q_out(0, 4, True)
            q_out(0, 5, True)
            cross_iteration(0, True, False)
            with act.Fori(1, NG - 1) as g:
                cross_iteration(g, False, False)
            cross_iteration(NG - 1, False, True)

            x2_round(4)
            x2_round(5)

            def gate(p, u):
                act.wait_ge(gu_ready, 4 * p + u + 1)
                if counted(4 * p + u - 1):
                    act.wait_ge(hf_done, 4 * p + u - 1)
                act.activation(silu[:, u % 2, :], bank[u % 2][:, :], ACT.Silu).then_inc(silu_done, 1)

            def hidden_round(p, u, first):
                act.wait_ge(hf_done, 4 * p + u + 1)
                if not first:
                    act.wait_ge(ffn_ready, 8 * (p - 1) + 4 * (u // 2) + 4)
                act.activation(hT_h[:, u // 2, u % 2, :], hf[:, u % 2, :], ACT.Copy).then_inc(hT_h_ready, 1)

            def ffn_piece(p, first, last):
                for u in range(4):
                    if first and u == 1:
                        x2_round(6)
                        x2_round(7)
                    gate(p, u)
                    hidden_round(p, u, first)
                    if u < 3 and not last:
                        sign(p + 1, u)

            ffn_piece(0, True, False)
            with act.Fori(1, NP - 1) as p:
                ffn_piece(p, False, False)
            ffn_piece(NP - 1, False, True)
            for b in range(NB):
                act.wait_ge(shift_ready, 2 if b < 4 else 2 * (b - 2))
                act.activation(xs[:, b, :], xs[:, b, :], ACT.Identity, bias=shift[:, b:b + 1],
                               scale=rstd[:, b:b + 1]).then_inc(ln_done, 1)


        @block.gpsimd
        def _(pool):
            def normalise(s, i):
                pool.wait_ge(rinv_ready, s + 1)
                pool.tensor_tensor(prob[:, i], prob[:, i], bcast(rinv[:, i, :], P, True), ALU.mult)\
                    .then_inc(norm_done, 1)

            def x_rest(b):
                pool.wait_ge(x_h_ready, b + 1)
                pool.tensor_tensor(xT_l[:, :, :], xT_r[:, :, :], xT_h[:, :, :].bitcast(F32), ALU.subtract)\
                    .then_inc(x_l_ready, 1)

            def wq_rest(g, e):
                pool.wait_ge(wq_h_ready, 4 * g + e + 1)
                pool.tensor_tensor(wq_l[:, e, :, :].rearrange("p k d -> p (k d)"), wq_r[:, e % 2, :],
                                   wq_h[:, e, :, :].rearrange("p k d -> p (k d)").bitcast(F32), ALU.subtract)\
                    .then_inc(wq_l_ready, 1)

            def rope_sums(b):
                pool.wait_ge(rope_ready, b + 1)
                if counted(4 * b):
                    pool.wait_ge(blkT_ready, 4 * b)
                pool.tensor_tensor(q_tok[:, :], rope1[:, 0:512], rope2[:, 0:512], ALU.add).then_inc(qk_ready, 1)

            def deviation(n, b, count=1):
                pool.wait_ge(varep_done, n + 1)
                pool.tensor_tensor(rstd[:, b:b + count], varep[:, b:b + count],
                                   cpow.to_broadcast([P, count]), ALU.pow).then_inc(rstd_ready, 1)

            def co_subtract(n):
                pool.wait_ge(co_in, 32 * (n + 1))
                pool.tensor_tensor(cw[:, :, :], cw[:, :, :], cm[:, :, :], ALU.subtract).then_inc(co_sub, 1)

            def self_iteration(b, first, last):
                for g in range(8):
                    if not (last and g == 7):
                        normalise(slot_of(b, g) + 1, (g + 1) % 4)
                    if g == 2 and not first:
                        deviation(b - 1, 0)
                    if last and 1 <= g <= 4:
                        wq_rest(0, g - 1)
                    if g == 0 and not last:
                        x_rest(b + 1)
                    if g == 2 and not last:
                        rope_sums(b + 1)

            pool.wait_ge(consts_in, 16)
            x_rest(0)
            rope_sums(0)
            normalise(0, 0)
            self_iteration(0, True, False)
            with pool.Fori(1, NB - 1) as b:
                self_iteration(b, False, False)
            self_iteration(NB - 1, False, True)

            def w13_rest(c):
                i = bass.ts(c, P)
                for m in range(2):
                    src = wf[:, m, :].rearrange("p (k i) -> p k i", k=KT)[:, :, i]
                    pool.wait_ge(w13_h_ready, 2 * c + m + 1)
                    w = pool.tensor_tensor(w13_l[:, m, :, i], src, w13_h[:, m, :, i].bitcast(F32), ALU.subtract)
                w.then_inc(w13_l_ready, 1)

            def difference(p, m):
                n = 3 * p + m
                pool.wait_ge(f_in[m], 32 * (p + 1))
                if counted(n - min(m, 1)):
                    pool.wait_ge(wf_ready, n - min(m, 1))
                pool.tensor_tensor(fd[:, m % 2, :], fw[:, m, :], fm[:, m, :], ALU.subtract).then_inc(fd_ready, 1)

            def cross_iteration(g, first, last):
                for b in range(NB):
                    s = 8 * g + b
                    if not last:
                        co_subtract(s)
                    if not (last and b == 7):
                        normalise(A_UNITS + s + 1, (b + 1) % 4)
                    if b < NE and not last:
                        wq_rest(g + 1, b)
                    if last and b >= 2:
                        deviation(NB + b - 2, b - 2)
                    if last and b >= 6:
                        w13_rest(b - 6)
                    if last and b in (2, 3, 5):
                        difference(0, {2: 0, 3: 1, 5: 2}[b])

            deviation(NB - 1, 0)
            normalise(A_UNITS, 0)
            cross_iteration(0, True, False)
            with pool.Fori(1, NG - 1) as g:
                cross_iteration(g, False, False)
            cross_iteration(NG - 1, False, True)
            deviation(2 * NB - 2, NB - 2)
            deviation(2 * NB - 1, NB - 1)

            with pool.Fori(1, NP) as p:
                for m in range(3):
                    difference(p, m)
            def last_shift(n, b, count):
                pool.wait_ge(rstd_ready, 2 * NB + n + 1)
                pool.tensor_tensor(shift[:, b:b + count], moments[:, b:b + count, 0], rstd[:, b:b + count],
                                   ALU.mult).then_inc(shift_ready, 1)
                pool.wait_ge(shift_ready, 2 * n + 1)
                pool.tensor_scalar(shift[:, b:b + count], shift[:, b:b + count], -1.0, None, ALU.mult)\
                    .then_inc(shift_ready, 1)

            deviation(2 * NB, 0, 4)
            last_shift(0, 0, 4)
            for t in range(4):
                deviation(2 * NB + 1 + t, 4 + t)
                last_shift(1 + t, 4 + t, 1)

        @block.vector
        def _(dve):
            dve.memset(csum3[:, 3:4], 0.0).then_inc(ln_done, LN0)

            def wkv_rest(c):
                dve.wait_ge(wkv_h_ready, c + 1)
                h, l = (wk_h, wk_l) if c < 4 else (wv_h, wv_l)
                dve.tensor_tensor(l[:, c % 4, :], wkv_r[:, c % 2, :], h[:, c % 4, :].bitcast(F32), ALU.subtract)\
                   .then_inc(wkv_l_ready, 1)

            def ctx_rest(h, k):
                dve.wait_ge(ctx_h_ready, 4 * h + k + 1)
                dve.tensor_tensor(cT_l[h][:, k, :], cT_r[:, k, :], cT_h[h][:, k, :].bitcast(F32), ALU.subtract)\
                   .then_inc(ctx_l_ready, 1)

            def value_out(h, i):
                dve.wait_ge(kv_ready, 16 * h + 8 + i + 1)
                dve.tensor_copy(vv[:, 4 * h + i // 2, bass.ts(i % 2, 512)], bank[i][:, :]).then_inc(v_copied, 1)

            for k in range(KT):
                wkv_rest(k)
                ctx_rest(0, k)
            for c in range(KT, 2 * KT):
                wkv_rest(c)
            for i in range(8):
                value_out(0, i)
                if i % 2 == 1:
                    ctx_rest(1, i // 2)

            def wo_rest(c):
                dve.wait_ge(wo_t_ready, c + 1)
                dve.scalar_tensor_tensor(out=wo_s[:, c, :], in0=wo_r[:, c % 2, :], scalar=half[:, 0:1],
                                         in1=wo_t[:, :], op0=ALU.mult, op1=ALU.add).then_inc(wo_ready, 1)

            def rope(b):
                dve.wait_ge(qkv_ready, b + 1)
                if counted(b):
                    dve.wait_ge(qk_ready, b)
                    dve.wait_ge(k_rep_ready, b)
                q, k = bank[0][:, 0:512], bank[1][:, 0:P]
                for src, at, n in ((q, 0, 32), (k, 512, 8)):
                    r1 = rope1[:, at:at + 16 * n].rearrange("p (h d) -> p h d", d=HD)
                    r2 = rope2[:, at:at + 16 * n].rearrange("p (h d) -> p h d", d=HD)
                    src = src.rearrange("p (h d) -> p h d", d=HD)
                    dve.tensor_tensor(r1, src, bcast(rcos, n, False), ALU.mult)
                    dve.tensor_tensor(r2[:, :, 0:8], src[:, :, 8:16], bcast(rsin[:, 0:8], n, False), ALU.mult)
                    dve.tensor_tensor(r2[:, :, 8:16], src[:, :, 0:8], bcast(rsin[:, 8:16], n, False), ALU.mult)
                dve.tensor_copy(v_tok[:, :], bank[1][:, P:2 * P]).then_inc(rope_ready, 1)

            def repeated_keys(b):
                dve.wait_ge(rope_ready, b + 1)
                if counted(4 * b):
                    dve.wait_ge(blkT_ready, 4 * b)
                k1, k2 = (r[:, 512:640].rearrange("p (g a d) -> p g a d", a=1, d=HD).to_broadcast([P, NG, NE, HD])
                          for r in (rope1, rope2))
                dve.tensor_tensor(k_rep[:, :].rearrange("p (g e d) -> p g e d", g=NG, e=NE), k1, k2, ALU.add)\
                   .then_inc(k_rep_ready, 1)

            def values_twice(b):
                dve.wait_ge(rope_ready, b + 1)
                if counted(2 * b):
                    dve.wait_ge(pv_ready, 2 * b)
                v = v_tok[:, :].rearrange("p (g a d) -> p g a d", a=1, d=HD).to_broadcast([P, NG, 2, HD])
                dve.tensor_copy(v_two[:, :, :, :], v).then_inc(v_two_ready, 1)

            def block_diagonal(b, j):
                dve.wait_ge(qT_ready, 4 * b + j + 1)
                if counted(8 * (b - 1) + 2 * j + 2):
                    dve.wait_ge(scores_ready, 8 * (b - 1) + 2 * j + 2)
                dve.tensor_tensor(bd[:, j, :, :], bcast(bank[j % 2][:, P:2 * P], 8, False),
                                  bcast(bmask, P, True), ALU.mult).then_inc(bd_ready, 1)

            def mask_and_max(s, i, score_bank, scale):
                dve.wait_ge(scores_ready, s + 1)
                if counted(s - 3):
                    dve.wait_ge(pT_ready, s - 3)
                dve.memset(gate_mark[:, :], 0.0)
                for e in range(NE):
                    m = dve.tensor_tensor_reduce(prob[:, i, e, :], score_bank[:, bass.ts(e, P)], cmask, 1.0,
                                                 -3.4e38, ALU.add, ALU.max, rmax[:, i, e:e + 1])
                m.then_inc(masked, 1)
                dve.wait_ge(masked, s + 1)
                dve.tensor_scalar(nbias[:, i, :], rmax[:, i, :], -scale, None, ALU.mult).then_inc(nbias_ready, 1)

            def inverse_sums(s, i):
                dve.wait_ge(exp_done, s + 1)
                if counted(s - 3):
                    dve.wait_ge(norm_done, s - 3)
                dve.reciprocal(rinv[:, i, :], rsum[:, i, :]).then_inc(rinv_ready, 1)

            def heads_rest(b, q):
                dve.wait_ge(oT_h_ready, 2 * b + q + 1)
                dve.tensor_tensor(oT_l[:, :, :].rearrange("p e t -> p (e t)"), bank[6][:, :],
                                  oT_h[:, :, :].rearrange("p e t -> p (e t)").bitcast(F32), ALU.subtract)\
                   .then_inc(oT_l_ready, 1)

            def rows_rest(b, i, h_ready, h, l, ready):
                dve.wait_ge(h_ready, b + 1)
                dve.tensor_tensor(l, bank[i][:, :].rearrange("p (k t) -> p k t", k=KT), h.bitcast(F32),
                                  ALU.subtract).then_inc(ready, 1)

            def xn_rest(b):
                rows_rest(b, XN_BANK[b], xnT_h_ready, half_rows(xnT_h, b), half_rows(xnT_l, b), xnT_l_ready)

            def x2_rest(b):
                tok = bass.ts(b, P)
                rows_rest(b, X2_BANK[b], x2T_h_ready, x2T_h[:, :, tok], x2T_l[:, :, tok], x2T_l_ready)

            def wq_round(g, e, first):
                dve.wait_ge(wq_in[e % 2], 16 * (2 * g + e // 2 + 1))
                if not first:
                    dve.wait_ge(q_ready, 8 * (g - 1) + 4 + e + 1)
                dve.tensor_copy(wq_h[:, e, :, :].rearrange("p k d -> p (k d)"), wq_r[:, e % 2, :])\
                   .then_inc(wq_h_ready, 1)

            def values_split(g, b, first):
                s = 8 * g + b
                if not first:
                    dve.wait_ge(cross_pv, s - 7)
                src = vv[:, b, bass.ts(g, P)]
                dve.tensor_copy(vg_h[:, b, :], src).then_inc(vg_h_ready, 1)
                dve.wait_ge(vg_h_ready, s + 1)
                dve.tensor_tensor(vg_l[:, b, :], src, vg_h[:, b, :].bitcast(F32), ALU.subtract)\
                   .then_inc(vg_ready, 1)

            def moments_of(n, b, i, rows_ready, count):
                dve.wait_ge(rows_ready, count)
                if i == 0:
                    dve.wait_ge(ln_done, LN0 + n)
                dve.memset(gate_mark[:, :], 0.0)
                dve.bn_stats(stats[:, i, :], xs[:, b, :]).then_inc(stats_done, 1)
                dve.wait_ge(stats_done, n + 1)
                dve.memset(gate_mark[:, :], 0.0)
                dve.bn_aggr(moments[:, i, :], stats[:, i, :]).then_inc(moments_done, 1)
                dve.wait_ge(moments_done, n + 1)
                dve.tensor_scalar(varep[:, i:i + 1], moments[:, i, 1:2], EPS, None, ALU.add).then_inc(varep_done, 1)

            def layer_norm(n, b, i):
                dve.wait_ge(rstd_ready, n + 1)
                dve.tensor_scalar(xs[:, b, :], xs[:, b, :], moments[:, i, 0:1], rstd[:, i:i + 1], ALU.subtract,
                                  ALU.mult).then_inc(ln_done, 1)

            def self_residual(b):
                dve.wait_ge(oT_used, 2 * b + 2)
                dve.wait_ge(res_in, 16 * (b + 1))
                dve.tensor_tensor(xs[:, b, :], bank[7][:, :], res[:, :], ALU.add).then_inc(y_done, 1)

            def self_iteration(b, first, last):
                for g in range(8):
                    s = slot_of(b, g)
                    if not (last and g >= 6):
                        mask_and_max(s + 2, (g + 2) % 4, bank[2 + g % 2], SELF_SCALE)
                    if not (last and g == 7):
                        inverse_sums(s + 1, (g + 1) % 4)
                    if g == 0 and not first:
                        heads_rest(b - 1, 1)
                    if g == 4:
                        heads_rest(b, 0)
                    if not first:
                        if g == 1:
                            values_twice(b)
                        if g == 2:
                            self_residual(b - 1)
                            moments_of(b - 1, b - 1, 0, y_done, b)
                        if g == 5:
                            layer_norm(b - 1, b - 1, 0)
                    if first:
                        wo_rest(g)
                    if not last:
                        if g == 2:
                            rope(b + 1)
                        if g == 3:
                            repeated_keys(b + 1)
                        if g == 4:
                            block_diagonal(b + 1, 0)
                        if g == 5:
                            block_diagonal(b + 1, 1)
                        if g == 6:
                            block_diagonal(b + 1, 2)
                    if g == 0 and not first:
                        block_diagonal(b, 3)
                    if last and 1 <= g <= 4:
                        if g == 1:
                            dve.wait_ge(qkv_ready, NB)
                        wq_round(0, g - 1, True)
                    if last and 2 <= g <= 5:
                        xn_rest(g - 2)
                    if last and g >= 4:
                        values_split(0, 2 * (g - 4), True)
                        values_split(0, 2 * (g - 4) + 1, True)

            for k in range(KT):
                value_out(1, k)
                dve.wait_ge(wqkv_h_ready, k + 1)
                dve.tensor_tensor(wqkv_l[:, k, :], wqkv_r[:, k % 2, :], wqkv_h[:, k, :].bitcast(F32), ALU.subtract)\
                   .then_inc(wqkv_l_ready, 1)
            value_out(1, 4)
            dve.wait_ge(consts_in, 16)
            rope(0)
            repeated_keys(0)
            value_out(1, 5)
            value_out(1, 6)
            block_diagonal(0, 0)
            block_diagonal(0, 1)
            value_out(1, 7)
            mask_and_max(0, 0, bank[2], SELF_SCALE)
            mask_and_max(1, 1, bank[3], SELF_SCALE)
            block_diagonal(0, 2)
            inverse_sums(0, 0)
            block_diagonal(0, 3)
            values_twice(0)
            self_iteration(0, True, False)
            with dve.Fori(1, NB - 1) as b:
                self_iteration(b, False, False)
            self_iteration(NB - 1, False, True)
            heads_rest(NB - 1, 1)
            self_residual(NB - 1)
            moments_of(NB - 1, NB - 1, 0, y_done, NB)

            def wd_rest(g, e):
                dve.wait_ge(wd_h_ready, 4 * g + e + 1)
                dve.tensor_tensor(wd_l[:, e, :], wd_r[:, e, :], wd_h[:, e, :].bitcast(F32), ALU.subtract)\
                   .then_inc(wd_l_ready, 1)

            def probs_rest(s, b):
                dve.wait_ge(pT_h_ready, s + 1)
                dve.tensor_tensor(pT_l[:, :], bank[3 + b % 2][:, :], pT_h[:, :].bitcast(F32), ALU.subtract)\
                   .then_inc(pT_l_ready, 1)

            def attended_rest(s, b):
                dve.wait_ge(aT_h_ready, s + 1)
                dve.tensor_tensor(aT_l[:, b % 2, :], bank[5][:, :], aT_h[:, b % 2, :].bitcast(F32),
                                  ALU.subtract).then_inc(aT_l_ready, 1)

            def cross_add(g, b):
                s = 8 * g + b
                dve.wait_ge(cross_y, s + 1)
                dve.wait_ge(ln_done, LN0 + b + 1)
                dve.tensor_tensor(xs[:, b, :], bank[6 + b % 2][:, :], xs[:, b, :], ALU.add)\
                   .then_inc(cross_added, 1)

            def rebuild(p, m):
                n = 3 * p + m
                dve.wait_ge(sign_ready, n + 1)
                if m < 2:
                    if counted(2 * p):
                        dve.wait_ge(w13_l_ready, 2 * p)
                else:
                    if counted(p):
                        dve.wait_ge(w2_l_ready, p)
                if isinstance(p, int) and p == 0:
                    dve.wait_ge(coeff_ready, 1)
                dve.scalar_tensor_tensor(out=wf[:, m, :], in0=fd[:, m % 2, :], scalar=coeff[:, m:m + 1],
                                         in1=fm[:, m, :], op0=ALU.mult, op1=ALU.add).then_inc(wf_ready, 1)

            def w13_split(p, c):
                dve.wait_ge(wf_ready, 3 * p + 2)
                dve.wait_ge(gu_ready, 4 * (p - 1) + 3 + c)
                i = bass.ts(c, P)
                for m in range(2):
                    src = wf[:, m, :].rearrange("p (k i) -> p k i", k=KT)[:, :, i]
                    dve.tensor_copy(w13_h[:, m, :, i], src).then_inc(w13_h_ready, 1)
                for m in range(2):
                    src = wf[:, m, :].rearrange("p (k i) -> p k i", k=KT)[:, :, i]
                    dve.wait_ge(w13_h_ready, 4 * p + 2 * c + m + 1)
                    w = dve.tensor_tensor(w13_l[:, m, :, i], src, w13_h[:, m, :, i].bitcast(F32), ALU.subtract)
                w.then_inc(w13_l_ready, 1)

            def w2_split(p, first):
                dve.wait_ge(wf_ready, 3 * p + 3)
                if not first:
                    dve.wait_ge(ffn_ready, 8 * p)
                h, l = (w[:, :, :].rearrange("p c n -> p (c n)") for w in (w2_h, w2_l))
                dve.tensor_copy(h, wf[:, 2, :]).then_inc(w2_h_ready, 1)
                dve.wait_ge(w2_h_ready, p + 1)
                dve.tensor_tensor(l, wf[:, 2, :], h.bitcast(F32), ALU.subtract).then_inc(w2_l_ready, 1)

            def co_reduce(n):
                dve.wait_ge(co_sub, n + 1)
                dve.memset(co_mark[:, :], 0.0)
                dve.tensor_reduce(csum[:, n, :], cw[:, :, :], AXX, ALU.add, apply_absolute_value=True)\
                   .then_inc(co_sum, 1)

            def cross_iteration(g, first, last):
                for b in range(NB):
                    s = 8 * g + b
                    probs_rest(s, b)
                    if not (last and b == 7):
                        inverse_sums(A_UNITS + s + 1, (b + 1) % 4)
                    if not last:
                        co_reduce(s)
                    if b > 0:
                        cross_add(g, b - 1)
                    elif not first:
                        cross_add(g - 1, 7)
                    attended_rest(s, b)
                    if not (last and b >= 6):
                        mask_and_max(A_UNITS + s + 2, (b + 2) % 4, bank[1 + b % 2], CROSS_SCALE)
                    if b == 0 and not first:
                        for e in range(NE):
                            wd_rest(g, e)
                    if not last:
                        if b < NE:
                            wq_round(g + 1, b, False)
                        values_split(g + 1, b, False)
                    else:
                        if b == 0:
                            dve.wait_ge(co_sum, NCO)
                            dve.tensor_reduce(csum3[:, 0:3], csum[:, :, :].rearrange("p n m -> p m n"), AXX,
                                              ALU.add).then_inc(cototal_ready, 1)
                        if b == 3:
                            dve.wait_ge(cototal_ready, 2)
                            dve.tensor_scalar(coeff[:, :], bank[0][:, 0:3], 1.0 / (INTER * DM), None, ALU.mult)\
                               .then_inc(coeff_ready, 1)
                        if b >= 1:
                            moments_of(NB + b - 1, b - 1, b - 1, cross_added, s)
                        if b >= 2:
                            layer_norm(NB + b - 2, b - 2, b - 2)
                        if b in (4, 5, 7):
                            rebuild(0, {4: 0, 5: 1, 7: 2}[b])
                        if b >= 6:
                            x2_rest(2 * (b - 6))
                            x2_rest(2 * (b - 6) + 1)

            layer_norm(NB - 1, NB - 1, 0)
            for b in range(4, 7):
                xn_rest(b)
            mask_and_max(A_UNITS, 0, bank[1], CROSS_SCALE)
            xn_rest(7)
            mask_and_max(A_UNITS + 1, 1, bank[2], CROSS_SCALE)
            for e in range(NE):
                wd_rest(0, e)
            inverse_sums(A_UNITS, 0)
            cross_iteration(0, True, False)
            with dve.Fori(1, NG - 1) as g:
                cross_iteration(g, False, False)
            cross_iteration(NG - 1, False, True)
            x2_rest(4)
            layer_norm(2 * NB - 2, NB - 2, NB - 2)
            cross_add(NG - 1, 7)
            moments_of(2 * NB - 1, NB - 1, NB - 1, cross_added, 64)
            x2_rest(5)
            layer_norm(2 * NB - 1, NB - 1, NB - 1)

            w2_split(0, True)

            def hidden(p, u):
                dve.wait_ge(silu_done, 4 * p + u + 1)
                if counted(4 * p + u - 1):
                    dve.wait_ge(hT_l_ready, 4 * p + u - 1)
                dve.tensor_tensor(hf[:, u % 2, :], bank[2 + u % 2][:, :], silu[:, u % 2, :], ALU.mult)\
                   .then_inc(hf_done, 1)

            def hidden_rest(p, u):
                dve.wait_ge(hT_h_ready, 4 * p + u + 1)
                dve.tensor_tensor(hT_l[:, u // 2, u % 2, :], hf[:, u % 2, :],
                                  hT_h[:, u // 2, u % 2, :].bitcast(F32), ALU.subtract).then_inc(hT_l_ready, 1)

            def ffn_add(p, h, t):
                n, b = 8 * p + 4 * h + t, 4 * h + t
                dve.wait_ge(ffn_ready, n + 1)
                dve.wait_ge(ln_done, LN0 + 2 * NB)
                dve.tensor_tensor(xs[:, b, :], bank[4 + t][:, :], xs[:, b, :], ALU.add).then_inc(ffn_added, 1)

            def ffn_piece(p, first, last):
                for u in range(4):
                    if first and u == 1:
                        x2_rest(6)
                        x2_rest(7)
                    hidden(p, u)
                    hidden_rest(p, u)
                    if u == 1 and not first:
                        for t in range(4):
                            ffn_add(p - 1, 1, t)
                        w2_split(p, False)
                    if not last:
                        if u < 3:
                            rebuild(p + 1, u)
                        if u >= 2:
                            w13_split(p + 1, u - 2)
                for t in range(4):
                    ffn_add(p, 0, t)

            ffn_piece(0, True, False)
            with dve.Fori(1, NP - 1) as p:
                ffn_piece(p, False, False)
            ffn_piece(NP - 1, False, True)
            def last_stats(b, n):
                dve.wait_ge(ffn_added, 8 * NP - 8 + b + 1)
                dve.bn_stats(stats[:, b, :], xs[:, b, :]).then_inc(stats_done, 1)
                dve.wait_ge(stats_done, n + 1)
                dve.bn_aggr(moments[:, b, :], stats[:, b, :]).then_inc(moments_done, 1)

            for b in range(4):
                last_stats(b, 2 * NB + b)
            dve.wait_ge(moments_done, 2 * NB + 4)
            dve.tensor_scalar(varep[:, 0:4], moments[:, 0:4, 1], EPS, None, ALU.add).then_inc(varep_done, 1)
            for t in range(4):
                b = 4 + t
                ffn_add(NP - 1, 1, t)
                last_stats(b, 2 * NB + b)
                dve.wait_ge(moments_done, 2 * NB + b + 1)
                dve.tensor_scalar(varep[:, b:b + 1], moments[:, b, 1:2], EPS, None, ALU.add).then_inc(varep_done, 1)


def constants():
    c = np.zeros((P, C_ALL), np.float32)
    r = np.arange(P)
    c[:, C_ID:C_ID + P] = np.eye(P)
    c[:, C_MASK:C_MASK + P] = np.where(r[None, :] <= r[:, None], 0.0, NEG)
    c[:, C_BM:C_BM + 8] = (r[:, None] // HD) == np.arange(8)[None, :]
    freq = (1.0 / np.float32(10000.0) ** (np.arange(0, HD, 2, dtype=np.float32) / np.float32(HD))).astype(np.float32)
    angle = r.astype(np.float32)[:, None] * freq[None, :]
    cos, sin = np.cos(angle), np.sin(angle)
    c[:, C_COS:C_COS + HD] = np.concatenate([cos, cos], 1)
    c[:, C_SIN:C_SIN + HD] = np.concatenate([-sin, sin], 1)
    second = (r // HD) % 2
    c[:, C_HALF] = second
    c[:, C_HALF + 1] = 1 - 2 * second
    c[:, C_EPS] = EPS
    c[:, C_POW] = -0.5
    c[:, C_ONE:C_ONE + P] = 1.0
    return c


def kernel(x, ctx_4096, L0_attn_w_qkv, L0_attn_w_o, L0_xattn_Wq, L0_xattn_Wk, L0_xattn_Wv, L0_xattn_Wd,
           L0_ffn_w1, L0_ffn_mean_w1, L0_ffn_w2, L0_ffn_mean_w2, L0_ffn_w3, L0_ffn_mean_w3):
    import concourse.bacc as bacc
    from concourse.bass_utils import run_bass_kernel_spmd

    def arr(a):
        return np.asarray(a)

    x, c4 = arr(x), arr(ctx_4096)
    turn = np.concatenate([np.arange(0, HD, 2), np.arange(1, HD, 2)])
    cols = np.concatenate([(np.arange(40)[:, None] * HD + turn[None, :]).ravel(), np.arange(640, QKV)])
    wqkv = arr(L0_attn_w_qkv)[:, cols]

    def w13(w):
        return arr(w).reshape(NP, PIECE, KT, P).transpose(0, 3, 2, 1).reshape(NP, P, 1024)

    def w2(w):
        return arr(w).T.reshape(NP, 2, P, DM).transpose(0, 2, 1, 3).reshape(NP, P, 1024)

    wo = arr(L0_attn_w_o).reshape(2, 4, NE, 1, HD, DM)
    wo = np.concatenate([wo, wo], 3).transpose(1, 3, 4, 0, 2, 5)
    arrays = {
        "consts": constants(),
        "x": x,
        "xT": x.reshape(NB, P, KT, P).transpose(0, 3, 2, 1),
        "ctxT": c4.reshape(2, 512, KT, P).transpose(0, 3, 2, 1),
        "wkv": np.concatenate([arr(L0_xattn_Wk).T.reshape(KT, P, 1024), arr(L0_xattn_Wv).T.reshape(KT, P, 1024)]),
        "wqkv": wqkv.reshape(KT, P, QKV).transpose(1, 0, 2),
        "wo": wo.reshape(P, 2 * NE, DM),
        "wq": arr(L0_xattn_Wq).reshape(NG * NE, P, KT, P).transpose(0, 3, 2, 1).reshape(NG * NE, P, 512),
        "wd": arr(L0_xattn_Wd).T.reshape(NG * NE, P, DM),
        "fw": np.stack([w13(L0_ffn_w1), w13(L0_ffn_w3), w2(L0_ffn_w2)], 2),
        "fm": np.stack([w13(L0_ffn_mean_w1), w13(L0_ffn_mean_w3), w2(L0_ffn_mean_w2)], 2),
    }
    arrays = {n + "_dram": np.ascontiguousarray(a) for n, a in arrays.items()}
    nc = bacc.Bacc("TRN2", target_bir_lowering=False, num_devices=1)
    args = [nc.dram_tensor(n, a.shape, mybir.dt.from_np(a.dtype), kind="ExternalInput").ap()
            for n, a in arrays.items()]
    out = nc.dram_tensor("out", (NB, P, DM), F32, kind="ExternalOutput").ap()
    decoder_layer(nc, *args, out)
    r = run_bass_kernel_spmd(nc, [arrays], core_ids=[0])
    return r.results[0]["out"]
```
